# Optimizing a Trainium2 kernel written in Bass

```python
import numpy as np
import jax
import jax.numpy as jnp

def _softmax(x, axis=-1):
    return jax.nn.softmax(x, axis=axis)

def _gelu(x):
    return jax.nn.gelu(x, approximate=True)

def _silu(x):
    return jax.nn.silu(x)

def _sigmoid(x):
    return jax.nn.sigmoid(x)

def _layernorm(x, axis=-1, eps=1e-05):
    m = jnp.mean(x, axis=axis, keepdims=True)
    v = jnp.var(x, axis=axis, keepdims=True)
    return (x - m) / jnp.sqrt(v + eps)

def _scatter_add(tgt, idx, src, axis=0):
    return tgt.at[idx].add(src)

def _segment_sum(src, seg, n):
    return jax.ops.segment_sum(src, seg, n)
kernel_name = 'mk_gnn_ffn_d2_gnn_r16_f87fe8'

def setup_inputs(seed: int=0):
    np.random.seed(seed)
    _w = jnp.asarray

    def _rec_inputs():
        import jax
        import jax.numpy as jnp
        _gk = jax.random.key(seed)
        x = -0.0003713 + 1 * jax.random.normal(jax.random.fold_in(_gk, 1), (3125, 256), jnp.float32)
        src = jax.random.randint(jax.random.fold_in(_gk, 2), (50000,), 0, 3125, jnp.int32)
        dst = jnp.minimum((3125 * jax.random.uniform(jax.random.fold_in(_gk, 3), (50000,)) ** 2.0).astype(jnp.int32), 49999)
        _o = jnp.argsort(dst, stable=True)
        src = src[_o]
        dst = dst[_o]
        edge_attr_64 = -5.3897e-05 + 0.999841 * jax.random.normal(jax.random.fold_in(_gk, 12), (50000, 64), jnp.float32)
        return (x, src, dst, edge_attr_64)
    x, src, dst, edge_attr_64 = _rec_inputs()

    def _L0_gnn_setup():
        import jax, jax.numpy as jnp
        import numpy as np
        N_NODES = 3125
        N_EDGES = 25000
        D_NODE = 256
        D_EDGE = 64
        LN_EPS = 1e-06

        def _layer_norm(x, scale, bias):
            mu = jnp.mean(x, axis=-1, keepdims=True)
            var = jnp.mean(jnp.square(x - mu), axis=-1, keepdims=True)
            return (x - mu) * jax.lax.rsqrt(var + LN_EPS) * scale + bias

        def _glorot(key, shape):
            fan_in, fan_out = shape
            std = jnp.sqrt(2.0 / (fan_in + fan_out))
            return std * jax.random.normal(key, shape, dtype=jnp.float32)

        def _relu_mlp_skip(x, Ws, bs):
            n = len(Ws)
            for i, (W, b) in enumerate(zip(Ws, bs)):
                y = x @ W + b
                if i < n - 1:
                    y = jax.nn.relu(y)
                x = x + y if y.shape[-1] == x.shape[-1] else y
            return x
        key = jax.random.key(seed)
        ks = jax.random.split(key, 10)
        inp = {'nodes': jax.random.normal(ks[0], (N_NODES, D_NODE), dtype=jnp.float32), 'edges': jax.random.normal(ks[1], (N_EDGES, D_EDGE), dtype=jnp.float32), 'senders': jax.random.randint(ks[2], (N_EDGES,), 0, N_NODES, dtype=jnp.int32), 'receivers': jax.random.randint(ks[3], (N_EDGES,), 0, N_NODES, dtype=jnp.int32), 'W_message': _glorot(ks[4], (D_NODE + D_EDGE, D_NODE)), 'mlp_W0': _glorot(ks[5], (D_NODE, D_NODE)), 'mlp_b0': jnp.zeros((D_NODE,), jnp.float32), 'mlp_W1': _glorot(ks[6], (D_NODE, D_NODE)), 'mlp_b1': jnp.zeros((D_NODE,), jnp.float32), 'mlp_W2': _glorot(ks[7], (D_NODE, D_NODE)), 'mlp_b2': jnp.zeros((D_NODE,), jnp.float32), 'ln_aggr_scale': jnp.ones((D_NODE,), jnp.float32), 'ln_aggr_bias': jnp.zeros((D_NODE,), jnp.float32), 'ln_out_scale': jnp.ones((D_NODE,), jnp.float32), 'ln_out_bias': jnp.zeros((D_NODE,), jnp.float32)}
        return inp
    _L0_gnn_all = _L0_gnn_setup()
    _L0_gnn_in = {k: v for k, v in _L0_gnn_all.items() if k in ('W_message', 'mlp_W0', 'mlp_b0', 'mlp_W1', 'mlp_b1', 'mlp_W2', 'mlp_b2', 'ln_aggr_scale', 'ln_aggr_bias', 'ln_out_scale', 'ln_out_bias')}
    del _L0_gnn_all

    def _L0_ffn_setup():
        import jax, jax.numpy as jnp
        import numpy as np
        B, S, H, F, E, K = (8, 256, 256, 512, 16, 2)
        EPS = 1e-05
        key = jax.random.key(seed)
        ks = jax.random.split(key, 9)
        sc = 0.02
        return {'x': jax.random.normal(ks[0], (B, S, H), dtype=jnp.float32), 'gate_w': jax.random.normal(ks[1], (H, E), dtype=jnp.float32) * sc, 'gate_b': jnp.zeros((E,), dtype=jnp.float32), 'w1': jax.random.normal(ks[2], (E, H, F), dtype=jnp.float32) * sc, 'b1': jnp.zeros((E, F), dtype=jnp.float32), 'w2': jax.random.normal(ks[3], (E, F, H), dtype=jnp.float32) * sc, 'b2': jnp.zeros((E, H), dtype=jnp.float32), 'gamma': jnp.ones((H,), dtype=jnp.float32), 'beta': jnp.zeros((H,), dtype=jnp.float32)}
    _L0_ffn_all = _L0_ffn_setup()
    _L0_ffn_in = {k: v for k, v in _L0_ffn_all.items() if k in ('gate_w', 'gate_b', 'w1', 'b1', 'w2', 'b2', 'gamma', 'beta')}
    del _L0_ffn_all

    def _L1_gnn_setup():
        import jax, jax.numpy as jnp
        import numpy as np
        N = 6250
        E = 100000
        IN_FEATS = 256
        OUT_FEATS = 256
        MAXK = 32

        def _maxk(x, k):
            _, idx = jax.lax.top_k(x, k)
            rows = jnp.arange(x.shape[0])[:, None]
            mask = jnp.zeros_like(x).at[rows, idx].set(1.0)
            return x * mask
        key = jax.random.key(seed)
        k1, k2, k3, k4, k5 = jax.random.split(key, 5)
        feat = jax.random.normal(k1, (N, IN_FEATS), dtype=jnp.float32)
        W_self = jax.random.normal(k2, (IN_FEATS, OUT_FEATS), dtype=jnp.float32) * (1.0 / np.sqrt(IN_FEATS))
        W_neigh = jax.random.normal(k3, (IN_FEATS, OUT_FEATS), dtype=jnp.float32) * (1.0 / np.sqrt(IN_FEATS))
        src = jax.random.randint(k4, (E,), 0, N, dtype=jnp.int64)
        dst = jax.random.randint(k5, (E,), 0, N, dtype=jnp.int64)
        return {'feat': feat, 'W_self': W_self, 'W_neigh': W_neigh, 'src': src, 'dst': dst}
    _L1_gnn_all = _L1_gnn_setup()
    _L1_gnn_in = {k: v for k, v in _L1_gnn_all.items() if k in ('W_self', 'W_neigh')}
    del _L1_gnn_all

    def _L1_ffn_setup():
        import jax, jax.numpy as jnp
        import numpy as np
        NUM_EXPERTS = 8
        TOP_K = 2
        B, S, D = (8, 512, 256)

        def _moe(tokens, router_w, w1, b1, w2, b2):
            N = tokens.shape[0]
            E = router_w.shape[0]
            logits = tokens.astype(jnp.float32) @ router_w.astype(jnp.float32).T
            probs = jax.nn.softmax(logits, axis=-1)
            rw, re = jax.lax.top_k(probs, TOP_K)
            if TOP_K > 1:
                rw = rw / jnp.maximum(rw.sum(-1, keepdims=True), 1e-12)
            rw = rw.astype(tokens.dtype)
            combine = jnp.zeros((N, E), tokens.dtype).at[jnp.arange(N)[:, None], re].set(rw)
            out = tokens
            for e in range(E):
                h = jax.nn.gelu(tokens @ w1[e] + b1[e], approximate=False)
                y = h @ w2[e] + b2[e]
                out = out + combine[:, e:e + 1] * y
            return out
        key = jax.random.key(seed)
        ks = jax.random.split(key, 4)
        scale = 1.0 / np.sqrt(D).astype(np.float32)
        return {'input_embeddings': jax.random.normal(ks[0], (B, S, D), jnp.float32), 'router_w': jax.random.normal(ks[1], (NUM_EXPERTS, D), jnp.float32) * scale, 'w1': jax.random.normal(ks[2], (NUM_EXPERTS, D, D), jnp.float32) * scale, 'b1': jnp.zeros((NUM_EXPERTS, D), jnp.float32), 'w2': jax.random.normal(ks[3], (NUM_EXPERTS, D, D), jnp.float32) * scale, 'b2': jnp.zeros((NUM_EXPERTS, D), jnp.float32)}
    _L1_ffn_all = _L1_ffn_setup()
    _L1_ffn_in = {k: v for k, v in _L1_ffn_all.items() if k in ('router_w', 'w1', 'b1', 'w2', 'b2')}
    del _L1_ffn_all
    return {'x': x, 'src': src, 'dst': dst, 'edge_attr_64': edge_attr_64, 'L0_gnn_W_message': _L0_gnn_in['W_message'], 'L0_gnn_mlp_W0': _L0_gnn_in['mlp_W0'], 'L0_gnn_mlp_b0': _L0_gnn_in['mlp_b0'], 'L0_gnn_mlp_W1': _L0_gnn_in['mlp_W1'], 'L0_gnn_mlp_b1': _L0_gnn_in['mlp_b1'], 'L0_gnn_mlp_W2': _L0_gnn_in['mlp_W2'], 'L0_gnn_mlp_b2': _L0_gnn_in['mlp_b2'], 'L0_gnn_ln_aggr_scale': _L0_gnn_in['ln_aggr_scale'], 'L0_gnn_ln_aggr_bias': _L0_gnn_in['ln_aggr_bias'], 'L0_gnn_ln_out_scale': _L0_gnn_in['ln_out_scale'], 'L0_gnn_ln_out_bias': _L0_gnn_in['ln_out_bias'], 'L0_ffn_gate_w': _L0_ffn_in['gate_w'], 'L0_ffn_gate_b': _L0_ffn_in['gate_b'], 'L0_ffn_w1': _L0_ffn_in['w1'], 'L0_ffn_b1': _L0_ffn_in['b1'], 'L0_ffn_w2': _L0_ffn_in['w2'], 'L0_ffn_b2': _L0_ffn_in['b2'], 'L0_ffn_gamma': _L0_ffn_in['gamma'], 'L0_ffn_beta': _L0_ffn_in['beta'], 'L1_gnn_W_self': _L1_gnn_in['W_self'], 'L1_gnn_W_neigh': _L1_gnn_in['W_neigh'], 'L1_ffn_router_w': _L1_ffn_in['router_w'], 'L1_ffn_w1': _L1_ffn_in['w1'], 'L1_ffn_b1': _L1_ffn_in['b1'], 'L1_ffn_w2': _L1_ffn_in['w2'], 'L1_ffn_b2': _L1_ffn_in['b2']}

def reference(x, src, dst, edge_attr_64, L0_gnn_W_message, L0_gnn_mlp_W0, L0_gnn_mlp_b0, L0_gnn_mlp_W1, L0_gnn_mlp_b1, L0_gnn_mlp_W2, L0_gnn_mlp_b2, L0_gnn_ln_aggr_scale, L0_gnn_ln_aggr_bias, L0_gnn_ln_out_scale, L0_gnn_ln_out_bias, L0_ffn_gate_w, L0_ffn_gate_b, L0_ffn_w1, L0_ffn_b1, L0_ffn_w2, L0_ffn_b2, L0_ffn_gamma, L0_ffn_beta, L1_gnn_W_self, L1_gnn_W_neigh, L1_ffn_router_w, L1_ffn_w1, L1_ffn_b1, L1_ffn_w2, L1_ffn_b2):
    import jax
    import jax.numpy as jnp

    def _L0_gnn_ref(nodes, edges, senders, receivers, W_message, mlp_W0, mlp_b0, mlp_W1, mlp_b1, mlp_W2, mlp_b2, ln_aggr_scale, ln_aggr_bias, ln_out_scale, ln_out_bias):
        import jax, jax.numpy as jnp
        import numpy as np
        N_NODES = 3125
        N_EDGES = 25000
        D_NODE = 256
        D_EDGE = 64
        LN_EPS = 1e-06

        def _layer_norm(x, scale, bias):
            mu = jnp.mean(x, axis=-1, keepdims=True)
            var = jnp.mean(jnp.square(x - mu), axis=-1, keepdims=True)
            return (x - mu) * jax.lax.rsqrt(var + LN_EPS) * scale + bias

        def _glorot(key, shape):
            fan_in, fan_out = shape
            std = jnp.sqrt(2.0 / (fan_in + fan_out))
            return std * jax.random.normal(key, shape, dtype=jnp.float32)

        def _relu_mlp_skip(x, Ws, bs):
            n = len(Ws)
            for i, (W, b) in enumerate(zip(Ws, bs)):
                y = x @ W + b
                if i < n - 1:
                    y = jax.nn.relu(y)
                x = x + y if y.shape[-1] == x.shape[-1] else y
            return x
        total_nodes = nodes.shape[0]
        sender_features = nodes[senders]
        msg_in = jnp.concatenate([sender_features, edges], axis=-1)
        messages = msg_in @ W_message
        agg = jax.ops.segment_sum(messages, receivers, num_segments=total_nodes)
        h = _layer_norm(jax.nn.relu(agg) + nodes, ln_aggr_scale, ln_aggr_bias)
        nodes_out = _relu_mlp_skip(h, [mlp_W0, mlp_W1, mlp_W2], [mlp_b0, mlp_b1, mlp_b2])
        nodes_new = _layer_norm(nodes + nodes_out, ln_out_scale, ln_out_bias)
        return nodes_new

    def _L0_ffn_ref(x, gate_w, gate_b, w1, b1, w2, b2, gamma, beta):
        import jax, jax.numpy as jnp
        import numpy as np
        B, S, H, F, E, K = (8, 256, 256, 512, 16, 2)
        EPS = 1e-05
        gate_logits = x @ gate_w + gate_b
        topk_vals, topk_idx = jax.lax.top_k(gate_logits, K)
        topk_w = jax.nn.softmax(topk_vals, axis=-1)
        h = jax.nn.relu(jnp.einsum('bsh,ehf->bsef', x, w1) + b1)
        expert_out = jnp.einsum('bsef,efh->bseh', h, w2) + b2
        sel = jnp.take_along_axis(expert_out, topk_idx[:, :, :, None], axis=2)
        moe = jnp.sum(topk_w[..., None] * sel, axis=2)
        y = x + moe
        mu = jnp.mean(y, axis=-1, keepdims=True)
        var = jnp.var(y, axis=-1, keepdims=True)
        return (y - mu) / jnp.sqrt(var + EPS) * gamma + beta

    def _L1_gnn_ref(feat, W_self, W_neigh, src, dst):
        import jax, jax.numpy as jnp
        import numpy as np
        N = 6250
        E = 100000
        IN_FEATS = 256
        OUT_FEATS = 256
        MAXK = 32

        def _maxk(x, k):
            _, idx = jax.lax.top_k(x, k)
            rows = jnp.arange(x.shape[0])[:, None]
            mask = jnp.zeros_like(x).at[rows, idx].set(1.0)
            return x * mask
        n = feat.shape[0]
        h_self = feat @ W_self
        h_neigh = feat @ W_neigh
        h_sparse = _maxk(h_neigh, MAXK)
        msg = h_sparse[src]
        summed = jax.ops.segment_sum(msg, dst, num_segments=n)
        deg = jax.ops.segment_sum(jnp.ones((src.shape[0],), dtype=feat.dtype), dst, num_segments=n)
        neigh = summed / jnp.maximum(deg, 1.0)[:, None]
        return h_self + neigh

    def _L1_ffn_ref(input_embeddings, router_w, w1, b1, w2, b2):
        import jax, jax.numpy as jnp
        import numpy as np
        NUM_EXPERTS = 8
        TOP_K = 2
        B, S, D = (8, 512, 256)

        def _moe(tokens, router_w, w1, b1, w2, b2):
            N = tokens.shape[0]
            E = router_w.shape[0]
            logits = tokens.astype(jnp.float32) @ router_w.astype(jnp.float32).T
            probs = jax.nn.softmax(logits, axis=-1)
            rw, re = jax.lax.top_k(probs, TOP_K)
            if TOP_K > 1:
                rw = rw / jnp.maximum(rw.sum(-1, keepdims=True), 1e-12)
            rw = rw.astype(tokens.dtype)
            combine = jnp.zeros((N, E), tokens.dtype).at[jnp.arange(N)[:, None], re].set(rw)
            out = tokens
            for e in range(E):
                h = jax.nn.gelu(tokens @ w1[e] + b1[e], approximate=False)
                y = h @ w2[e] + b2[e]
                out = out + combine[:, e:e + 1] * y
            return out
        b, s, d = input_embeddings.shape
        tokens = input_embeddings.reshape(b * s, d)
        return _moe(tokens, router_w, w1, b1, w2, b2).reshape(b, s, d)
    x = x + _L0_gnn_ref(_layernorm(x, axis=-1), edge_attr_64, src, dst, L0_gnn_W_message, L0_gnn_mlp_W0, L0_gnn_mlp_b0, L0_gnn_mlp_W1, L0_gnn_mlp_b1, L0_gnn_mlp_W2, L0_gnn_mlp_b2, L0_gnn_ln_aggr_scale, L0_gnn_ln_aggr_bias, L0_gnn_ln_out_scale, L0_gnn_ln_out_bias)
    x = x + _L0_ffn_ref(_layernorm(x, axis=-1)[None], L0_ffn_gate_w, L0_ffn_gate_b, L0_ffn_w1, L0_ffn_b1, L0_ffn_w2, L0_ffn_b2, L0_ffn_gamma, L0_ffn_beta)[0]
    x = x + _L1_gnn_ref(_layernorm(x, axis=-1), L1_gnn_W_self, L1_gnn_W_neigh, src, dst)
    x = x + _L1_ffn_ref(_layernorm(x, axis=-1)[None], L1_ffn_router_w, L1_ffn_w1, L1_ffn_b1, L1_ffn_w2, L1_ffn_b2)[0]
    return x

_drawn_inputs = setup_inputs


def setup_inputs(seed=0):
    import zlib

    import numpy as np

    out = dict(_drawn_inputs(seed))
    spreads = {'L0_gnn_mlp_b0': (0.0, 0.1),
     'L0_gnn_mlp_b1': (0.0, 0.275),
     'L0_gnn_mlp_b2': (0.0, 0.295),
     'L0_gnn_ln_aggr_scale': (1.0, 0.2),
     'L0_gnn_ln_aggr_bias': (0.0, 0.1),
     'L0_gnn_ln_out_scale': (1.0, 0.2),
     'L0_gnn_ln_out_bias': (0.0, 0.1),
     'L0_ffn_gate_b': (0.0, 0.1),
     'L0_ffn_b1': (0.0, 0.632),
     'L0_ffn_b2': (0.0, 0.1),
     'L0_ffn_gamma': (1.0, 0.2),
     'L0_ffn_beta': (0.0, 0.1),
     'L1_ffn_b1': (0.0, 0.6),
     'L1_ffn_b2': (0.0, 0.426)}
    factors = {}
    for name, (base, spread) in spreads.items():
        noise = np.random.default_rng([zlib.crc32(name.encode()), seed]).standard_normal(out[name].shape)
        drawn = base * np.exp(spread * noise) if base else spread * noise
        out[name] = jnp.asarray(drawn.astype(out[name].dtype))
    for name, factor in factors.items():
        out[name] = (out[name] * factor).astype(out[name].dtype)
    return out
```

```python
from contextlib import ExitStack

import numpy as np
import concourse.bass as bass
from concourse import mybir

P = 128
F32 = mybir.dt.float32
I32 = mybir.dt.int32
U32 = mybir.dt.uint32
ALU = mybir.AluOpType
ACT = mybir.ActivationFunctionType
AX_X = mybir.AxisListType.X
ds = bass.ds

TU = 5
GC = 4
GU = 7
BU = 4
FAR = 1.0e6


def build(nc, a, out, debug=None):
    N, D = a["x"].shape
    E_N, DE = a["edge_attr_64"].shape
    T = -(-N // P)
    NPAD = T * P
    LAST = N - (T - 1) * P
    IT = T // TU
    assert IT * TU == T and D == 256
    GE = GC * P
    NG = -(-E_N // GE)
    GI = NG // GU
    assert GI * GU == NG and NG <= P
    E_LAST = E_N - (NG - 1) * GE
    P_LAST = E_LAST // GC
    assert P_LAST * GC == E_LAST
    WIN = NPAD + P
    K2 = D // P

    E0, _, F0 = a["L0_ffn_w1"].shape
    E1, _, F1 = a["L1_ffn_w1"].shape

    def n_blocks(experts):
        most = 2 * N // P + experts
        return -(-most // BU) * BU

    NB0, NB1 = n_blocks(E0), n_blocks(E1)
    XS_ROWS = max(NB0, NB1) * P

    n_dram = nc.dram_tensor("n_rows", [NPAD, D], F32, kind="Internal").ap()
    xs_dram = nc.dram_tensor("expert_in", [XS_ROWS, D], F32, kind="Internal").ap()
    ys_dram = nc.dram_tensor("expert_out", [XS_ROWS, D], F32, kind="Internal").ap()

    with ExitStack() as ctx:
        def sb(name, shape, dt=F32, c=ctx):
            return c.enter_context(nc.sbuf_tensor(name, shape, dt))

        def pb(name, shape, c=ctx):
            return c.enter_context(nc.psum_tensor(name, shape, F32))

        step_sems = []

        def sem(name):
            step_sems.append(nc.alloc_semaphore(name=name))
            return step_sems[-1]

        def held_sem(name):
            return ctx.enter_context(nc.semaphore(name))

        def end_step():
            nc.clear_and_free_semaphores(step_sems)
            step_sems.clear()
            nc.all_engine_barrier()

        carried = {e: held_sem(e + "_carried") for e in ("dve", "pool", "pe")}

        def hold(eng, name, semaphore, value):
            eng.wait_ge(semaphore, value)
            eng.sem_inc(carried[name], 1)

        X = sb("X", [P, T, D])
        NR = sb("NR", [P, T, D])
        sumT = sb("sumT", [P, 3, WIN])
        ident = sb("ident", [P, P])
        ones = sb("ones", [P, P])
        before = sb("before", [P, P])
        iota_w = sb("iota_w", [P, P])
        win_off = sb("win_off", [P, T])
        row_far = sb("row_far", [P, T])
        src_tab = sb("src_tab", [P, NG, GC], I32)
        rel_tab = sb("rel_tab", [P, NG + 1, GC])
        base_row = sb("base_row", [1, NG], I32)
        wide_flag = sb("wide_flag", [1, 1], I32)
        deg_inv = sb("deg_inv", [P, T])
        top_val = sb("top_val", [P, T, 2])
        top_idx = sb("top_idx", [P, T, 2])
        top_w = sb("top_w", [P, T, 2])
        slot = sb("slot", [P, T, 2], I32)
        block_expert = sb("block_expert", [1, max(NB0, NB1)], I32)

        w_nodes = sb("w_nodes", [P, K2, D])
        w_edges = sb("w_edges", [DE, D])
        w_mlp = sb("w_mlp", [P, 3, K2, D])
        b_mlp = sb("b_mlp", [P, 3, K2])
        ln_rows = sb("ln_rows", [P, 6, D])
        gate_w0 = sb("gate_w0", [P, K2, E0])
        gate_b0 = sb("gate_b0", [P, E0])
        gate_w1 = sb("gate_w1", [P, K2, E1])
        router_rows = sb("router_rows", [E1, D])
        w_dense = sb("w_dense", [P, K2, 2 * D])
        FJ0, FJ1 = F0 // P, F1 // P
        b1_cols0 = sb("b1_cols0", [P, E0 * FJ0])
        b1_cols1 = sb("b1_cols1", [P, E1 * FJ1])
        b2_row = sb("b2_row", [1, E0 * D])
        s_w = held_sem("weights_loaded")
        N_LOADS = 22
        LN_NAMES = ["L0_gnn_ln_aggr_scale", "L0_gnn_ln_aggr_bias", "L0_gnn_ln_out_scale", "L0_gnn_ln_out_bias",
                    "L0_ffn_gamma", "L0_ffn_beta"]
        AGG_S, AGG_B, OUT_S, OUT_B, FFN_S, FFN_B = (ln_rows[:, k, :] for k in range(6))

        with ExitStack() as c1:
            srci = sb("srci", [NG, GE], I32, c1)
            dsti = sb("dsti", [NG, GE], I32, c1)
            srcf = sb("srcf", [NG, GE], F32, c1)
            dstf = sb("dstf", [NG, GE], F32, c1)
            dlow = sb("dlow", [NG, GE], F32, c1)
            ends = sb("ends", [NG, 2], F32, c1)
            endr = sb("endr", [1, 2, NG], F32, c1)
            rowid = sb("rowid", [P, T], I32, c1)
            iota_i = sb("iota_i", [P, P], I32, c1)
            offi = sb("offi", [P, T], I32, c1)
            zeros = sb("zeros", [P, 2048], F32, c1)
            st = sb("st", [P, T, 6], F32, c1)
            mv = sb("mv", [P, T, 2], F32, c1)
            rs = sb("rs", [P, T], F32, c1)
            b1r0 = sb("b1r0", [E0 * FJ0, P], F32, c1)
            b1r1 = sb("b1r1", [E1 * FJ1, P], F32, c1)
            bmr = sb("bmr", [3 * K2, P], F32, c1)
            ps_w = pb("ps_w", [P, 512], c1)
            ps_t = pb("ps_t", [P, GC, P], c1)
            ps_u = pb("ps_u", [P, GC, P], c1)
            ps_e = pb("ps_e", [P, 512], c1)
            ps_b = pb("ps_b", [P, 512], c1)

            s_x, s_edges, s_zero, s_n = sem("x_loaded"), sem("edges_loaded"), sem("zeros_stored"), sem("norm_stored")
            s_pad, s_cst, s_pc = sem("pads_set"), sem("consts_set"), sem("pool_chain")
            s_f, s_tr, s_end, s_rowp, s_row, s_bb, s_dv = (sem("edges_float"), sem("edges_transposed"), sem("ends_found"),
                                                           sem("ends_transposed"), sem("base_row_ready"), sem("base_broadcast"), sem("dve_chain"))
            s_wt = sem("weights_turned")
            s_sq, s_rs = sem("deviation"), sem("deviation_inverse")
            block = c1.enter_context(nc.Block())

            @block.sync
            def _(sp):
                sp.wait_ge(s_pad, 1)
                sp.dma_start(X[:, 0:T - 1, :], a["x"][0:(T - 1) * P, :].rearrange("(t p) d -> p t d", p=P)).then_inc(s_x, 16)
                sp.dma_start(X[0:LAST, T - 1, :], a["x"][(T - 1) * P:N, :]).then_inc(s_x, 16)
                for tab, name in ((srci, "src"), (dsti, "dst")):
                    sp.dma_start(tab[0:NG - 1, :], a[name][0:(NG - 1) * GE].rearrange("(g e) -> g e", e=GE)).then_inc(s_edges, 16)
                    sp.dma_start(tab[NG - 1:NG, 0:E_LAST], a[name][(NG - 1) * GE:E_N].rearrange("(a e) -> a e", a=1)).then_inc(s_edges, 16)
                sp.wait_ge(s_cst, 1)
                for r in range(0, XS_ROWS, 1024):
                    sp.dma_start(xs_dram[r:r + 1024, :].rearrange("(p r) d -> p (r d)", p=P), zeros[:]).then_inc(s_zero, 16)
                sp.wait_ge(s_dv, 6)
                sp.dma_start(n_dram.rearrange("(t p) d -> p t d", p=P), NR[:]).then_inc(s_n, 16)
                sp.wait_ge(s_n, 16)
                sp.wait_ge(s_zero, 16 * (XS_ROWS // 1024))

            @block.gpsimd
            def _(pool):
                nc.gpsimd.memset(X[:, T - 1, :], 0.0)
                nc.gpsimd.memset(srci[:], 0)
                nc.gpsimd.memset(dsti[:], -1).then_inc(s_pad, 1)
                nc.gpsimd.memset(zeros[:], 0.0)
                nc.gpsimd.memset(ident[:], 0.0)
                nc.gpsimd.memset(ones[:], 1.0)
                nc.gpsimd.memset(before[:], 1.0)
                nc.gpsimd.iota(iota_i[:], [[1, P]], base=0, channel_multiplier=0)
                nc.gpsimd.iota(offi[:], [[P, T]], base=0, channel_multiplier=0)
                nc.gpsimd.iota(rowid[:], [[P, T]], base=0, channel_multiplier=1)
                nc.gpsimd.memset(rel_tab[:], -1.0).then_inc(s_pc, 1)
                pool.wait_ge(s_pc, 1)
                nc.gpsimd.affine_select(out=ident[:], in_=ident[:], compare_op=ALU.not_equal, fill=1.0,
                                        base=0, pattern=[[-1, P]], channel_multiplier=1)
                nc.gpsimd.affine_select(out=before[:], in_=before[:], compare_op=ALU.is_gt, fill=0.0,
                                        base=0, pattern=[[1, P]], channel_multiplier=-1)
                nc.gpsimd.tensor_copy(iota_w[:], iota_i[:])
                nc.gpsimd.tensor_copy(win_off[:], offi[:])
                nc.gpsimd.tensor_scalar(row_far[:], rowid[:], float(N), FAR, ALU.is_ge, ALU.mult).then_inc(s_cst, 1)
                nc.gpsimd.memset(sumT[:], 0.0).then_inc(s_cst, 1)

            @block.scalar
            def _(act):
                loads = [(w_nodes[:], a["L0_gnn_W_message"][0:D, :].rearrange("(k p) n -> p k n", p=P)),
                         (w_edges[:], a["L0_gnn_W_message"][D:D + DE, :]),
                         (gate_w0[:], a["L0_ffn_gate_w"].rearrange("(k p) n -> p k n", p=P)),
                         (gate_b0[:], a["L0_ffn_gate_b"].rearrange("(a n) -> a n", a=1).to_broadcast([P, E0])),
                         (router_rows[:], a["L1_ffn_router_w"]),
                         (w_dense[:, :, 0:D], a["L1_gnn_W_self"].rearrange("(k p) n -> p k n", p=P)),
                         (w_dense[:, :, D:2 * D], a["L1_gnn_W_neigh"].rearrange("(k p) n -> p k n", p=P)),
                         (b1r0[:], a["L0_ffn_b1"].rearrange("e (j p) -> (e j) p", p=P)),
                         (b1r1[:], a["L1_ffn_b1"].rearrange("e (j p) -> (e j) p", p=P)),
                         (b2_row[:], a["L0_ffn_b2"].rearrange("(a e) d -> a (e d)", a=1))]
                for l in range(3):
                    loads.append((w_mlp[:, l, :, :], a[f"L0_gnn_mlp_W{l}"].rearrange("(k p) n -> p k n", p=P)))
                    loads.append((bmr[K2 * l:K2 * l + K2, :], a[f"L0_gnn_mlp_b{l}"].rearrange("(k p) -> k p", p=P)))
                for k, name in enumerate(LN_NAMES):
                    loads.append((ln_rows[:, k, :], a[name].rearrange("(a n) -> a n", a=1).to_broadcast([P, D])))
                for to, src in loads:
                    act.dma_start(to, src).then_inc(s_w, 16)
                assert len(loads) == N_LOADS
                act.wait_ge(s_edges, 64)
                nc.scalar.activation(srcf[:], srci[:], ACT.Copy).then_inc(s_f, 1)
                act.wait_ge(s_dv, 4)
                nc.scalar.activation(rs[:], rs[:], ACT.Sqrt).then_inc(s_sq, 1)

            @block.tensor
            def _(pe):
                pe.wait_ge(s_cst, 1)
                pe.wait_ge(s_f, 1)
                pe.wait_ge(s_dv, 1)
                for c in range(GC):
                    nc.tensor.transpose(ps_t[:, c, 0:NG], srcf[:, c::GC], ident[0:NG, 0:NG])
                for c in range(GC):
                    last = nc.tensor.transpose(ps_u[:, c, 0:NG], dstf[:, c::GC], ident[0:NG, 0:NG])
                last.then_inc(s_tr, 1)
                pe.wait_ge(s_end, 1)
                for c in range(2):
                    last = nc.tensor.matmul(ps_e[0:1, c * P:c * P + NG], ends[:, c:c + 1], ident[0:NG, 0:NG], start=True, stop=True)
                last.then_inc(s_rowp, 1)
                pe.wait_ge(s_row, 1)
                nc.tensor.matmul(ps_b[:, 0:NG], ones[0:1, :], endr[0:1, 0, :], start=True, stop=True).then_inc(s_bb, 1)
                pe.wait_ge(s_w, 16 * N_LOADS)
                at = 0
                for rows in (b1r0[:], b1r1[:], bmr[:], router_rows[:, 0:P], router_rows[:, P:D]):
                    n = rows.shape[0]
                    last = nc.tensor.transpose(ps_w[:, at:at + n], rows, ident[0:n, 0:n])
                    at += n
                last.then_inc(s_wt, 1)

            @block.vector
            def _(dve):
                dve.wait_ge(s_edges, 64)
                nc.vector.tensor_copy(dstf[:], dsti[:]).then_inc(s_dv, 1)
                dve.wait_ge(s_x, 32)
                for t in range(T):
                    last = nc.vector.bn_stats(st[:, t, :], X[:, t, :])
                last.then_inc(s_dv, 1)
                dve.wait_ge(s_dv, 2)
                for t in range(T):
                    last = nc.vector.bn_aggr(mv[:, t, :], st[:, t, :])
                last.then_inc(s_dv, 1)
                dve.wait_ge(s_dv, 3)
                nc.vector.tensor_scalar(rs[:], mv[:, :, 1], 1e-5, None, ALU.add).then_inc(s_dv, 1)
                nc.vector.tensor_scalar(dlow[:], dstf[:], 0.0, FAR, ALU.is_lt, ALU.mult).then_inc(s_dv, 1)
                dve.wait_ge(s_sq, 1)
                nc.vector.reciprocal(rs[:], rs[:]).then_inc(s_rs, 1)
                dve.wait_ge(s_rs, 1)
                for t in range(T):
                    last = nc.vector.tensor_scalar(NR[:, t, :], X[:, t, :], mv[:, t, 0:1], rs[:, t:t + 1], ALU.subtract, ALU.mult)
                last.then_inc(s_dv, 1)
                nc.vector.tensor_tensor(dlow[:], dlow[:], dstf[:], ALU.add).then_inc(s_dv, 1)
                dve.wait_ge(s_dv, 7)
                nc.vector.tensor_reduce(ends[:, 0:1], dlow[:], AX_X, ALU.min)
                nc.vector.tensor_reduce(ends[:, 1:2], dstf[:], AX_X, ALU.max).then_inc(s_dv, 1)
                dve.wait_ge(s_dv, 8)
                nc.vector.tensor_scalar(ends[:, 0:1], ends[:, 0:1], float(NPAD), None, ALU.min).then_inc(s_dv, 1)
                dve.wait_ge(s_dv, 9)
                nc.vector.tensor_tensor(ends[:, 1:2], ends[:, 1:2], ends[:, 0:1], ALU.subtract).then_inc(s_end, 1)
                dve.wait_ge(s_tr, 1)
                nc.vector.tensor_copy(src_tab[:].rearrange("p g c -> p c g"), ps_t[:, :, 0:NG])
                dve.wait_ge(s_rowp, 1)
                nc.vector.tensor_copy(endr[:], ps_e[0:1, 0:2 * P].rearrange("p (c g) -> p c g", c=2)[:, :, 0:NG]).then_inc(s_row, 1)
                dve.wait_ge(s_row, 1)
                nc.vector.tensor_copy(base_row[:], endr[0:1, 0, :])
                nc.vector.tensor_reduce(endr[0:1, 1, 0:1], endr[0:1, 1, :], AX_X, ALU.max).then_inc(s_dv, 1)
                dve.wait_ge(s_dv, 10)
                nc.vector.tensor_scalar(wide_flag[:], endr[0:1, 1, 0:1], float(P), None, ALU.is_ge)
                dve.wait_ge(s_bb, 1)
                dve.wait_ge(s_pc, 1)
                nc.vector.tensor_copy(rel_tab[:, 0:NG, :].rearrange("p g c -> p c g"), ps_u[:, :, 0:NG]).then_inc(s_dv, 1)
                dve.wait_ge(s_dv, 11)
                nc.vector.tensor_tensor(rel_tab[:, 0:NG, :], rel_tab[:, 0:NG, :],
                                        ps_b[:, 0:NG].unsqueeze(2).to_broadcast([P, NG, GC]), ALU.subtract).then_inc(s_dv, 1)
                dve.wait_ge(s_wt, 1)
                at = 0
                for to in (b1_cols0[:], b1_cols1[:], b_mlp[:].rearrange("p l k -> p (l k)"), gate_w1[:, 0, :], gate_w1[:, 1, :]):
                    n = to.shape[1]
                    nc.vector.tensor_copy(to, ps_w[:, at:at + n])
                    at += n

        def segment_sums(tag, rows_dram, with_edges):
            halves = 3 if with_edges else 2
            with ExitStack() as c:
                G = sb(tag + "G", [P, GU, GC, D], F32, c)
                EA = sb(tag + "EA", [P, GU, GC, P], F32, c) if with_edges else None
                OH = sb(tag + "OH", [P, GU, GC, P], F32, c)
                idx = sb(tag + "idx", [P, GU, GC], I32, c)
                rel_s = sb(tag + "rel_s", [P, GC], F32, c)
                wbase = sb(tag + "wbase", [1, 1], I32, c)
                ps = pb(tag + "ps", [P, GU, 512], c)
                gathered = [held_sem(f"{tag}gathered{s}") for s in range(GU)]
                edges_in = [sem(f"{tag}edges_in{s}") for s in range(GU)]
                idx_ready, hot_ready, summed, added = (sem(tag + "idx_ready"), sem(tag + "hot_ready"),
                                                       sem(tag + "summed"), sem(tag + "added"))
                ones_set = sem(tag + "ones_set")
                w_idx, w_gath, w_edge, w_hot, w_sum, w_turn, w_rel = (sem(tag + "wide_idx"), held_sem(tag + "wide_gathered"), sem(tag + "wide_edges"),
                                                                     sem(tag + "wide_hot"), sem(tag + "wide_summed"), sem(tag + "wide_turn"), sem(tag + "wide_rel"))
                w_free = sem(tag + "wide_free")
                block = c.enter_context(nc.Block())

                def edge_rows(g):
                    return a["edge_attr_64"][ds(g * GE, GE), :].rearrange("(p c) f -> p c f", c=GC)

                edge_rows_last = a["edge_attr_64"][(NG - 1) * GE:E_N, :].rearrange("(p c) f -> p c f", c=GC)

                def in_loops(eng, body):
                    body(0, True)
                    with eng.Fori(1, GI) as i:
                        body(i, False)

                def wide_groups(eng, group, window=None):
                    with eng.If(eng.value_load(wide_flag[0:1, 0:1], min_val=0, max_val=1) > 0):
                        with eng.Fori(0, NG) as g:
                            group(g)
                            if window:
                                with eng.Fori(1, T) as w:
                                    window(g, w, g * (T - 1) + w)

                if with_edges:
                    @block.sync
                    def _(sp):
                        sp.wait_ge(ones_set, 1)

                        def body(i, first, last=False):
                            for s in range(GU):
                                if not first:
                                    sp.wait_ge(summed, i * GU + s + 1 - GU)
                                if last and s == GU - 1:
                                    sp.dma_start(EA[0:P_LAST, s, :, 0:DE], edge_rows_last).then_inc(edges_in[s], 16)
                                else:
                                    sp.dma_start(EA[:, s, :, 0:DE], edge_rows(i * GU + s)).then_inc(edges_in[s], 16)

                        body(0, True)
                        with sp.Fori(1, GI - 1) as i:
                            body(i, False)
                        body(GI - 1, False, True)

                        with sp.If(sp.value_load(wide_flag[0:1, 0:1], min_val=0, max_val=1) > 0):
                            sp.wait_ge(summed, NG)
                            sp.dma_start(EA[:, 0, :, 0:DE], edge_rows(0)).then_inc(w_edge, 16)
                            with sp.Fori(1, NG - 1) as g:
                                sp.wait_ge(w_sum, g * (T - 1))
                                sp.dma_start(EA[:, 0, :, 0:DE], edge_rows(g)).then_inc(w_edge, 16)
                            sp.wait_ge(w_sum, (NG - 1) * (T - 1))
                            sp.dma_start(EA[0:P_LAST, 0, :, 0:DE], edge_rows_last).then_inc(w_edge, 16)

                @block.gpsimd
                def _(pool):
                    if with_edges:
                        nc.gpsimd.memset(EA[:], 1.0).then_inc(ones_set, 1)

                    def body(i, first):
                        for s in range(GU):
                            hold(pool, "pool", idx_ready, i * GU + s + 1)
                            for k in range(GC):
                                pool.indirect_dma_start(out=G[:, s, k, :], out_offset=None, in_=rows_dram,
                                                        in_offset=bass.IndirectOffsetOnAxis(ap=idx[:, s, k:k + 1], axis=0)
                                                        ).then_inc(gathered[s], 16)

                    in_loops(pool, body)

                    def wide(g):
                        hold(pool, "pool", w_idx, g + 1)
                        for k in range(GC):
                            pool.indirect_dma_start(out=G[:, 0, k, :], out_offset=None, in_=rows_dram,
                                                    in_offset=bass.IndirectOffsetOnAxis(ap=idx[:, 0, k:k + 1], axis=0)
                                                    ).then_inc(w_gath, 16)

                    wide_groups(pool, wide)

                @block.scalar
                def _(act):
                    def body(i, first):
                        for s in range(GU):
                            if not first:
                                act.wait_ge(summed, i * GU + s + 1 - GU)
                            nc.scalar.activation(idx[:, s, :], src_tab[:, ds(i * GU + s, 1), :].rearrange("p a c -> p (a c)"),
                                                 ACT.Copy).then_inc(idx_ready, 1)

                    in_loops(act, body)

                    def wide(g):
                        act.wait_ge(w_free, g + 1)
                        nc.scalar.activation(idx[:, 0, :], src_tab[:, ds(g, 1), :].rearrange("p a c -> p (a c)"),
                                             ACT.Copy).then_inc(w_idx, 1)

                    wide_groups(act, wide)

                def products(pe, s):
                    for h in range(halves):
                        for k in range(GC):
                            rows = EA[:, s, k, :] if h == 2 else G[:, s, k, h * P:(h + 1) * P]
                            last = nc.tensor.matmul(ps[:, s, h * P:(h + 1) * P], rows, OH[:, s, k, :],
                                                    start=(k == 0), stop=(k == GC - 1))
                    return last

                @block.tensor
                def _(pe):
                    def body(i, first):
                        for s in range(GU):
                            pe.wait_ge(hot_ready, i * GU + s + 1)
                            if with_edges:
                                pe.wait_ge(edges_in[s], (i + 1) * 16)
                            pe.wait_ge(gathered[s], (i + 1) * 16 * GC)
                            if not first:
                                pe.wait_ge(added, i * GU + s + 1 - GU)
                            products(pe, s).then_inc(summed, 1)

                    in_loops(pe, body)

                    def wide(g):
                        if with_edges:
                            pe.wait_ge(w_edge, (g + 1) * 16)
                        hold(pe, "pe", w_gath, (g + 1) * 16 * GC)

                    def window(g, w, n):
                        pe.wait_ge(w_hot, n)
                        products(pe, 0).then_inc(w_sum, 1)

                    wide_groups(pe, wide, window)

                @block.vector
                def _(dve):
                    iota_b = iota_w[:].unsqueeze(1).to_broadcast([P, GC, P])

                    def hot(g, s):
                        return nc.vector.tensor_tensor(
                            OH[:, s, :, :], iota_b,
                            rel_tab[:, ds(g, 1), :].rearrange("p a c -> p (a c)").unsqueeze(2).to_broadcast([P, GC, P]), ALU.is_equal)

                    def add(base, s):
                        window = sumT[:, 0:halves, ds(base, P)]
                        return nc.vector.tensor_tensor(window, window,
                                                       ps[:, s, 0:halves * P].rearrange("p (h w) -> p h w", h=halves), ALU.add)

                    def body(i, first):
                        for s in range(GU):
                            if not (first and s < GU - 1):
                                dve.wait_ge(summed, i * GU + s + 2 - GU)
                            hot(i * GU + s + 1, (s + 1) % GU).then_inc(hot_ready, 1)
                            base = dve.value_load(base_row[0:1, ds(i * GU + s, 1)], min_val=0, max_val=NPAD)
                            dve.wait_ge(summed, i * GU + s + 1)
                            if not (first and s == 0):
                                dve.wait_ge(added, i * GU + s)
                            add(base, s).then_inc(added, 1)

                    hot(0, 0).then_inc(hot_ready, 1)
                    in_loops(dve, body)

                    def wide(g):
                        dve.sem_inc(w_free, 1)

                    def window(g, w, n):
                        dve.wait_ge(w_turn, n)
                        rel_g = rel_tab[:, ds(g, 1), :].rearrange("p a c -> p (a c)")
                        nc.vector.tensor_scalar(rel_s[:], rel_g, win_off[:, ds(w, 1)], None, ALU.subtract)
                        nc.vector.tensor_scalar(wbase[:], base_row[0:1, ds(g, 1)], win_off[0:1, ds(w, 1)], float(NPAD),
                                                ALU.add, ALU.min).then_inc(w_rel, 1)
                        dve.wait_ge(w_rel, n)
                        nc.vector.tensor_tensor(OH[:, 0, :, :], iota_b, rel_s[:].unsqueeze(2).to_broadcast([P, GC, P]),
                                                ALU.is_equal).then_inc(w_hot, 1)
                        base = dve.value_load(wbase[0:1, 0:1], min_val=0, max_val=NPAD)
                        dve.wait_ge(w_sum, n)
                        add(base, 0).then_inc(w_turn, 1)

                    dve.wait_ge(added, NG)
                    dve.wait_ge(hot_ready, NG + 1)
                    dve.sem_inc(w_turn, 1)
                    wide_groups(dve, wide, window)

        end_step()
        segment_sums("L0_", n_dram, True)
        end_step()
        if debug == "sums":
            with ExitStack() as c:
                s_o = sem("dbg")
                block = c.enter_context(nc.Block())

                @block.sync
                def _(sp):
                    sp.dma_start(out.rearrange("h p w -> p h w"), sumT[:, :, 0:N]).then_inc(s_o, 16)
                    sp.wait_ge(s_o, 16)
            return

        def tile_of(t3, t):
            return t3[:, ds(t, 1), :].rearrange("p a d -> p (a d)")

        def turn2(ps_half, rows, ready):
            for k in range(K2):
                last = nc.tensor.transpose(ps_half[:, k * P:(k + 1) * P], rows[:, k * P:(k + 1) * P], ident[:])
            last.then_inc(ready, 1)

        class Norm:

            def __init__(self, tag, c, per_iter):
                self.st, self.mv = sb(tag + "st", [P, TU, 6], F32, c), sb(tag + "mv", [P, TU, 2], F32, c)
                self.rs = sb(tag + "rs", [P, TU], F32, c)
                self.stats, self.aggr, self.var, self.dev, self.inv = (
                    sem(tag + "stats_taken"), sem(tag + "stats_joined"), sem(tag + "variance"), sem(tag + "deviation"),
                    sem(tag + "deviation_inverse"))
                self.per_iter = per_iter

            def deviation(self, act, i, k):
                act.wait_ge(self.var, i * self.per_iter + k + 1)
                nc.scalar.activation(self.rs[:], self.rs[:], ACT.Sqrt).then_inc(self.dev, 1)

            def take(self, dve, i, k, u, rows):
                nc.vector.bn_stats(self.st[:, u, :], rows).then_inc(self.stats, 1)

            def factors(self, dve, i, k, eps):
                n = i * self.per_iter + k + 1
                hold(dve, "dve", self.stats, n * TU)
                for u in range(TU):
                    last = nc.vector.bn_aggr(self.mv[:, u, :], self.st[:, u, :])
                last.then_inc(self.aggr, 1)
                dve.wait_ge(self.aggr, n)
                nc.vector.tensor_scalar(self.rs[:], self.mv[:, :, 1], eps, None, ALU.add).then_inc(self.var, 1)
                dve.wait_ge(self.dev, n)
                nc.vector.reciprocal(self.rs[:], self.rs[:]).then_inc(self.inv, 1)
                dve.wait_ge(self.inv, n)

            def apply(self, out, rows, u):
                return nc.vector.tensor_scalar(out, rows, self.mv[:, u, 0:1], self.rs[:, u:u + 1], ALU.subtract, ALU.mult)

        with ExitStack() as c:
            lhs = sb("lhs", [P, TU, 3, P], F32, c)
            H = sb("H", [P, TU, D], F32, c)
            hT = sb("hT", [P, TU, K2, P], F32, c)
            yT = sb("yT", [P, TU, K2, P], F32, c)
            LG = sb("LG", [P, TU, E0], F32, c)
            v8 = sb("v8", [P, TU, 8], F32, c)
            i8 = sb("i8", [P, TU, 8], U32, c)
            ps = pb("psn", [P, TU, 512], c)
            norm = Norm("n0", c, 3)
            names = ["free", "lhs_ready", "agg_done", "hpre", "hnorm", "hscaled", "h_ready", "tp_done", "hT_ready", "ly_done", "y_ready",
                     "skip_added", "back_done", "zpre", "znorm", "zscaled", "z_ready", "x_ready", "n2_ready", "tn_done",
                     "nT_ready", "lg_done", "lg_ready", "v8_ready", "i8_ready", "kept", "deg_in"]
            S = {n: sem("N0" + n) for n in names}
            block = c.enter_context(nc.Block())

            def LO(u):
                return ps[:, u, 0:D]

            def HI(u):
                return ps[:, u, D:2 * D]

            @block.scalar
            def _(act):
                with act.Fori(0, IT) as i:
                    act.wait_ge(S["free"], i + 1)
                    for u in range(TU):
                        nc.scalar.activation(lhs[:, u, :, :], sumT[:, :, ds((i * TU + u) * P, P)], ACT.Copy).then_inc(S["lhs_ready"], 1)
                    norm.deviation(act, i, 0)
                    for u in range(TU):
                        act.wait_ge(S["tp_done"], i * TU + u + 1)
                        nc.scalar.activation(hT[:, u, :, :].rearrange("p k n -> p (k n)"), HI(u), ACT.Copy).then_inc(S["hT_ready"], 1)
                    for l in range(3):
                        for u in range(TU):
                            act.wait_ge(S["ly_done"], (i * 3 + l) * TU + u + 1)
                            half = (LO, HI, LO)[l](u)
                            for m in range(K2):
                                last = nc.scalar.activation(yT[:, u, m, :], half[:, m * P:(m + 1) * P],
                                                            ACT.Relu if l < 2 else ACT.Identity, bias=b_mlp[:, l, m:m + 1])
                            last.then_inc(S["y_ready"], 1)
                    norm.deviation(act, i, 1)
                    norm.deviation(act, i, 2)
                    for u in range(TU):
                        act.wait_ge(S["tn_done"], i * TU + u + 1)
                        nc.scalar.activation(yT[:, u, :, :].rearrange("p k n -> p (k n)"), LO(u), ACT.Copy).then_inc(S["nT_ready"], 1)

            @block.tensor
            def _(pe):
                with pe.Fori(0, IT) as i:
                    for u in range(TU):
                        pe.wait_ge(S["lhs_ready"], i * TU + u + 1)
                        for k in range(K2):
                            nc.tensor.matmul(LO(u), lhs[:, u, k, :], w_nodes[:, k, :], start=(k == 0), stop=False)
                        nc.tensor.matmul(LO(u), lhs[0:DE, u, 2, :], w_edges[:], start=False, stop=True)
                        nc.tensor.matmul(ps[:, u, D:D + 1], lhs[:, u, 2, :], ident[:, DE:DE + 1], start=True, stop=True).then_inc(S["agg_done"], 1)
                    for u in range(TU):
                        pe.wait_ge(S["h_ready"], i * TU + u + 1)
                        turn2(HI(u), H[:, u, :], S["tp_done"])
                    for l in range(3):
                        for u in range(TU):
                            if l == 0:
                                pe.wait_ge(S["hT_ready"], i * TU + u + 1)
                            else:
                                pe.wait_ge(S["skip_added"], (i * 3 + l - 1) * TU + u + 1)
                            half = (LO, HI, LO)[l](u)
                            for m in range(K2):
                                for k in range(K2):
                                    last = nc.tensor.matmul(half[:, m * P:(m + 1) * P], w_mlp[:, l, k, m * P:(m + 1) * P],
                                                            hT[:, u, k, :], start=(k == 0), stop=(k == K2 - 1))
                            last.then_inc(S["ly_done"], 1)
                    for u in range(TU):
                        pe.wait_ge(S["skip_added"], (i * 3 + 2) * TU + u + 1)
                        for k in range(K2):
                            last = nc.tensor.transpose(HI(u)[:, k * P:(k + 1) * P], hT[:, u, k, :], ident[:])
                        last.then_inc(S["back_done"], 1)
                    for u in range(TU):
                        pe.wait_ge(S["n2_ready"], i * TU + u + 1)
                        turn2(LO(u), H[:, u, :], S["tn_done"])
                    for u in range(TU):
                        pe.wait_ge(S["nT_ready"], i * TU + u + 1)
                        for k in range(K2):
                            last = nc.tensor.matmul(ps[:, u, D:D + E0], yT[:, u, k, :], gate_w0[:, k, :], start=(k == 0), stop=(k == K2 - 1))
                        last.then_inc(S["lg_done"], 1)

            @block.gpsimd
            def _(pool):
                with pool.Fori(0, IT) as i:
                    def scale_bias(u, ready, scaled, done, scale, bias):
                        pool.wait_ge(S[ready], i * TU + u + 1)
                        nc.gpsimd.tensor_tensor(H[:, u, :], H[:, u, :], scale, ALU.mult).then_inc(S[scaled], 1)
                        pool.wait_ge(S[scaled], i * TU + u + 1)
                        nc.gpsimd.tensor_tensor(H[:, u, :], H[:, u, :], bias, ALU.add).then_inc(S[done], 1)

                    for u in range(TU):
                        scale_bias(u, "hnorm", "hscaled", "h_ready", AGG_S, AGG_B)
                    for l in range(3):
                        for u in range(TU):
                            pool.wait_ge(S["y_ready"], (i * 3 + l) * TU + u + 1)
                            nc.gpsimd.tensor_tensor(hT[:, u, :, :], hT[:, u, :, :], yT[:, u, :, :], ALU.add).then_inc(S["skip_added"], 1)
                    for u in range(TU):
                        scale_bias(u, "znorm", "zscaled", "z_ready", OUT_S, OUT_B)

            @block.vector
            def _(dve):
                dve.sem_inc(S["free"], 1)
                with dve.Fori(0, IT) as i:
                    for u in range(TU):
                        n = i * TU + u + 1
                        dve.wait_ge(S["agg_done"], n)
                        nc.vector.tensor_scalar(deg_inv[:, ds(i * TU + u, 1)], ps[:, u, D:D + 1], 1.0, None, ALU.max).then_inc(S["deg_in"], 1)
                        nc.vector.scalar_tensor_tensor(H[:, u, :], LO(u), 0.0, tile_of(NR, i * TU + u), ALU.max, ALU.add).then_inc(S["hpre"], 1)
                        hold(dve, "dve", S["hpre"], n)
                        norm.take(dve, i, 0, u, H[:, u, :])
                    norm.factors(dve, i, 0, 1e-6)
                    for u in range(TU):
                        norm.apply(H[:, u, :], H[:, u, :], u).then_inc(S["hnorm"], 1)
                    for u in range(TU):
                        n = i * TU + u + 1
                        dve.wait_ge(S["back_done"], n)
                        nc.vector.tensor_tensor(H[:, u, :], HI(u), tile_of(NR, i * TU + u), ALU.add).then_inc(S["zpre"], 1)
                        hold(dve, "dve", S["zpre"], n)
                        norm.take(dve, i, 1, u, H[:, u, :])
                    norm.factors(dve, i, 1, 1e-6)
                    for u in range(TU):
                        norm.apply(H[:, u, :], H[:, u, :], u).then_inc(S["znorm"], 1)
                    for u in range(TU):
                        n = i * TU + u + 1
                        xt = tile_of(X, i * TU + u)
                        dve.wait_ge(S["z_ready"], n)
                        nc.vector.tensor_tensor(xt, xt, H[:, u, :], ALU.add).then_inc(S["x_ready"], 1)
                        hold(dve, "dve", S["x_ready"], n)
                        norm.take(dve, i, 2, u, xt)
                    norm.factors(dve, i, 2, 1e-5)
                    for u in range(TU):
                        norm.apply(H[:, u, :], tile_of(X, i * TU + u), u).then_inc(S["n2_ready"], 1)
                    hold(dve, "dve", S["n2_ready"], (i + 1) * TU)
                    nc.vector.tensor_copy(NR[:, ds(i * TU, TU), :], H[:]).then_inc(S["kept"], 1)
                    for u in range(TU):
                        n = i * TU + u + 1
                        dve.wait_ge(S["lg_done"], n)
                        nc.vector.tensor_tensor(LG[:, u, :], ps[:, u, D:D + E0], gate_b0[:], ALU.add).then_inc(S["lg_ready"], 1)
                        hold(dve, "dve", S["lg_ready"], n)
                        nc.vector.max(v8[:, u, :], LG[:, u, :]).then_inc(S["v8_ready"], 1)
                        hold(dve, "dve", S["v8_ready"], n)
                        nc.vector.max_index(i8[:, u, :], v8[:, u, :], LG[:, u, :]).then_inc(S["i8_ready"], 1)
                    hold(dve, "dve", S["i8_ready"], (i + 1) * TU)
                    nc.vector.tensor_copy(top_val[:, ds(i * TU, TU), :], v8[:, :, 0:2])
                    nc.vector.tensor_copy(top_idx[:, ds(i * TU, TU), :], i8[:, :, 0:2]).then_inc(S["free"], 1)
                dve.wait_ge(S["deg_in"], T)
                nc.vector.reciprocal(deg_inv[:], deg_inv[:])

        def route(tag, E, NB, softmax_of_two):
            with ExitStack() as c:
                hot = sb(tag + "hot", [P, 2, T, E], F32, c)
                both = sb(tag + "both", [P, T, E], F32, c)
                tot = sb(tag + "tot", [P, E, T], F32, c)
                inc = sb(tag + "inc", [P, E, T], F32, c)
                fresh = sb(tag + "fresh", [P, E, T], F32, c)
                cnt_i = sb(tag + "cnt_i", [P, E], I32, c)
                cnt = sb(tag + "cnt", [P, E], F32, c)
                end = sb(tag + "end", [P, E], F32, c)
                iota_e = sb(tag + "iota_e", [P, E], F32, c)
                at = sb(tag + "at", [P, T, E], F32, c)
                tmp = sb(tag + "tmp", [P, T, E], F32, c)
                rowf = sb(tag + "rowf", [P, T, 2], F32, c)
                blk_at = sb(tag + "blk_at", [1, NB], F32, c)
                blk_ge = sb(tag + "blk_ge", [1, NB, E], F32, c)
                blk_f = sb(tag + "blk_f", [1, NB], F32, c)
                ii = sb(tag + "ii", [P, E], I32, c)
                bi = sb(tag + "bi", [1, NB], I32, c)
                e1 = sb(tag + "e1", [P, T], F32, c)
                e2 = sb(tag + "e2", [P, T], F32, c)
                ps_b = pb(tag + "ps_before", [P, 512], c)
                ps_a = pb(tag + "ps_all", [P, 512], c)
                s_c, s_h, s_p, s_d, s_e, s_s = (sem(tag + "consts"), sem(tag + "hot_ready"), sem(tag + "counted"),
                                                sem(tag + "dve_chain"), sem(tag + "exp"), held_sem(tag + "scattered"))
                s_slot, s_pc = sem(tag + "slots_ready"), sem(tag + "pool_chain")
                block = c.enter_context(nc.Block())
                TE = T * E

                @block.gpsimd
                def _(pool):
                    nc.gpsimd.iota(ii[:], [[1, E]], base=0, channel_multiplier=0)
                    nc.gpsimd.iota(bi[:], [[P, NB]], base=0, channel_multiplier=0)
                    nc.gpsimd.memset(fresh[:], 1.0).then_inc(s_pc, 1)
                    pool.wait_ge(s_pc, 1)
                    nc.gpsimd.tensor_copy(iota_e[:], ii[:])
                    nc.gpsimd.tensor_copy(blk_at[:], bi[:])
                    nc.gpsimd.memset(fresh[:, :, 0], 0.0).then_inc(s_c, 1)
                    pool.wait_ge(s_slot, 1)
                    for t in range(T):
                        for k in range(2):
                            pool.indirect_dma_start(out=xs_dram, out_offset=bass.IndirectOffsetOnAxis(ap=slot[:, t, k:k + 1], axis=0),
                                                    in_=NR[:, t, :], in_offset=None, bounds_check=NB * P - 1,
                                                    oob_is_err=False).then_inc(s_s, 16)
                    pool.wait_ge(s_s, 16 * 2 * T)

                @block.tensor
                def _(pe):
                    pe.wait_ge(s_h, 1)
                    nc.tensor.matmul(ps_b[:, 0:TE], before[:], both[:].rearrange("p t e -> p (t e)"), start=True, stop=True)
                    nc.tensor.matmul(ps_a[:, 0:TE], ones[:], both[:].rearrange("p t e -> p (t e)"), start=True, stop=True).then_inc(s_p, 1)

                @block.scalar
                def _(act):
                    if softmax_of_two:
                        act.wait_ge(s_e, 1)
                        nc.scalar.activation(e1[:], e1[:], ACT.Exp).then_inc(s_e, 1)

                @block.vector
                def _(dve):
                    n = [0]

                    def link(ins):
                        n[0] += 1
                        ins.then_inc(s_d, 1)
                        dve.wait_ge(s_d, n[0])

                    if softmax_of_two:
                        nc.vector.tensor_tensor(e1[:], top_val[:, :, 1], top_val[:, :, 0], ALU.subtract).then_inc(s_e, 1)
                        dve.wait_ge(s_e, 2)
                        link(nc.vector.tensor_scalar(e2[:], e1[:], 1.0, None, ALU.add))
                        link(nc.vector.reciprocal(top_w[:, :, 0], e2[:]))
                        nc.vector.tensor_tensor(top_w[:, :, 1], top_w[:, :, 0], e1[:], ALU.mult)
                    else:
                        link(nc.vector.tensor_tensor(e1[:], top_val[:, :, 1], top_val[:, :, 0], ALU.add))
                        link(nc.vector.tensor_scalar(e1[:], e1[:], 1e-12, None, ALU.max))
                        link(nc.vector.reciprocal(e2[:], e1[:]))
                        nc.vector.tensor_tensor(top_w[:], top_val[:], e2[:].unsqueeze(2).to_broadcast([P, T, 2]), ALU.mult)
                    link(nc.vector.tensor_tensor(top_idx[:], top_idx[:], row_far[:].unsqueeze(2).to_broadcast([P, T, 2]), ALU.add))
                    dve.wait_ge(s_c, 1)
                    for k in range(2):
                        last = nc.vector.tensor_tensor(hot[:, k, :, :], iota_e[:].unsqueeze(1).to_broadcast([P, T, E]),
                                                       top_idx[:, :, k:k + 1].to_broadcast([P, T, E]), ALU.is_equal)
                    link(last)
                    nc.vector.tensor_tensor(both[:], hot[:, 0, :, :], hot[:, 1, :, :], ALU.add).then_inc(s_h, 1)
                    dve.wait_ge(s_p, 1)
                    link(nc.vector.tensor_copy(tot[:], ps_a[:, 0:TE].rearrange("p (t e) -> p e t", e=E)))
                    link(nc.vector.tensor_tensor_scan(inc[:].rearrange("p e t -> p (e t)"), fresh[:].rearrange("p e t -> p (e t)"),
                                                      tot[:].rearrange("p e t -> p (e t)"), 0.0, ALU.mult, ALU.add))
                    link(nc.vector.tensor_scalar(cnt_i[:], inc[:, :, T - 1], float(P - 1), None, ALU.add))
                    link(nc.vector.tensor_scalar(cnt_i[:], cnt_i[:], 7, 7, ALU.arith_shift_right, ALU.logical_shift_left))
                    link(nc.vector.tensor_copy(cnt[:], cnt_i[:]))
                    link(nc.vector.tensor_tensor_scan(end[:], ones[:, 0:E], cnt[:], 0.0, ALU.mult, ALU.add))
                    link(nc.vector.tensor_tensor(cnt[:], end[:], cnt[:], ALU.subtract))
                    link(nc.vector.tensor_tensor(inc[:], inc[:], tot[:], ALU.subtract))
                    link(nc.vector.tensor_tensor(inc[:], inc[:], cnt[:].unsqueeze(2).to_broadcast([P, E, T]), ALU.add))
                    link(nc.vector.tensor_tensor(at[:], ps_b[:, 0:TE].rearrange("p (t e) -> p t e", e=E),
                                                 inc[:].rearrange("p e t -> p t e"), ALU.add))
                    for k in range(2):
                        link(nc.vector.tensor_tensor(tmp[:], hot[:, k, :, :], at[:], ALU.mult))
                        link(nc.vector.tensor_reduce(rowf[:, :, k], tmp[:], AX_X, ALU.add))
                    nc.vector.tensor_tensor(slot[:], rowf[:], row_far[:].unsqueeze(2).to_broadcast([P, T, 2]), ALU.add).then_inc(s_slot, 1)
                    link(nc.vector.tensor_tensor(blk_ge[:], blk_at[:].unsqueeze(2).to_broadcast([1, NB, E]),
                                                 end[0:1, :].unsqueeze(1).to_broadcast([1, NB, E]), ALU.is_ge))
                    link(nc.vector.tensor_reduce(blk_f[:], blk_ge[:], AX_X, ALU.add))
                    nc.vector.tensor_scalar(block_expert[:, 0:NB], blk_f[:], float(E - 1), None, ALU.min)

        def experts(tag, E, F, NB, w1, b1_cols, w2, b2, func):
            FJ = F // P
            with ExitStack() as c:
                xs = sb(tag + "xs", [P, BU, D], F32, c)
                xT = sb(tag + "xT", [P, BU, K2, P], F32, c)
                W1 = sb(tag + "W1", [P, BU, K2, F], F32, c)
                W2 = sb(tag + "W2", [P, BU, FJ, D], F32, c)
                hidT = sb(tag + "hidT", [P, BU, FJ, P], F32, c)
                ys = sb(tag + "ys", [P, BU, D], F32, c)
                b2r = sb(tag + "b2r", [1, E * D], F32, c)
                ps_x = pb(tag + "ps_x", [P, 2, 512], c)
                ps_h = pb(tag + "ps_h", [P, 2, 512], c)
                ps_y = pb(tag + "ps_y", [P, 2, 512], c)
                rows_in = [sem(f"{tag}rows_in{s}") for s in range(BU)]
                w1_in = [sem(f"{tag}w1_in{s}") for s in range(BU)]
                w2_in = [sem(f"{tag}w2_in{s}") for s in range(BU)]
                stored = [held_sem(f"{tag}stored{s}") for s in range(BU)]
                b2_in, turned, xT_ready, mm1, hid_ready, mm2, y_ready = (sem(tag + n) for n in (
                    "b2_in", "turned", "xT_ready", "first_done", "hidden_ready", "second_done", "y_ready"))
                block = c.enter_context(nc.Block())
                NI = NB // BU
                assert NI * BU == NB

                def in_loops(eng, body):
                    body(0, True)
                    with eng.Fori(1, NI) as i:
                        body(i, False)

                def expert_of(eng, b):
                    return eng.value_load(block_expert[0:1, ds(b, 1)], min_val=0, max_val=E - 1)

                @block.sync
                def _(sp):
                    sp.dma_start(b2r[:], b2.rearrange("(a e) d -> a (e d)", a=1)).then_inc(b2_in, 16)

                    def body(i, first):
                        for s in range(BU):
                            b = i * BU + s
                            e = expert_of(sp, b)
                            if not first:
                                sp.wait_ge(turned, b + 1 - BU)
                            sp.dma_start(xs[:, s, :], xs_dram[ds(b * P, P), :]).then_inc(rows_in[s], 16)
                            if not first:
                                sp.wait_ge(mm1, b + 1 - BU)
                            sp.dma_start(W1[:, s, :, :], w1[ds(e, 1), :, :].rearrange("a (k p) f -> p (a k) f", p=P)).then_inc(w1_in[s], 16)
                            if not first:
                                sp.wait_ge(mm2, b + 1 - BU)
                            sp.dma_start(W2[:, s, :, :], w2[ds(e, 1), :, :].rearrange("a (j p) d -> p (a j) d", p=P)).then_inc(w2_in[s], 16)

                    in_loops(sp, body)

                @block.tensor
                def _(pe):
                    def turn(b, s, pre, reuse):
                        pe.wait_ge(rows_in[s], pre)
                        if reuse:
                            pe.wait_ge(xT_ready, b - 1)
                        turn2(ps_x[:, s % 2, 0:D], xs[:, s, :], turned)

                    def first_layer(b, s, pre, reuse):
                        pe.wait_ge(w1_in[s], pre)
                        pe.wait_ge(xT_ready, b + 1)
                        if reuse:
                            pe.wait_ge(hid_ready, b - 1)
                        for j in range(FJ):
                            for k in range(K2):
                                last = nc.tensor.matmul(ps_h[:, s % 2, j * P:(j + 1) * P], W1[:, s, k, j * P:(j + 1) * P],
                                                        xT[:, s, k, :], start=(k == 0), stop=(k == K2 - 1))
                        last.then_inc(mm1, 1)

                    def second_layer(b, s, pre, reuse):
                        e = expert_of(pe, b)
                        pe.wait_ge(w2_in[s], pre)
                        pe.wait_ge(hid_ready, b + 1)
                        if reuse:
                            pe.wait_ge(y_ready, b - 1)
                        for j in range(FJ):
                            nc.tensor.matmul(ps_y[:, s % 2, 0:D], hidT[:, s, j, :], W2[:, s, j, :], start=(j == 0), stop=False)
                        nc.tensor.matmul(ps_y[:, s % 2, 0:D], ones[0:1, :], b2r[0:1, ds(e * D, D)], start=False, stop=True).then_inc(mm2, 1)

                    def body(i, first, last=False):
                        for s in range(BU):
                            b = i * BU + s
                            t = (s + 1) % BU
                            if not (last and s == BU - 1):
                                turn(b + 1, t, (i + 1 + (s == BU - 1)) * 16, not (first and s < 1))
                            first_layer(b, s, (i + 1) * 16, not (first and s < 2))
                            if not (first and s == 0):
                                second_layer(b - 1, (s - 1) % BU, (i + (s > 0)) * 16, not (first and s < 3))

                    pe.wait_ge(b2_in, 16)
                    turn(0, 0, 16, False)
                    body(0, True)
                    with pe.Fori(1, NI - 1) as i:
                        body(i, False)
                    body(NI - 1, False, True)
                    second_layer(NB - 1, BU - 1, NI * 16, True)

                @block.scalar
                def _(act):
                    def xT_copy(b, s, first):
                        act.wait_ge(turned, b + 1)
                        if not first:
                            act.wait_ge(mm1, b + 1 - BU)
                        nc.scalar.activation(xT[:, s, :, :].rearrange("p k n -> p (k n)"), ps_x[:, s % 2, 0:D], ACT.Copy).then_inc(xT_ready, 1)

                    def hidden(b, s, first):
                        e = expert_of(act, b)
                        act.wait_ge(mm1, b + 1)
                        if not first:
                            act.wait_ge(mm2, b + 1 - BU)
                        for j in range(FJ):
                            last = nc.scalar.activation(hidT[:, s, j, :], ps_h[:, s % 2, j * P:(j + 1) * P], func,
                                                        bias=b1_cols[:, ds(e * FJ + j, 1)])
                        last.then_inc(hid_ready, 1)

                    def body(i, first, last=False):
                        for s in range(BU):
                            b = i * BU + s
                            if not (last and s == BU - 1):
                                xT_copy(b + 1, (s + 1) % BU, first and s < BU - 1)
                            hidden(b, s, first)

                    xT_copy(0, 0, True)
                    body(0, True)
                    with act.Fori(1, NI - 1) as i:
                        body(i, False)
                    body(NI - 1, False, True)

                @block.vector
                def _(dve):
                    def body(i, first):
                        for s in range(BU):
                            b = i * BU + s
                            dve.wait_ge(mm2, b + 1)
                            if not first:
                                dve.wait_ge(stored[s], i * 16)
                            nc.vector.tensor_copy(ys[:, s, :], ps_y[:, s % 2, 0:D]).then_inc(y_ready, 1)

                    in_loops(dve, body)

                @block.gpsimd
                def _(pool):
                    def body(i, first):
                        for s in range(BU):
                            b = i * BU + s
                            pool.wait_ge(y_ready, b + 1)
                            pool.dma_start(ys_dram[ds(b * P, P), :], ys[:, s, :]).then_inc(stored[s], 16)

                    in_loops(pool, body)
                    for s in range(BU):
                        pool.wait_ge(stored[s], NI * 16)

        class Mix:

            def __init__(self, tag, c, NB):
                self.Y = sb(tag + "Y", [P, TU, 2, D], F32, c)
                self.idx = sb(tag + "gidx", [P, TU, 2], I32, c)
                self.gathered = [held_sem(f"{tag}gathered{u}") for u in range(TU)]
                self.cleared, self.idx_ready, self.once, self.twice = (
                    sem(tag + n) for n in ("cleared", "idx_ready", "mixed_once", "mixed_twice"))
                self.NB = NB

            def clear(self, pool):
                nc.gpsimd.memset(self.Y[:], 0.0).then_inc(self.cleared, 1)
                pool.wait_ge(self.cleared, 1)

            def indices(self, act, i):
                if not isinstance(i, int):
                    act.wait_ge(self.twice, i * TU)
                nc.scalar.activation(self.idx[:], slot[:, ds(i * TU, TU), :], ACT.Copy).then_inc(self.idx_ready, 1)

            def gathers(self, pool, i):
                hold(pool, "pool", self.idx_ready, i + 1)
                for u in range(TU):
                    for k in range(2):
                        pool.indirect_dma_start(out=self.Y[:, u, k, :], out_offset=None, in_=ys_dram,
                                                in_offset=bass.IndirectOffsetOnAxis(ap=self.idx[:, u, k:k + 1], axis=0),
                                                bounds_check=self.NB * P - 1, oob_is_err=False).then_inc(self.gathered[u], 16)

            def mix(self, dve, i, u, out, own):
                dve.wait_ge(self.gathered[u], (i + 1) * 32)
                t = i * TU + u
                nc.vector.scalar_tensor_tensor(out, self.Y[:, u, 0, :], top_w[:, ds(t, 1), 0], own, ALU.mult, ALU.add).then_inc(self.once, 1)
                dve.wait_ge(self.once, t + 1)
                nc.vector.scalar_tensor_tensor(out, self.Y[:, u, 1, :], top_w[:, ds(t, 1), 1], out, ALU.mult, ALU.add).then_inc(self.twice, 1)
                hold(dve, "dve", self.twice, t + 1)

        def once_and_loop(eng, body):
            body(0)
            with eng.Fori(1, IT) as i:
                body(i)

        def sparse_products():
            BIG = -3.0e38
            with ExitStack() as c:
                H = sb("m0H", [P, TU, D], F32, c)
                nT = sb("m0nT", [P, TU, K2, P], F32, c)
                HN = sb("m0HN", [P, TU, D], F32, c)
                WK = sb("m0WK", [P, TU, D], F32, c)
                v8 = sb("m0v8", [P, TU, 8], F32, c)
                ps = pb("m0ps", [P, TU, 512], c)
                norm = Norm("m0", c, 2)
                mixer = Mix("m0", c, NB0)
                S = {n: sem("M0" + n) for n in ("free", "znorm", "zscaled", "z_ready", "x_ready", "n_ready", "turned", "nT_ready", "dense",
                                                "neigh", "x_added", "max8", "replaced", "masked", "sparse", "stored", "cleared")}
                block = c.enter_context(nc.Block())

                @block.gpsimd
                def _(pool):
                    mixer.clear(pool)
                    nc.gpsimd.memset(sumT[:], 0.0).then_inc(S["cleared"], 1)

                    def body(i):
                        mixer.gathers(pool, i)
                        for u in range(TU):
                            n = i * TU + u + 1
                            pool.wait_ge(S["znorm"], n)
                            nc.gpsimd.tensor_tensor(H[:, u, :], H[:, u, :], FFN_S, ALU.mult).then_inc(S["zscaled"], 1)
                            pool.wait_ge(S["zscaled"], n)
                            nc.gpsimd.tensor_tensor(H[:, u, :], H[:, u, :], FFN_B, ALU.add).then_inc(S["z_ready"], 1)
                        for u in range(TU):
                            n = i * TU + u + 1
                            pool.wait_ge(S["masked"], n)
                            nc.gpsimd.tensor_tensor(WK[:, u, :], WK[:, u, :], HN[:, u, :], ALU.mult).then_inc(S["sparse"], 1)

                    once_and_loop(pool, body)

                @block.sync
                def _(sp):
                    def body(i):
                        sp.wait_ge(S["sparse"], (i + 1) * TU)
                        sp.dma_start(n_dram[ds(i * TU * P, TU * P), :].rearrange("(u p) d -> p u d", p=P), WK[:]).then_inc(S["stored"], 16)

                    once_and_loop(sp, body)
                    sp.wait_ge(S["stored"], IT * 16)

                @block.scalar
                def _(act):
                    def body(i):
                        mixer.indices(act, i)
                        norm.deviation(act, i, 0)
                        norm.deviation(act, i, 1)
                        for u in range(TU):
                            act.wait_ge(S["turned"], i * TU + u + 1)
                            nc.scalar.activation(nT[:, u, :, :].rearrange("p k n -> p (k n)"), ps[:, u, 0:D], ACT.Copy).then_inc(S["nT_ready"], 1)
                        for u in range(TU):
                            act.wait_ge(S["dense"], i * TU + u + 1)
                            if not isinstance(i, int):
                                act.wait_ge(S["sparse"], i * TU)
                            nc.scalar.activation(HN[:, u, :], ps[:, u, D:2 * D], ACT.Copy).then_inc(S["neigh"], 1)

                    once_and_loop(act, body)

                @block.tensor
                def _(pe):
                    def body(i):
                        for u in range(TU):
                            pe.wait_ge(S["n_ready"], i * TU + u + 1)
                            if not isinstance(i, int):
                                pe.wait_ge(S["x_added"], (i - 1) * TU + u + 1)
                                pe.wait_ge(S["neigh"], (i - 1) * TU + u + 1)
                            turn2(ps[:, u, 0:D], H[:, u, :], S["turned"])
                        for u in range(TU):
                            pe.wait_ge(S["nT_ready"], i * TU + u + 1)
                            for k in range(K2):
                                last = nc.tensor.matmul(ps[:, u, :], nT[:, u, k, :], w_dense[:, k, :], start=(k == 0), stop=(k == K2 - 1))
                            last.then_inc(S["dense"], 1)

                    once_and_loop(pe, body)

                @block.vector
                def _(dve):
                    def body(i):
                        for u in range(TU):
                            if not isinstance(i, int):
                                dve.wait_ge(S["dense"], (i - 1) * TU + u + 1)
                            mixer.mix(dve, i, u, H[:, u, :], tile_of(NR, i * TU + u))
                            norm.take(dve, i, 0, u, H[:, u, :])
                        norm.factors(dve, i, 0, 1e-5)
                        for u in range(TU):
                            norm.apply(H[:, u, :], H[:, u, :], u).then_inc(S["znorm"], 1)
                        for u in range(TU):
                            n = i * TU + u + 1
                            xt = tile_of(X, i * TU + u)
                            dve.wait_ge(S["z_ready"], n)
                            nc.vector.tensor_tensor(xt, xt, H[:, u, :], ALU.add).then_inc(S["x_ready"], 1)
                            hold(dve, "dve", S["x_ready"], n)
                            norm.take(dve, i, 1, u, xt)
                        norm.factors(dve, i, 1, 1e-5)
                        for u in range(TU):
                            norm.apply(H[:, u, :], tile_of(X, i * TU + u), u).then_inc(S["n_ready"], 1)
                        for u in range(TU):
                            n = i * TU + u + 1
                            xt = tile_of(X, i * TU + u)
                            dve.wait_ge(S["neigh"], n)
                            nc.vector.tensor_tensor(xt, xt, ps[:, u, 0:D], ALU.add).then_inc(S["x_added"], 1)
                        if not isinstance(i, int):
                            hold(dve, "dve", S["stored"], i * 16)
                        for r in range(4):
                            for u in range(TU):
                                n = (i * 4 + r) * TU + u + 1
                                src = HN[:, u, :] if r == 0 else WK[:, u, :]
                                if r == 0:
                                    hold(dve, "dve", S["neigh"], i * TU + u + 1)
                                else:
                                    hold(dve, "dve", S["replaced"], n - TU)
                                nc.vector.max(v8[:, u, :], src).then_inc(S["max8"], 1)
                                hold(dve, "dve", S["max8"], n)
                                nc.vector.match_replace(WK[:, u, :], v8[:, u, :], src, BIG).then_inc(S["replaced"], 1)
                        for u in range(TU):
                            dve.wait_ge(S["replaced"], (i * 4 + 3) * TU + u + 1)
                            nc.vector.tensor_tensor(WK[:, u, :], WK[:, u, :], HN[:, u, :], ALU.not_equal).then_inc(S["masked"], 1)

                    once_and_loop(dve, body)

        def neighbour_means():
            with ExitStack() as c:
                lhs = sb("a1lhs", [P, TU, K2, P], F32, c)
                H = sb("a1H", [P, TU, D], F32, c)
                nT = sb("a1nT", [P, TU, K2, P], F32, c)
                LG = sb("a1LG", [P, TU, E1], F32, c)
                v8 = sb("a1v8", [P, TU, 8], F32, c)
                i8 = sb("a1i8", [P, TU, 8], U32, c)
                mx = sb("a1mx", [P, TU], F32, c)
                zs = sb("a1zs", [P, TU], F32, c)
                ps = pb("a1ps", [P, TU, 512], c)
                norm = Norm("a1", c, 1)
                S = {n: sem("A1" + n) for n in ("free", "lhs_ready", "turned", "x_ready", "n_ready", "kept", "n_turned", "nT_ready",
                                                "lg_done", "lg_ready", "mx", "less", "exp", "zs", "zi", "probs", "v8", "i8")}
                block = c.enter_context(nc.Block())

                @block.scalar
                def _(act):
                    with act.Fori(0, IT) as i:
                        act.wait_ge(S["free"], i + 1)
                        for u in range(TU):
                            nc.scalar.activation(lhs[:, u, :, :], sumT[:, 0:K2, ds((i * TU + u) * P, P)], ACT.Copy).then_inc(S["lhs_ready"], 1)
                        norm.deviation(act, i, 0)
                        for u in range(TU):
                            act.wait_ge(S["n_turned"], i * TU + u + 1)
                            nc.scalar.activation(nT[:, u, :, :].rearrange("p k n -> p (k n)"), ps[:, u, D:2 * D], ACT.Copy).then_inc(S["nT_ready"], 1)
                        act.wait_ge(S["less"], i + 1)
                        nc.scalar.activation(LG[:], LG[:], ACT.Exp).then_inc(S["exp"], 1)

                @block.tensor
                def _(pe):
                    with pe.Fori(0, IT) as i:
                        for u in range(TU):
                            pe.wait_ge(S["lhs_ready"], i * TU + u + 1)
                            for k in range(K2):
                                last = nc.tensor.transpose(ps[:, u, k * P:(k + 1) * P], lhs[:, u, k, :], ident[:])
                            last.then_inc(S["turned"], 1)
                        for u in range(TU):
                            pe.wait_ge(S["n_ready"], i * TU + u + 1)
                            turn2(ps[:, u, D:2 * D], H[:, u, :], S["n_turned"])
                        for u in range(TU):
                            pe.wait_ge(S["nT_ready"], i * TU + u + 1)
                            for k in range(K2):
                                last = nc.tensor.matmul(ps[:, u, 0:E1], nT[:, u, k, :], gate_w1[:, k, :], start=(k == 0), stop=(k == K2 - 1))
                            last.then_inc(S["lg_done"], 1)

                @block.vector
                def _(dve):
                    dve.sem_inc(S["free"], 1)
                    with dve.Fori(0, IT) as i:
                        for u in range(TU):
                            n = i * TU + u + 1
                            xt = tile_of(X, i * TU + u)
                            dve.wait_ge(S["turned"], n)
                            nc.vector.scalar_tensor_tensor(xt, ps[:, u, 0:D], deg_inv[:, ds(i * TU + u, 1)], xt, ALU.mult, ALU.add).then_inc(S["x_ready"], 1)
                            hold(dve, "dve", S["x_ready"], n)
                            norm.take(dve, i, 0, u, xt)
                        norm.factors(dve, i, 0, 1e-5)
                        for u in range(TU):
                            norm.apply(H[:, u, :], tile_of(X, i * TU + u), u).then_inc(S["n_ready"], 1)
                        hold(dve, "dve", S["n_ready"], (i + 1) * TU)
                        nc.vector.tensor_copy(NR[:, ds(i * TU, TU), :], H[:]).then_inc(S["kept"], 1)
                        for u in range(TU):
                            dve.wait_ge(S["lg_done"], i * TU + u + 1)
                            nc.vector.tensor_copy(LG[:, u, :], ps[:, u, 0:E1]).then_inc(S["lg_ready"], 1)
                        dve.wait_ge(S["lg_ready"], (i + 1) * TU)
                        nc.vector.tensor_reduce(mx[:], LG[:], AX_X, ALU.max).then_inc(S["mx"], 1)
                        dve.wait_ge(S["mx"], i + 1)
                        nc.vector.tensor_tensor(LG[:], LG[:], mx[:].unsqueeze(2).to_broadcast([P, TU, E1]), ALU.subtract).then_inc(S["less"], 1)
                        dve.wait_ge(S["exp"], i + 1)
                        nc.vector.tensor_reduce(zs[:], LG[:], AX_X, ALU.add).then_inc(S["zs"], 1)
                        dve.wait_ge(S["zs"], i + 1)
                        nc.vector.reciprocal(zs[:], zs[:]).then_inc(S["zi"], 1)
                        dve.wait_ge(S["zi"], i + 1)
                        nc.vector.tensor_tensor(LG[:], LG[:], zs[:].unsqueeze(2).to_broadcast([P, TU, E1]), ALU.mult).then_inc(S["probs"], 1)
                        hold(dve, "dve", S["probs"], i + 1)
                        for u in range(TU):
                            n = i * TU + u + 1
                            nc.vector.max(v8[:, u, :], LG[:, u, :]).then_inc(S["v8"], 1)
                            hold(dve, "dve", S["v8"], n)
                            nc.vector.max_index(i8[:, u, :], v8[:, u, :], LG[:, u, :]).then_inc(S["i8"], 1)
                        hold(dve, "dve", S["i8"], (i + 1) * TU)
                        nc.vector.tensor_copy(top_val[:, ds(i * TU, TU), :], v8[:, :, 0:2])
                        nc.vector.tensor_copy(top_idx[:, ds(i * TU, TU), :], i8[:, :, 0:2]).then_inc(S["free"], 1)

        def last_sums():
            with ExitStack() as c:
                H = sb("o1H", [P, TU, D], F32, c)
                mixer = Mix("o1", c, NB1)
                s_out, s_res, s_last = sem("out_stored"), sem("result_ready"), sem("last_stored")
                block = c.enter_context(nc.Block())

                @block.gpsimd
                def _(pool):
                    mixer.clear(pool)
                    once_and_loop(pool, lambda i: mixer.gathers(pool, i))

                @block.scalar
                def _(act):
                    once_and_loop(act, lambda i: mixer.indices(act, i))

                @block.vector
                def _(dve):
                    def body(i):
                        if not isinstance(i, int):
                            dve.wait_ge(s_out, i * 16)
                        for u in range(TU):
                            t = i * TU + u
                            mixer.mix(dve, i, u, H[:, u, :], tile_of(NR, t))
                            nc.vector.tensor_tensor(H[:, u, :], H[:, u, :], tile_of(X, t), ALU.add).then_inc(s_res, 1)

                    once_and_loop(dve, body)

                @block.sync
                def _(sp):
                    def rows(i):
                        return out[ds(i * TU * P, TU * P), :].rearrange("(u p) d -> p u d", p=P)

                    with sp.Fori(0, IT - 1) as i:
                        sp.wait_ge(s_res, (i + 1) * TU)
                        sp.dma_start(rows(i), H[:]).then_inc(s_out, 16)
                    sp.wait_ge(s_res, T)
                    at = (T - TU) * P
                    sp.dma_start(out[at:at + (TU - 1) * P, :].rearrange("(u p) d -> p u d", p=P), H[:, 0:TU - 1, :]).then_inc(s_last, 16)
                    sp.dma_start(out[(T - 1) * P:N, :], H[0:LAST, TU - 1, :]).then_inc(s_last, 16)
                    sp.wait_ge(s_out, (IT - 1) * 16)
                    sp.wait_ge(s_last, 32)

        def show_x():
            with ExitStack() as c:
                s_o = sem("dbgx")
                block = c.enter_context(nc.Block())

                @block.sync
                def _(sp):
                    sp.dma_start(out[0:(T - 1) * P, :].rearrange("(t p) d -> p t d", p=P), X[:, 0:T - 1, :]).then_inc(s_o, 16)
                    sp.dma_start(out[(T - 1) * P:N, :], X[0:LAST, T - 1, :]).then_inc(s_o, 16)
                    sp.wait_ge(s_o, 32)

        end_step()
        if debug == "x1":
            return show_x()
        route("r0", E0, NB0, True)
        end_step()
        experts("e0", E0, F0, NB0, a["L0_ffn_w1"], b1_cols0, a["L0_ffn_w2"], a["L0_ffn_b2"], ACT.Relu)
        end_step()
        sparse_products()
        end_step()
        if debug == "x2":
            return show_x()
        segment_sums("L1_", n_dram, False)
        end_step()
        neighbour_means()
        end_step()
        if debug == "x3":
            return show_x()
        route("r1", E1, NB1, False)
        end_step()
        experts("e1", E1, F1, NB1, a["L1_ffn_w1"], b1_cols1, a["L1_ffn_w2"], a["L1_ffn_b2"], ACT.Gelu)
        end_step()
        last_sums()


def kernel(**inputs):
    import numpy as _np
    import concourse.bacc as _bacc
    from concourse import mybir as _mybir
    from concourse.bass_utils import run_bass_kernel_spmd as _run

    nc = _bacc.Bacc("TRN2", target_bir_lowering=False, num_devices=1)
    arrays, args = {}, {}
    for name in inputs:
        v = _np.ascontiguousarray(inputs[name])
        arrays[f"in_{name}"] = v
        args[name] = nc.dram_tensor(f"in_{name}", v.shape, _mybir.dt.from_np(v.dtype), kind="ExternalInput").ap()
    shape = DBG_SHAPE or inputs["x"].shape
    out = nc.dram_tensor("out", shape, _mybir.dt.from_np(_np.dtype("float32")), kind="ExternalOutput").ap()
    build(nc, args, out, DEBUG)
    r = _run(nc, [arrays], core_ids=[0])
    return r.results[0]["out"]


DEBUG, DBG_SHAPE = None, None
```

```python
from contextlib import ExitStack

import numpy as np
import concourse.bass as bass
from concourse import mybir

P = 128
F32 = mybir.dt.float32
I32 = mybir.dt.int32
U32 = mybir.dt.uint32
ALU = mybir.AluOpType
ACT = mybir.ActivationFunctionType
AX_X = mybir.AxisListType.X
ds = bass.ds

TU = 5
GC = 4
GU = 7
BU = 4
FAR = 1.0e6


def build(nc, a, out, debug=None):
    N, D = a["x"].shape
    E_N, DE = a["edge_attr_64"].shape
    T = -(-N // P)
    NPAD = T * P
    LAST = N - (T - 1) * P
    IT = T // TU
    assert IT * TU == T and D == 256
    GE = GC * P
    NG = -(-E_N // GE)
    GI = NG // GU
    assert GI * GU == NG and NG <= P
    E_LAST = E_N - (NG - 1) * GE
    P_LAST = E_LAST // GC
    assert P_LAST * GC == E_LAST
    WIN = NPAD + P
    K2 = D // P

    E0, _, F0 = a["L0_ffn_w1"].shape
    E1, _, F1 = a["L1_ffn_w1"].shape

    def n_blocks(experts):
        most = 2 * N // P + experts
        return -(-most // BU) * BU

    NB0, NB1 = n_blocks(E0), n_blocks(E1)
    XS_ROWS = max(NB0, NB1) * P

    n_dram = nc.dram_tensor("n_rows", [NPAD, D], F32, kind="Internal").ap()
    hs_dram = nc.dram_tensor("sparse_rows", [NPAD, D], F32, kind="Internal").ap()
    ys_dram = nc.dram_tensor("expert_out", [XS_ROWS, D], F32, kind="Internal").ap()

    with ExitStack() as ctx:
        def sb(name, shape, dt=F32, c=ctx):
            return c.enter_context(nc.sbuf_tensor(name, shape, dt))

        def pb(name, shape, c=ctx):
            return c.enter_context(nc.psum_tensor(name, shape, F32))

        step_sems = []

        def sem(name):
            step_sems.append(nc.alloc_semaphore(name=name))
            return step_sems[-1]

        def held_sem(name):
            return ctx.enter_context(nc.semaphore(name))

        def end_step():
            nc.clear_and_free_semaphores(step_sems)
            step_sems.clear()
            nc.all_engine_barrier()

        carried = {e: held_sem(e + "_carried") for e in ("dve", "pool", "pe")}

        def hold(eng, name, semaphore, value):
            eng.wait_ge(semaphore, value)
            eng.sem_inc(carried[name], 1)

        X = sb("X", [P, T, D])
        NR = sb("NR", [P, T, D])
        sumT = sb("sumT", [P, 3, WIN])
        ident = sb("ident", [P, P])
        ones = sb("ones", [P, P])
        before = sb("before", [P, P])
        iota_w = sb("iota_w", [P, P])
        win_off = sb("win_off", [P, T])
        row_far = sb("row_far", [P, T])
        src_tab = sb("src_tab", [P, NG, GC], I32)
        rel_tab = sb("rel_tab", [P, NG + 1, GC])
        base_row = sb("base_row", [1, NG], I32)
        wide_flag = sb("wide_flag", [1, 1], I32)
        deg_inv = sb("deg_inv", [P, T])
        row_1 = sb("row_1", [P, T])
        logit0 = sb("logit0", [P, T, E0])
        logit1 = sb("logit1", [P, T, E1])
        token = sb("token", [P, max(NB0, NB1)], I32)
        eps5 = sb("eps5", [P, 1])
        eps6 = sb("eps6", [P, 1])
        top_w = sb("top_w", [P, T, 2])
        slot = sb("slot", [P, T, 2], I32)
        block_expert = sb("block_expert", [1, max(NB0, NB1)], I32)

        w_nodes = sb("w_nodes", [P, K2, D])
        w_edges = sb("w_edges", [DE, D])
        w_mlp = sb("w_mlp", [P, 3, K2, D])
        b_mlp = sb("b_mlp", [P, 3, K2])
        ln_rows = sb("ln_rows", [P, 4, D])
        gate_w0 = sb("gate_w0", [P, K2, E0])
        gate_b0 = sb("gate_b0", [P, E0])
        gate_w1 = sb("gate_w1", [P, K2, E1])
        router_rows = sb("router_rows", [E1, D])
        w_dense = sb("w_dense", [P, K2, 2 * D])
        FJ0, FJ1 = F0 // P, F1 // P
        b1_cols0 = sb("b1_cols0", [P, E0 * FJ0])
        b1_cols1 = sb("b1_cols1", [P, E1 * FJ1])
        aggr_cols = sb("aggr_cols", [P, 2, K2])
        s_w = held_sem("weights_loaded")
        N_LOADS = 21
        LN_NAMES = ["L0_gnn_ln_out_scale", "L0_gnn_ln_out_bias",
                    "L0_ffn_gamma", "L0_ffn_beta"]
        OUT_S, OUT_B, FFN_S, FFN_B = (ln_rows[:, k, :] for k in range(4))

        with ExitStack() as c1:
            srci = sb("srci", [NG, GE], I32, c1)
            dsti = sb("dsti", [NG, GE], I32, c1)
            srcf = sb("srcf", [NG, GE], F32, c1)
            dstf = sb("dstf", [NG, GE], F32, c1)
            dlow = sb("dlow", [NG, GE], F32, c1)
            ends = sb("ends", [NG, 2], F32, c1)
            endr = sb("endr", [1, 2, NG], F32, c1)
            rowid = sb("rowid", [P, T], I32, c1)
            iota_i = sb("iota_i", [P, P], I32, c1)
            offi = sb("offi", [P, T], I32, c1)
            st = sb("st", [P, T, 6], F32, c1)
            mv = sb("mv", [P, T, 2], F32, c1)
            rs = sb("rs", [P, T], F32, c1)
            b1r0 = sb("b1r0", [E0 * FJ0, P], F32, c1)
            b1r1 = sb("b1r1", [E1 * FJ1, P], F32, c1)
            bmr = sb("bmr", [5 * K2, P], F32, c1)
            ps_w = pb("ps_w", [P, 512], c1)
            ps_t = pb("ps_t", [P, GC, P], c1)
            ps_u = pb("ps_u", [P, GC, P], c1)
            ps_e = pb("ps_e", [P, 512], c1)
            ps_b = pb("ps_b", [P, 512], c1)

            s_x, s_edges, s_n = sem("x_loaded"), sem("edges_loaded"), sem("norm_stored")
            s_pad, s_cst, s_pc = sem("pads_set"), sem("consts_set"), sem("pool_chain")
            s_f, s_tr, s_end, s_rowp, s_row, s_bb, s_dv = (sem("edges_float"), sem("edges_transposed"), sem("ends_found"),
                                                           sem("ends_transposed"), sem("base_row_ready"), sem("base_broadcast"), sem("dve_chain"))
            s_wt = sem("weights_turned")
            s_sq, s_rs = sem("deviation"), sem("deviation_inverse")
            block = c1.enter_context(nc.Block())

            @block.sync
            def _(sp):
                sp.wait_ge(s_pad, 1)
                sp.dma_start(X[:, 0:T - 1, :], a["x"][0:(T - 1) * P, :].rearrange("(t p) d -> p t d", p=P)).then_inc(s_x, 16)
                sp.dma_start(X[0:LAST, T - 1, :], a["x"][(T - 1) * P:N, :]).then_inc(s_x, 16)
                for tab, name in ((srci, "src"), (dsti, "dst")):
                    sp.dma_start(tab[0:NG - 1, :], a[name][0:(NG - 1) * GE].rearrange("(g e) -> g e", e=GE)).then_inc(s_edges, 16)
                    sp.dma_start(tab[NG - 1:NG, 0:E_LAST], a[name][(NG - 1) * GE:E_N].rearrange("(a e) -> a e", a=1)).then_inc(s_edges, 16)
                sp.wait_ge(s_dv, 6)
                sp.dma_start(n_dram.rearrange("(t p) d -> p t d", p=P), NR[:]).then_inc(s_n, 16)
                sp.wait_ge(s_n, 16)

            @block.gpsimd
            def _(pool):
                nc.gpsimd.memset(X[:, T - 1, :], 0.0)
                nc.gpsimd.memset(srci[:], 0)
                nc.gpsimd.memset(dsti[:], -1).then_inc(s_pad, 1)
                nc.gpsimd.memset(eps5[:], 1e-5)
                nc.gpsimd.memset(eps6[:], 1e-6)
                nc.gpsimd.memset(ident[:], 0.0)
                nc.gpsimd.memset(ones[:], 1.0)
                nc.gpsimd.memset(before[:], 1.0)
                nc.gpsimd.iota(iota_i[:], [[1, P]], base=0, channel_multiplier=0)
                nc.gpsimd.iota(offi[:], [[P, T]], base=0, channel_multiplier=0)
                nc.gpsimd.iota(rowid[:], [[P, T]], base=0, channel_multiplier=1)
                nc.gpsimd.memset(rel_tab[:], -1.0).then_inc(s_pc, 1)
                pool.wait_ge(s_pc, 1)
                nc.gpsimd.affine_select(out=ident[:], in_=ident[:], compare_op=ALU.not_equal, fill=1.0,
                                        base=0, pattern=[[-1, P]], channel_multiplier=1)
                nc.gpsimd.affine_select(out=before[:], in_=before[:], compare_op=ALU.is_gt, fill=0.0,
                                        base=0, pattern=[[1, P]], channel_multiplier=-1)
                nc.gpsimd.tensor_copy(iota_w[:], iota_i[:])
                nc.gpsimd.tensor_copy(win_off[:], offi[:])
                nc.gpsimd.tensor_scalar(row_1[:], rowid[:], 1.0, None, ALU.add)
                nc.gpsimd.tensor_scalar(row_far[:], rowid[:], float(N), FAR, ALU.is_ge, ALU.mult).then_inc(s_cst, 1)
                nc.gpsimd.memset(sumT[:], 0.0)

            @block.scalar
            def _(act):
                loads = [(w_nodes[:], a["L0_gnn_W_message"][0:D, :].rearrange("(k p) n -> p k n", p=P)),
                         (w_edges[:], a["L0_gnn_W_message"][D:D + DE, :]),
                         (gate_w0[:], a["L0_ffn_gate_w"].rearrange("(k p) n -> p k n", p=P)),
                         (gate_b0[:], a["L0_ffn_gate_b"].rearrange("(a n) -> a n", a=1).to_broadcast([P, E0])),
                         (router_rows[:], a["L1_ffn_router_w"]),
                         (w_dense[:, :, 0:D], a["L1_gnn_W_self"].rearrange("(k p) n -> p k n", p=P)),
                         (w_dense[:, :, D:2 * D], a["L1_gnn_W_neigh"].rearrange("(k p) n -> p k n", p=P)),
                         (b1r0[:], a["L0_ffn_b1"].rearrange("e (j p) -> (e j) p", p=P)),
                         (b1r1[:], a["L1_ffn_b1"].rearrange("e (j p) -> (e j) p", p=P)),
                         (bmr[3 * K2:4 * K2, :], a["L0_gnn_ln_aggr_scale"].rearrange("(k p) -> k p", p=P)),
                         (bmr[4 * K2:5 * K2, :], a["L0_gnn_ln_aggr_bias"].rearrange("(k p) -> k p", p=P))]
                for l in range(3):
                    loads.append((w_mlp[:, l, :, :], a[f"L0_gnn_mlp_W{l}"].rearrange("(k p) n -> p k n", p=P)))
                    loads.append((bmr[K2 * l:K2 * l + K2, :], a[f"L0_gnn_mlp_b{l}"].rearrange("(k p) -> k p", p=P)))
                for k, name in enumerate(LN_NAMES):
                    loads.append((ln_rows[:, k, :], a[name].rearrange("(a n) -> a n", a=1).to_broadcast([P, D])))
                for to, src in loads:
                    act.dma_start(to, src).then_inc(s_w, 16)
                assert len(loads) == N_LOADS
                act.wait_ge(s_edges, 64)
                nc.scalar.activation(srcf[:], srci[:], ACT.Copy).then_inc(s_f, 1)
                act.wait_ge(s_dv, 4)
                nc.scalar.activation(rs[:], rs[:], ACT.Sqrt).then_inc(s_sq, 1)

            @block.tensor
            def _(pe):
                pe.wait_ge(s_cst, 1)
                pe.wait_ge(s_f, 1)
                pe.wait_ge(s_dv, 1)
                for c in range(GC):
                    nc.tensor.transpose(ps_t[:, c, 0:NG], srcf[:, c::GC], ident[0:NG, 0:NG])
                for c in range(GC):
                    last = nc.tensor.transpose(ps_u[:, c, 0:NG], dstf[:, c::GC], ident[0:NG, 0:NG])
                last.then_inc(s_tr, 1)
                pe.wait_ge(s_end, 1)
                for c in range(2):
                    last = nc.tensor.matmul(ps_e[0:1, c * P:c * P + NG], ends[:, c:c + 1], ident[0:NG, 0:NG], start=True, stop=True)
                last.then_inc(s_rowp, 1)
                pe.wait_ge(s_row, 1)
                nc.tensor.matmul(ps_b[:, 0:NG], ones[0:1, :], endr[0:1, 0, :], start=True, stop=True).then_inc(s_bb, 1)
                pe.wait_ge(s_w, 16 * N_LOADS)
                at = 0
                for rows in (b1r0[:], b1r1[:], bmr[:], router_rows[:, 0:P], router_rows[:, P:D]):
                    n = rows.shape[0]
                    last = nc.tensor.transpose(ps_w[:, at:at + n], rows, ident[0:n, 0:n])
                    at += n
                last.then_inc(s_wt, 1)

            @block.vector
            def _(dve):
                dve.wait_ge(s_edges, 64)
                nc.vector.tensor_copy(dstf[:], dsti[:]).then_inc(s_dv, 1)
                dve.wait_ge(s_x, 32)
                for t in range(T):
                    last = nc.vector.bn_stats(st[:, t, :], X[:, t, :])
                last.then_inc(s_dv, 1)
                dve.wait_ge(s_dv, 2)
                for t in range(T):
                    last = nc.vector.bn_aggr(mv[:, t, :], st[:, t, :])
                last.then_inc(s_dv, 1)
                dve.wait_ge(s_dv, 3)
                nc.vector.tensor_scalar(rs[:], mv[:, :, 1], 1e-5, None, ALU.add).then_inc(s_dv, 1)
                nc.vector.tensor_scalar(dlow[:], dstf[:], 0.0, FAR, ALU.is_lt, ALU.mult).then_inc(s_dv, 1)
                dve.wait_ge(s_sq, 1)
                nc.vector.reciprocal(rs[:], rs[:]).then_inc(s_rs, 1)
                dve.wait_ge(s_rs, 1)
                for t in range(T):
                    last = nc.vector.tensor_scalar(NR[:, t, :], X[:, t, :], mv[:, t, 0:1], rs[:, t:t + 1], ALU.subtract, ALU.mult)
                last.then_inc(s_dv, 1)
                nc.vector.tensor_tensor(dlow[:], dlow[:], dstf[:], ALU.add).then_inc(s_dv, 1)
                dve.wait_ge(s_dv, 7)
                nc.vector.tensor_reduce(ends[:, 0:1], dlow[:], AX_X, ALU.min)
                nc.vector.tensor_reduce(ends[:, 1:2], dstf[:], AX_X, ALU.max).then_inc(s_dv, 1)
                dve.wait_ge(s_dv, 8)
                nc.vector.tensor_scalar(ends[:, 0:1], ends[:, 0:1], float(NPAD), None, ALU.min).then_inc(s_dv, 1)
                dve.wait_ge(s_dv, 9)
                nc.vector.tensor_tensor(ends[:, 1:2], ends[:, 1:2], ends[:, 0:1], ALU.subtract).then_inc(s_end, 1)
                dve.wait_ge(s_tr, 1)
                nc.vector.tensor_copy(src_tab[:].rearrange("p g c -> p c g"), ps_t[:, :, 0:NG])
                dve.wait_ge(s_rowp, 1)
                nc.vector.tensor_copy(endr[:], ps_e[0:1, 0:2 * P].rearrange("p (c g) -> p c g", c=2)[:, :, 0:NG]).then_inc(s_row, 1)
                dve.wait_ge(s_row, 1)
                nc.vector.tensor_copy(base_row[:], endr[0:1, 0, :])
                nc.vector.tensor_reduce(endr[0:1, 1, 0:1], endr[0:1, 1, :], AX_X, ALU.max).then_inc(s_dv, 1)
                dve.wait_ge(s_dv, 10)
                nc.vector.tensor_scalar(wide_flag[:], endr[0:1, 1, 0:1], float(P), None, ALU.is_ge)
                dve.wait_ge(s_bb, 1)
                dve.wait_ge(s_pc, 1)
                nc.vector.tensor_copy(rel_tab[:, 0:NG, :].rearrange("p g c -> p c g"), ps_u[:, :, 0:NG]).then_inc(s_dv, 1)
                dve.wait_ge(s_dv, 11)
                nc.vector.tensor_tensor(rel_tab[:, 0:NG, :], rel_tab[:, 0:NG, :],
                                        ps_b[:, 0:NG].unsqueeze(2).to_broadcast([P, NG, GC]), ALU.subtract).then_inc(s_dv, 1)
                dve.wait_ge(s_wt, 1)
                at = 0
                for to in (b1_cols0[:], b1_cols1[:], b_mlp[:].rearrange("p l k -> p (l k)"), aggr_cols[:].rearrange("p l k -> p (l k)"), gate_w1[:, 0, :], gate_w1[:, 1, :]):
                    n = to.shape[1]
                    nc.vector.tensor_copy(to, ps_w[:, at:at + n])
                    at += n

        def segment_sums(tag, rows_dram, with_edges):
            halves = 3 if with_edges else 2
            with ExitStack() as c:
                G = sb(tag + "G", [P, GU, GC, D], F32, c)
                EA = sb(tag + "EA", [P, GU, GC, P], F32, c) if with_edges else None
                OH = sb(tag + "OH", [P, GU, GC, P], F32, c)
                idx = sb(tag + "idx", [P, GU, GC], I32, c)
                rel_s = sb(tag + "rel_s", [P, GC], F32, c)
                wbase = sb(tag + "wbase", [1, 1], I32, c)
                ps = pb(tag + "ps", [P, GU, 512], c)
                gathered = [held_sem(f"{tag}gathered{s}") for s in range(GU)]
                edges_in = [sem(f"{tag}edges_in{s}") for s in range(GU)]
                idx_ready, hot_ready, summed, added = (sem(tag + "idx_ready"), sem(tag + "hot_ready"),
                                                       sem(tag + "summed"), sem(tag + "added"))
                ones_set = sem(tag + "ones_set")
                w_idx, w_gath, w_edge, w_hot, w_sum, w_turn, w_rel = (sem(tag + "wide_idx"), held_sem(tag + "wide_gathered"), sem(tag + "wide_edges"),
                                                                     sem(tag + "wide_hot"), sem(tag + "wide_summed"), sem(tag + "wide_turn"), sem(tag + "wide_rel"))
                w_free = sem(tag + "wide_free")
                block = c.enter_context(nc.Block())

                def edge_rows(g):
                    return a["edge_attr_64"][ds(g * GE, GE), :].rearrange("(p c) f -> p c f", c=GC)

                edge_rows_last = a["edge_attr_64"][(NG - 1) * GE:E_N, :].rearrange("(p c) f -> p c f", c=GC)

                def in_loops(eng, body):
                    body(0, True)
                    with eng.Fori(1, GI) as i:
                        body(i, False)

                def wide_groups(eng, group, window=None):
                    with eng.If(eng.value_load(wide_flag[0:1, 0:1], min_val=0, max_val=1) > 0):
                        with eng.Fori(0, NG) as g:
                            group(g)
                            if window:
                                with eng.Fori(1, T) as w:
                                    window(g, w, g * (T - 1) + w)

                if with_edges:
                    @block.sync
                    def _(sp):
                        def body(i, first, last=False):
                            for s in range(GU):
                                if not first:
                                    sp.wait_ge(summed, i * GU + s + 1 - GU)
                                if last and s == GU - 1:
                                    sp.dma_start(EA[0:P_LAST, s, :, 0:DE], edge_rows_last).then_inc(edges_in[s], 16)
                                else:
                                    sp.dma_start(EA[:, s, :, 0:DE], edge_rows(i * GU + s)).then_inc(edges_in[s], 16)

                        body(0, True)
                        with sp.Fori(1, GI - 1) as i:
                            body(i, False)
                        body(GI - 1, False, True)

                        with sp.If(sp.value_load(wide_flag[0:1, 0:1], min_val=0, max_val=1) > 0):
                            sp.wait_ge(summed, NG)
                            sp.dma_start(EA[:, 0, :, 0:DE], edge_rows(0)).then_inc(w_edge, 16)
                            with sp.Fori(1, NG - 1) as g:
                                sp.wait_ge(w_sum, g * (T - 1))
                                sp.dma_start(EA[:, 0, :, 0:DE], edge_rows(g)).then_inc(w_edge, 16)
                            sp.wait_ge(w_sum, (NG - 1) * (T - 1))
                            sp.dma_start(EA[0:P_LAST, 0, :, 0:DE], edge_rows_last).then_inc(w_edge, 16)

                @block.gpsimd
                def _(pool):
                    def body(i, first):
                        for s in range(GU):
                            hold(pool, "pool", idx_ready, i * GU + s + 1)
                            for k in range(GC):
                                pool.indirect_dma_start(out=G[:, s, k, :], out_offset=None, in_=rows_dram,
                                                        in_offset=bass.IndirectOffsetOnAxis(ap=idx[:, s, k:k + 1], axis=0)
                                                        ).then_inc(gathered[s], 16)

                    in_loops(pool, body)

                    def wide(g):
                        hold(pool, "pool", w_idx, g + 1)
                        for k in range(GC):
                            pool.indirect_dma_start(out=G[:, 0, k, :], out_offset=None, in_=rows_dram,
                                                    in_offset=bass.IndirectOffsetOnAxis(ap=idx[:, 0, k:k + 1], axis=0)
                                                    ).then_inc(w_gath, 16)

                    wide_groups(pool, wide)

                @block.scalar
                def _(act):
                    def body(i, first):
                        for s in range(GU):
                            if not first:
                                act.wait_ge(summed, i * GU + s + 1 - GU)
                            nc.scalar.activation(idx[:, s, :], src_tab[:, ds(i * GU + s, 1), :].rearrange("p a c -> p (a c)"),
                                                 ACT.Copy).then_inc(idx_ready, 1)

                    in_loops(act, body)

                    def wide(g):
                        act.wait_ge(w_free, g + 1)
                        nc.scalar.activation(idx[:, 0, :], src_tab[:, ds(g, 1), :].rearrange("p a c -> p (a c)"),
                                             ACT.Copy).then_inc(w_idx, 1)

                    wide_groups(act, wide)

                def products(pe, s):
                    for h in range(halves):
                        for k in range(GC):
                            rows = EA[:, s, k, :] if h == 2 else G[:, s, k, h * P:(h + 1) * P]
                            last = nc.tensor.matmul(ps[:, s, h * P:(h + 1) * P], rows, OH[:, s, k, :],
                                                    start=(k == 0), stop=(k == GC - 1))
                    return last

                @block.tensor
                def _(pe):
                    if with_edges:
                        pe.wait_ge(ones_set, 1)

                    def body(i, first):
                        for s in range(GU):
                            pe.wait_ge(hot_ready, i * GU + s + 1)
                            if with_edges:
                                pe.wait_ge(edges_in[s], (i + 1) * 16)
                            pe.wait_ge(gathered[s], (i + 1) * 16 * GC)
                            if not first:
                                pe.wait_ge(added, i * GU + s + 1 - GU)
                            products(pe, s).then_inc(summed, 1)

                    in_loops(pe, body)

                    def wide(g):
                        if with_edges:
                            pe.wait_ge(w_edge, (g + 1) * 16)
                        hold(pe, "pe", w_gath, (g + 1) * 16 * GC)

                    def window(g, w, n):
                        pe.wait_ge(w_hot, n)
                        products(pe, 0).then_inc(w_sum, 1)

                    wide_groups(pe, wide, window)

                @block.vector
                def _(dve):
                    iota_b = iota_w[:].unsqueeze(1).to_broadcast([P, GC, P])

                    def hot(g, s):
                        return nc.vector.tensor_tensor(
                            OH[:, s, :, :], iota_b,
                            rel_tab[:, ds(g, 1), :].rearrange("p a c -> p (a c)").unsqueeze(2).to_broadcast([P, GC, P]), ALU.is_equal)

                    def add(base, s):
                        window = sumT[:, 0:halves, ds(base, P)]
                        return nc.vector.tensor_tensor(window, window,
                                                       ps[:, s, 0:halves * P].rearrange("p (h w) -> p h w", h=halves), ALU.add)

                    def body(i, first):
                        for s in range(GU):
                            if not (first and s < GU - 1):
                                dve.wait_ge(summed, i * GU + s + 2 - GU)
                            hot(i * GU + s + 1, (s + 1) % GU).then_inc(hot_ready, 1)
                            base = dve.value_load(base_row[0:1, ds(i * GU + s, 1)], min_val=0, max_val=NPAD)
                            dve.wait_ge(summed, i * GU + s + 1)
                            if not (first and s == 0):
                                dve.wait_ge(added, i * GU + s)
                            add(base, s).then_inc(added, 1)

                    hot(0, 0).then_inc(hot_ready, 1)
                    if with_edges:
                        nc.vector.memset(EA[:, :, :, DE:P], 1.0).then_inc(ones_set, 1)
                    in_loops(dve, body)

                    def wide(g):
                        dve.sem_inc(w_free, 1)

                    def window(g, w, n):
                        dve.wait_ge(w_turn, n)
                        rel_g = rel_tab[:, ds(g, 1), :].rearrange("p a c -> p (a c)")
                        nc.vector.tensor_scalar(rel_s[:], rel_g, win_off[:, ds(w, 1)], None, ALU.subtract)
                        nc.vector.tensor_scalar(wbase[:], base_row[0:1, ds(g, 1)], win_off[0:1, ds(w, 1)], float(NPAD),
                                                ALU.add, ALU.min).then_inc(w_rel, 1)
                        dve.wait_ge(w_rel, n)
                        nc.vector.tensor_tensor(OH[:, 0, :, :], iota_b, rel_s[:].unsqueeze(2).to_broadcast([P, GC, P]),
                                                ALU.is_equal).then_inc(w_hot, 1)
                        base = dve.value_load(wbase[0:1, 0:1], min_val=0, max_val=NPAD)
                        dve.wait_ge(w_sum, n)
                        add(base, 0).then_inc(w_turn, 1)

                    dve.wait_ge(added, NG)
                    dve.wait_ge(hot_ready, NG + 1)
                    dve.sem_inc(w_turn, 1)
                    wide_groups(dve, wide, window)

        end_step()
        segment_sums("L0_", n_dram, True)
        end_step()
        if debug == "sums":
            with ExitStack() as c:
                s_o = sem("dbg")
                block = c.enter_context(nc.Block())

                @block.sync
                def _(sp):
                    sp.dma_start(out.rearrange("h p w -> p h w"), sumT[:, :, 0:N]).then_inc(s_o, 16)
                    sp.wait_ge(s_o, 16)
            return

        def tile_of(t3, t):
            return t3[:, ds(t, 1), :].rearrange("p a d -> p (a d)")

        def rows_of(dram, t):
            return dram[ds(t * P, P), :]

        def turn2(ps_cols, rows, ready):
            for k in range(K2):
                last = nc.tensor.transpose(ps_cols[:, k * P:(k + 1) * P], rows[:, k * P:(k + 1) * P], ident[:])
            last.then_inc(ready, 1)

        def tile_steps(eng, step, most):
            def turn(i, u):
                def at(lag, with_round=False):
                    t = i * TU + u - lag
                    if isinstance(t, int) and not 0 <= t < T:
                        return None
                    return (t, (u - lag) % TU, i + (u - lag) // TU) if with_round else (t, (u - lag) % TU)
                step(at)

            for u in range(TU):
                turn(0, u)
            with eng.Fori(1, IT) as i:
                for u in range(TU):
                    turn(i, u)
            for u in range(most):
                turn(IT, u)

        def wait_tile(eng, semaphore, t, ago=0, per=1):
            n = (t + 1 - ago) * per
            if not (isinstance(n, int) and n <= 0):
                eng.wait_ge(semaphore, n)

        def hold_tile(eng, name, semaphore, t, ago=0, per=1):
            n = (t + 1 - ago) * per
            if not (isinstance(n, int) and n <= 0):
                hold(eng, name, semaphore, n)

        class Stores:

            def __init__(self, tag):
                self.free = [sem(f"{tag}slot_stored{u}") for u in range(TU)]

            def begin(self, sp):
                for u in range(TU):
                    sp.sem_inc(self.free[u], 16)

            def wait_free(self, eng, s, r):
                eng.wait_ge(self.free[s], (r + 1) * 16)

            def hold_free(self, name, eng, s, r):
                hold(eng, name, self.free[s], (r + 1) * 16)

            def store(self, sp, out, rows, s):
                sp.dma_start(out, rows).then_inc(self.free[s], 16)

            def wait_all(self, sp):
                for u in range(TU):
                    sp.wait_ge(self.free[u], (T // TU + 1) * 16)

        class Norm:

            def __init__(self, tag, c, eps):
                self.st, self.mv = sb(tag + "st", [P, TU, 6], F32, c), sb(tag + "mv", [P, TU, 2], F32, c)
                self.rs = sb(tag + "rs", [P, TU], F32, c)
                self.stats, self.joined, self.dev, self.inv = (
                    sem(tag + "stats_taken"), sem(tag + "stats_joined"), sem(tag + "deviation"), sem(tag + "deviation_inverse"))
                self.eps = eps

            def take(self, dve, t, s, rows, written):
                self.take_stats(dve, t, s, rows, written)
                self.join_stats(dve, t, s)

            def take_stats(self, dve, t, s, rows, written):
                hold_tile(dve, "dve", written, t)
                nc.vector.bn_stats(self.st[:, s, :], rows).then_inc(self.stats, 1)

            def join_stats(self, dve, t, s):
                hold_tile(dve, "dve", self.stats, t)
                nc.vector.bn_aggr(self.mv[:, s, :], self.st[:, s, :]).then_inc(self.joined, 1)

            def deviation(self, act, t, s):
                wait_tile(act, self.joined, t)
                nc.scalar.activation(self.rs[:, s:s + 1], self.mv[:, s, 1:2], ACT.Sqrt, bias=self.eps).then_inc(self.dev, 1)

            def invert(self, dve, t, s):
                wait_tile(dve, self.dev, t)
                nc.vector.reciprocal(self.rs[:, s:s + 1], self.rs[:, s:s + 1]).then_inc(self.inv, 1)
                wait_tile(dve, self.inv, t)

            def mean(self, s):
                return self.mv[:, s, 0:1]

            def inverse(self, s):
                return self.rs[:, s:s + 1]

        def node_mlp():
            with ExitStack() as c:
                lhs = sb("lhs", [P, TU, 3, P], F32, c)
                H = sb("H", [P, TU, D], F32, c)
                hT = sb("hT", [P, TU, K2, P], F32, c)
                yT = sb("yT", [P, TU, K2, P], F32, c)
                Z = sb("Z", [P, TU, D], F32, c)
                XB = sb("XB", [P, TU, D], F32, c)
                N2 = sb("N2", [P, TU, D], F32, c)
                nT = sb("nT", [P, TU, K2, P], F32, c)
                ps_agg, ps_t, ps_0, ps_1, ps_2, ps_back, ps_n, ps_g = (pb("N0ps_" + n, [P, 512], c) for n in (
                    "agg", "t", "0", "1", "2", "back", "n", "g"))
                h_norm, z_norm, x_norm = Norm("nh", c, eps6[:]), Norm("nz", c, eps6[:]), Norm("nx", c, eps5[:])
                S = {n: sem("N0" + n) for n in (
                    "lhs_ready", "agg_done", "hpre", "h_ready", "turned", "hT_ready", "first", "relu0", "added0", "second", "relu1",
                    "added1", "third", "added2", "back", "z_ready", "centred", "xb_ready", "x_ready", "n2_ready", "n_turned",
                    "nT_ready", "logits", "logits_in")}
                n_stores = Stores("N0")
                block = c.enter_context(nc.Block())

                def flat(t4, s):
                    return t4[:, s, :, :].rearrange("p k n -> p (k n)")

                @block.scalar
                def _(act):
                    def relu(l, ps_l, t, s, done):
                        for m in range(K2):
                            nc.scalar.activation(yT[:, s, m, :], ps_l[:, m * P:(m + 1) * P], ACT.Relu, bias=b_mlp[:, l, m:m + 1]).then_inc(done, 1)

                    def step(at):
                        if x := at(0):
                            t, s = x
                            wait_tile(act, S["agg_done"], t, TU)
                            nc.scalar.activation(lhs[:, s, :, :], sumT[:, :, ds(t * P, P)], ACT.Copy).then_inc(S["lhs_ready"], 1)
                        if x := at(5):
                            x_norm.deviation(act, *x)
                        if x := at(1):
                            h_norm.deviation(act, *x)
                        if x := at(2):
                            t, s = x
                            wait_tile(act, S["turned"], t)
                            for k in range(K2):
                                last = nc.scalar.activation(hT[:, s, k, :], ps_t[:, k * P:(k + 1) * P], ACT.Identity,
                                                            bias=aggr_cols[:, 1, k:k + 1], scale=aggr_cols[:, 0, k:k + 1])
                            last.then_inc(S["hT_ready"], 1)
                        if x := at(3):
                            t, s = x
                            wait_tile(act, S["second"], t)
                            relu(1, ps_1, t, s, S["relu1"])
                        if x := at(2):
                            t, s = x
                            wait_tile(act, S["first"], t)
                            relu(0, ps_0, t, s, S["relu0"])
                        if x := at(4):
                            z_norm.deviation(act, *x)
                        if x := at(5):
                            t, s = x
                            wait_tile(act, S["n_turned"], t)
                            nc.scalar.activation(flat(nT, s), ps_n[:, 0:D], ACT.Copy).then_inc(S["nT_ready"], 1)

                    tile_steps(act, step, 5)

                @block.tensor
                def _(pe):
                    def layer(l, ps_l, s, done):
                        for m in range(K2):
                            for k in range(K2):
                                last = nc.tensor.matmul(ps_l[:, m * P:(m + 1) * P], w_mlp[:, l, k, m * P:(m + 1) * P],
                                                        hT[:, s, k, :], start=(k == 0), stop=(k == K2 - 1))
                        last.then_inc(done, 1)

                    def step(at):
                        if x := at(2):
                            t, s = x
                            wait_tile(pe, S["h_ready"], t)
                            wait_tile(pe, S["hT_ready"], t, 1)
                            turn2(ps_t, H[:, s, :], S["turned"])
                        if x := at(4):
                            t, s = x
                            wait_tile(pe, S["added2"], t)
                            wait_tile(pe, S["z_ready"], t, 1)
                            for k in range(K2):
                                last = nc.tensor.transpose(ps_back[:, k * P:(k + 1) * P], hT[:, s, k, :], ident[:])
                            last.then_inc(S["back"], 1)
                        if x := at(0):
                            t, s = x
                            wait_tile(pe, S["lhs_ready"], t)
                            wait_tile(pe, S["hpre"], t, 1)
                            for k in range(K2):
                                nc.tensor.matmul(ps_agg[:, 0:D], lhs[:, s, k, :], w_nodes[:, k, :], start=(k == 0), stop=False)
                            nc.tensor.matmul(ps_agg[:, 0:D], lhs[0:DE, s, 2, :], w_edges[:], start=False, stop=True)
                            nc.tensor.matmul(ps_agg[:, D:D + 1], lhs[:, s, 2, :], ident[:, DE:DE + 1], start=True, stop=True).then_inc(S["agg_done"], 1)
                        if x := at(2):
                            t, s = x
                            wait_tile(pe, S["hT_ready"], t)
                            wait_tile(pe, S["relu0"], t, 1, K2)
                            layer(0, ps_0, s, S["first"])
                        if x := at(3):
                            t, s = x
                            wait_tile(pe, S["added1"], t)
                            wait_tile(pe, S["added2"], t, 1)
                            layer(2, ps_2, s, S["third"])
                        if x := at(5):
                            t, s = x
                            wait_tile(pe, S["n2_ready"], t)
                            wait_tile(pe, S["nT_ready"], t, 1)
                            turn2(ps_n, N2[:, s, :], S["n_turned"])
                        if x := at(5):
                            t, s = x
                            wait_tile(pe, S["nT_ready"], t)
                            wait_tile(pe, S["logits_in"], t, 1)
                            for k in range(K2):
                                last = nc.tensor.matmul(ps_g[:, 0:E0], nT[:, s, k, :], gate_w0[:, k, :], start=(k == 0), stop=(k == K2 - 1))
                            last.then_inc(S["logits"], 1)
                        if x := at(2):
                            t, s = x
                            wait_tile(pe, S["added0"], t)
                            wait_tile(pe, S["relu1"], t, 1, K2)
                            layer(1, ps_1, s, S["second"])

                    tile_steps(pe, step, 5)

                @block.gpsimd
                def _(pool):
                    def add_skip(t, s, ready, done):
                        for m in range(K2):
                            pool.wait_ge(ready, t * K2 + m + 1)
                            last = nc.gpsimd.tensor_tensor(hT[:, s, m, :], hT[:, s, m, :], yT[:, s, m, :], ALU.add)
                        last.then_inc(done, 1)

                    def step(at):
                        if x := at(3):
                            add_skip(*x, S["relu1"], S["added1"])
                        if x := at(2):
                            add_skip(*x, S["relu0"], S["added0"])
                        if x := at(0):
                            t, s = x
                            wait_tile(pool, S["x_ready"], t, TU)
                            nc.gpsimd.tensor_tensor(XB[:, s, :], tile_of(X, t), OUT_B, ALU.add).then_inc(S["xb_ready"], 1)

                    tile_steps(pool, step, 3)

                @block.vector
                def _(dve):
                    def step(at):
                        x0, x1, x3, x4, x5 = at(0), at(1), at(3), at(4), at(5, True)
                        if x5:
                            t5, s5, r = x5
                            x_norm.invert(dve, t5, s5)
                        if x1:
                            h_norm.invert(dve, *x1)
                        if x5:
                            n_stores.wait_free(dve, s5, r)
                            nc.vector.tensor_scalar(N2[:, s5, :], tile_of(X, t5), x_norm.mean(s5), x_norm.inverse(s5),
                                                    ALU.subtract, ALU.mult).then_inc(S["n2_ready"], 1)
                        if x1:
                            t, s = x1
                            nc.vector.tensor_scalar(H[:, s, :], H[:, s, :], h_norm.mean(s), h_norm.inverse(s),
                                                    ALU.subtract, ALU.mult).then_inc(S["h_ready"], 1)
                        if x4:
                            t, s = x4
                            wait_tile(dve, S["back"], t)
                            nc.vector.tensor_tensor(Z[:, s, :], ps_back[:, 0:D], tile_of(NR, t), ALU.add).then_inc(S["z_ready"], 1)
                        if x0:
                            t0, s0 = x0
                            wait_tile(dve, S["agg_done"], t0)
                            nc.vector.scalar_tensor_tensor(H[:, s0, :], ps_agg[:, 0:D], 0.0, tile_of(NR, t0), ALU.max, ALU.add)
                            nc.vector.tensor_scalar(deg_inv[:, ds(t0, 1)], ps_agg[:, D:D + 1], 1.0, None, ALU.max).then_inc(S["hpre"], 1)
                        if x4:
                            z_norm.take_stats(dve, t, s, Z[:, s, :], S["z_ready"])
                        if x0:
                            h_norm.take_stats(dve, t0, s0, H[:, s0, :], S["hpre"])
                        if x4:
                            z_norm.join_stats(dve, t, s)
                        if x0:
                            h_norm.join_stats(dve, t0, s0)
                        if x4:
                            wait_tile(dve, z_norm.joined, t)
                            nc.vector.scalar_tensor_tensor(Z[:, s, :], Z[:, s, :], z_norm.mean(s), OUT_S, ALU.subtract, ALU.mult).then_inc(S["centred"], 1)
                        if x3:
                            t3, s3 = x3
                            wait_tile(dve, S["third"], t3)
                            for m in range(K2):
                                last = nc.vector.scalar_tensor_tensor(hT[:, s3, m, :], ps_2[:, m * P:(m + 1) * P], b_mlp[:, 2, m:m + 1],
                                                                      hT[:, s3, m, :], ALU.add, ALU.add)
                            last.then_inc(S["added2"], 1)
                        if x4:
                            z_norm.invert(dve, t, s)
                            wait_tile(dve, S["centred"], t)
                            wait_tile(dve, S["xb_ready"], t)
                            nc.vector.scalar_tensor_tensor(tile_of(X, t), Z[:, s, :], z_norm.inverse(s), XB[:, s, :],
                                                           ALU.mult, ALU.add).then_inc(S["x_ready"], 1)
                            x_norm.take_stats(dve, t, s, tile_of(X, t), S["x_ready"])
                        if x5:
                            wait_tile(dve, S["logits"], t5)
                            nc.vector.tensor_tensor(tile_of(logit0, t5), ps_g[:, 0:E0], gate_b0[:], ALU.add).then_inc(S["logits_in"], 1)
                        if x4:
                            x_norm.join_stats(dve, t, s)

                    tile_steps(dve, step, 5)
                    dve.wait_ge(S["hpre"], T)
                    nc.vector.reciprocal(deg_inv[:], deg_inv[:])

                @block.sync
                def _(sp):
                    def step(at):
                        if x := at(5):
                            t, s = x
                            wait_tile(sp, S["n2_ready"], t)
                            n_stores.store(sp, rows_of(n_dram, t), N2[:, s, :], s)

                    n_stores.begin(sp)
                    tile_steps(sp, step, 5)
                    n_stores.wait_all(sp)

        def route(tag, E, NB, logits, of_probs):
            with ExitStack() as c:
                hot = sb(tag + "hot", [P, 2, T, E], F32, c)
                both = sb(tag + "both", [P, T, E], F32, c)
                tot = sb(tag + "tot", [P, E, T], F32, c)
                inc = sb(tag + "inc", [P, E, T], F32, c)
                fresh = sb(tag + "fresh", [P, E, T], F32, c)
                cnt_i = sb(tag + "cnt_i", [P, E], I32, c)
                cnt = sb(tag + "cnt", [P, E], F32, c)
                end = sb(tag + "end", [P, E], F32, c)
                iota_e = sb(tag + "iota_e", [P, E], F32, c)
                at_e = sb(tag + "at", [P, T, E], F32, c)
                tmp = sb(tag + "tmp", [P, T, E], F32, c)
                v8 = sb(tag + "v8", [P, T, 8], F32, c)
                i8 = sb(tag + "i8", [P, T, 8], U32, c)
                top_idx = sb(tag + "top_idx", [P, T, 2], F32, c)
                rowf = sb(tag + "rowf", [P, T, 2], F32, c)
                part_i = sb(tag + "part_i", [P, 2, T, 2], I32, c)
                part = sb(tag + "part", [P, 2, T, 2], F32, c)
                in_block = sb(tag + "in_block", [P, TU, 2, NB], F32, c)
                in_place = sb(tag + "in_place", [P, 2, TU, 2, P], F32, c)
                named = sb(tag + "named", [P, 2, TU, 2, NB], F32, c)
                tok_f = sb(tag + "tok_f", [NB, P], F32, c)
                iota_bk = sb(tag + "iota_bk", [P, NB], F32, c)
                blk_ge = sb(tag + "blk_ge", [1, NB, E], F32, c)
                blk_f = sb(tag + "blk_f", [1, NB], F32, c)
                ii = sb(tag + "ii", [P, NB], I32, c)
                e1 = sb(tag + "e1", [P, T], F32, c)
                e2 = sb(tag + "e2", [P, T], F32, c)
                ps_b = pb(tag + "ps_before", [P, 512], c)
                ps_a = pb(tag + "ps_all", [P, 512], c)
                ps_n = pb(tag + "ps_token", [P, 512], c)
                ps_c = pb(tag + "ps_turned", [P, 512], c)
                s_c, s_h, s_p, s_d, s_less, s_exp = (sem(tag + "consts"), sem(tag + "hot_ready"), sem(tag + "counted"),
                                                     sem(tag + "dve_chain"), sem(tag + "differences"), sem(tag + "exp"))
                s_pc, s_named, s_mm, s_tok, s_turned = (sem(tag + n) for n in ("pool_chain", "named", "placed", "tokens", "turned"))
                block = c.enter_context(nc.Block())
                TE = T * E

                @block.gpsimd
                def _(pool):
                    nc.gpsimd.iota(ii[:], [[1, NB]], base=0, channel_multiplier=0)
                    nc.gpsimd.memset(fresh[:], 1.0).then_inc(s_pc, 1)
                    pool.wait_ge(s_pc, 1)
                    nc.gpsimd.tensor_copy(iota_e[:], ii[:, 0:E])
                    nc.gpsimd.tensor_copy(iota_bk[:], ii[:])
                    nc.gpsimd.memset(fresh[:, :, 0], 0.0).then_inc(s_c, 1)

                @block.tensor
                def _(pe):
                    pe.wait_ge(s_h, 1)
                    nc.tensor.matmul(ps_b[:, 0:TE], before[:], both[:].rearrange("p t e -> p (t e)"), start=True, stop=True)
                    nc.tensor.matmul(ps_a[:, 0:TE], ones[:], both[:].rearrange("p t e -> p (t e)"), start=True, stop=True).then_inc(s_p, 1)
                    for i in range(IT):
                        pe.wait_ge(s_named, i + 1)
                        for u in range(TU):
                            for k in range(2):
                                last = nc.tensor.matmul(ps_n[0:NB, 0:P], named[:, i % 2, u, k, :], in_place[:, i % 2, u, k, :],
                                                        start=(i == u == k == 0), stop=(i == IT - 1 and u == TU - 1 and k == 1))
                        last.then_inc(s_mm, 1)
                    pe.wait_ge(s_tok, 1)
                    nc.tensor.transpose(ps_c[:, 0:NB], tok_f[:], ident[0:NB, 0:NB]).then_inc(s_turned, 1)

                @block.scalar
                def _(act):
                    act.wait_ge(s_less, 1)
                    if of_probs:
                        nc.scalar.activation(logits[:], logits[:], ACT.Exp).then_inc(s_exp, 1)
                    else:
                        nc.scalar.activation(e1[:], e1[:], ACT.Exp).then_inc(s_exp, 1)

                @block.vector
                def _(dve):
                    n = [0]

                    def link(ins):
                        n[0] += 1
                        ins.then_inc(s_d, 1)
                        dve.wait_ge(s_d, n[0])

                    if of_probs:
                        link(nc.vector.tensor_reduce(e1[:], logits[:], AX_X, ALU.max))
                        nc.vector.tensor_tensor(logits[:], logits[:], e1[:].unsqueeze(2).to_broadcast([P, T, E]), ALU.subtract).then_inc(s_less, 1)
                        dve.wait_ge(s_exp, 1)
                        link(nc.vector.tensor_reduce(e1[:], logits[:], AX_X, ALU.add))
                        link(nc.vector.reciprocal(e2[:], e1[:]))
                        link(nc.vector.tensor_tensor(logits[:], logits[:], e2[:].unsqueeze(2).to_broadcast([P, T, E]), ALU.mult))
                    for t in range(T):
                        last = nc.vector.max(v8[:, t, :], logits[:, t, :])
                    link(last)
                    for t in range(T):
                        last = nc.vector.max_index(i8[:, t, :], v8[:, t, :], logits[:, t, :])
                    link(last)
                    if of_probs:
                        link(nc.vector.tensor_tensor(e1[:], v8[:, :, 1], v8[:, :, 0], ALU.add))
                        link(nc.vector.tensor_scalar(e1[:], e1[:], 1e-12, None, ALU.max))
                        link(nc.vector.reciprocal(e2[:], e1[:]))
                        nc.vector.tensor_tensor(top_w[:], v8[:, :, 0:2], e2[:].unsqueeze(2).to_broadcast([P, T, 2]), ALU.mult)
                    else:
                        nc.vector.tensor_tensor(e1[:], v8[:, :, 1], v8[:, :, 0], ALU.subtract).then_inc(s_less, 1)
                    link(nc.vector.tensor_tensor(top_idx[:], i8[:, :, 0:2], row_far[:].unsqueeze(2).to_broadcast([P, T, 2]), ALU.add))
                    dve.wait_ge(s_c, 1)
                    for k in range(2):
                        last = nc.vector.tensor_tensor(hot[:, k, :, :], iota_e[:].unsqueeze(1).to_broadcast([P, T, E]),
                                                       top_idx[:, :, k:k + 1].to_broadcast([P, T, E]), ALU.is_equal)
                    link(last)
                    nc.vector.tensor_tensor(both[:], hot[:, 0, :, :], hot[:, 1, :, :], ALU.add).then_inc(s_h, 1)
                    if not of_probs:
                        dve.wait_ge(s_exp, 1)
                        link(nc.vector.tensor_scalar(e2[:], e1[:], 1.0, None, ALU.add))
                        link(nc.vector.reciprocal(top_w[:, :, 0], e2[:]))
                        nc.vector.tensor_tensor(top_w[:, :, 1], top_w[:, :, 0], e1[:], ALU.mult)
                    dve.wait_ge(s_p, 1)
                    link(nc.vector.tensor_copy(tot[:], ps_a[:, 0:TE].rearrange("p (t e) -> p e t", e=E)))
                    link(nc.vector.tensor_tensor_scan(inc[:].rearrange("p e t -> p (e t)"), fresh[:].rearrange("p e t -> p (e t)"),
                                                      tot[:].rearrange("p e t -> p (e t)"), 0.0, ALU.mult, ALU.add))
                    link(nc.vector.tensor_scalar(cnt_i[:], inc[:, :, T - 1], float(P - 1), None, ALU.add))
                    link(nc.vector.tensor_scalar(cnt_i[:], cnt_i[:], 7, 7, ALU.arith_shift_right, ALU.logical_shift_left))
                    link(nc.vector.tensor_copy(cnt[:], cnt_i[:]))
                    link(nc.vector.tensor_tensor_scan(end[:], ones[:, 0:E], cnt[:], 0.0, ALU.mult, ALU.add))
                    link(nc.vector.tensor_tensor(cnt[:], end[:], cnt[:], ALU.subtract))
                    link(nc.vector.tensor_tensor(inc[:], inc[:], tot[:], ALU.subtract))
                    link(nc.vector.tensor_tensor(inc[:], inc[:], cnt[:].unsqueeze(2).to_broadcast([P, E, T]), ALU.add))
                    link(nc.vector.tensor_tensor(at_e[:], ps_b[:, 0:TE].rearrange("p (t e) -> p t e", e=E),
                                                 inc[:].rearrange("p e t -> p t e"), ALU.add))
                    for k in range(2):
                        link(nc.vector.tensor_tensor(tmp[:], hot[:, k, :, :], at_e[:], ALU.mult))
                        link(nc.vector.tensor_reduce(rowf[:, :, k], tmp[:], AX_X, ALU.add))
                    link(nc.vector.tensor_tensor(slot[:], rowf[:], row_far[:].unsqueeze(2).to_broadcast([P, T, 2]), ALU.add))
                    nc.vector.tensor_scalar(part_i[:, 0, :, :], slot[:], 7, None, ALU.arith_shift_right)
                    link(nc.vector.tensor_scalar(part_i[:, 1, :, :], slot[:], P - 1, None, ALU.bitwise_and))
                    link(nc.vector.tensor_copy(part[:], part_i[:]))
                    for i in range(IT):
                        ts_ = slice(i * TU, (i + 1) * TU)
                        if i >= 2:
                            dve.wait_ge(s_mm, i - 1)
                        nc.vector.tensor_tensor(in_place[:, i % 2], iota_w[:].unsqueeze(1).unsqueeze(1).to_broadcast([P, TU, 2, P]),
                                                part[:, 1, ts_, :].unsqueeze(3).to_broadcast([P, TU, 2, P]), ALU.is_equal)
                        link(nc.vector.tensor_tensor(in_block[:], iota_bk[:].unsqueeze(1).unsqueeze(1).to_broadcast([P, TU, 2, NB]),
                                                     part[:, 0, ts_, :].unsqueeze(3).to_broadcast([P, TU, 2, NB]), ALU.is_equal))
                        nc.vector.tensor_tensor(named[:, i % 2], in_block[:],
                                                row_1[:, ts_].unsqueeze(2).unsqueeze(3).to_broadcast([P, TU, 2, NB]), ALU.mult).then_inc(s_named, 1)
                        dve.wait_ge(s_named, i + 1)
                    link(nc.vector.tensor_scalar(blk_f[:], iota_bk[0:1, :], float(P), None, ALU.mult))
                    link(nc.vector.tensor_tensor(blk_ge[:], blk_f[:].unsqueeze(2).to_broadcast([1, NB, E]),
                                                 end[0:1, :].unsqueeze(1).to_broadcast([1, NB, E]), ALU.is_ge))
                    link(nc.vector.tensor_reduce(blk_f[:], blk_ge[:], AX_X, ALU.add))
                    nc.vector.tensor_scalar(block_expert[:, 0:NB], blk_f[:], float(E - 1), None, ALU.min)
                    dve.wait_ge(s_mm, IT)
                    nc.vector.tensor_copy(tok_f[:], ps_n[0:NB, 0:P]).then_inc(s_tok, 1)
                    dve.wait_ge(s_turned, 1)
                    nc.vector.tensor_scalar(token[:, 0:NB], ps_c[:, 0:NB], 1.0, 0.0, ALU.subtract, ALU.max)

        def experts(tag, E, F, NB, w1, b1_cols, w2, b2, func):
            FJ = F // P
            with ExitStack() as c:
                xs = sb(tag + "xs", [P, BU, D], F32, c)
                xT = sb(tag + "xT", [P, BU, K2, P], F32, c)
                W1 = sb(tag + "W1", [P, BU, K2, F], F32, c)
                W2 = sb(tag + "W2", [P, BU, FJ, D], F32, c)
                hidT = sb(tag + "hidT", [P, BU, FJ, P], F32, c)
                ys = sb(tag + "ys", [P, BU, D], F32, c)
                idx = sb(tag + "idx", [P, BU], I32, c)
                b2_rows = sb(tag + "b2_rows", [P, E, D], F32, c)
                ps_x = pb(tag + "ps_x", [P, 2, 512], c)
                ps_h = pb(tag + "ps_h", [P, 2, 512], c)
                ps_y = pb(tag + "ps_y", [P, 2, 512], c)
                rows_in = [held_sem(f"{tag}rows_in{s}") for s in range(BU)]
                w1_in = [sem(f"{tag}w1_in{s}") for s in range(BU)]
                w2_in = [sem(f"{tag}w2_in{s}") for s in range(BU)]
                stored = [sem(f"{tag}stored{s}") for s in range(BU)]
                b2_in, idx_ready, turned, xT_ready, mm1, hid_ready, mm2, y_ready = (sem(tag + n) for n in (
                    "b2_in", "idx_ready", "turned", "xT_ready", "first_done", "hidden_ready", "second_done", "y_ready"))
                block = c.enter_context(nc.Block())
                NI = NB // BU
                assert NI * BU == NB

                def in_loops(eng, body):
                    body(0, True)
                    with eng.Fori(1, NI) as i:
                        body(i, False)

                def expert_of(eng, b):
                    return eng.value_load(block_expert[0:1, ds(b, 1)], min_val=0, max_val=E - 1)

                @block.sync
                def _(sp):
                    def store(b, s):
                        sp.wait_ge(y_ready, b + 1)
                        sp.dma_start(rows_of(ys_dram, b), ys[:, s, :]).then_inc(stored[s], 16)

                    def body(i, first):
                        for s in range(BU):
                            b = i * BU + s
                            e = expert_of(sp, b)
                            if not first:
                                sp.wait_ge(mm1, b + 1 - BU)
                            sp.dma_start(W1[:, s, :, :], w1[ds(e, 1), :, :].rearrange("a (k p) f -> p (a k) f", p=P)).then_inc(w1_in[s], 16)
                            if not first:
                                sp.wait_ge(mm2, b + 1 - BU)
                            sp.dma_start(W2[:, s, :, :], w2[ds(e, 1), :, :].rearrange("a (j p) d -> p (a j) d", p=P)).then_inc(w2_in[s], 16)
                            if first and s == 0:
                                sp.dma_start(b2_rows[:], b2.rearrange("(a e) d -> a e d", a=1).to_broadcast([P, E, D])).then_inc(b2_in, 16)
                            if not first:
                                store(b - BU, s)

                    in_loops(sp, body)
                    for s in range(BU):
                        store(NB - BU + s, s)
                    for s in range(BU):
                        sp.wait_ge(stored[s], NI * 16)

                @block.gpsimd
                def _(pool):
                    def body(i, first):
                        for s in range(BU):
                            hold(pool, "pool", idx_ready, i * BU + s + 1)
                            pool.indirect_dma_start(out=xs[:, s, :], out_offset=None, in_=n_dram,
                                                    in_offset=bass.IndirectOffsetOnAxis(ap=idx[:, s:s + 1], axis=0)).then_inc(rows_in[s], 16)
                        if first:
                            nc.gpsimd.memset(sumT[:], 0.0)

                    in_loops(pool, body)

                @block.tensor
                def _(pe):
                    def turn(b, s, pre, reuse):
                        pe.wait_ge(rows_in[s], pre)
                        if reuse:
                            pe.wait_ge(xT_ready, b - 1)
                        turn2(ps_x[:, s % 2, 0:D], xs[:, s, :], turned)

                    def first_layer(b, s, pre, reuse):
                        pe.wait_ge(w1_in[s], pre)
                        pe.wait_ge(xT_ready, b + 1)
                        if reuse:
                            pe.wait_ge(hid_ready, b - 1)
                        for j in range(FJ):
                            for k in range(K2):
                                last = nc.tensor.matmul(ps_h[:, s % 2, j * P:(j + 1) * P], W1[:, s, k, j * P:(j + 1) * P],
                                                        xT[:, s, k, :], start=(k == 0), stop=(k == K2 - 1))
                        last.then_inc(mm1, 1)

                    def second_layer(b, s, pre, reuse):
                        pe.wait_ge(w2_in[s], pre)
                        pe.wait_ge(hid_ready, b + 1)
                        if reuse:
                            pe.wait_ge(y_ready, b - 1)
                        for j in range(FJ):
                            last = nc.tensor.matmul(ps_y[:, s % 2, 0:D], hidT[:, s, j, :], W2[:, s, j, :], start=(j == 0), stop=(j == FJ - 1))
                        last.then_inc(mm2, 1)

                    def body(i, first, last=False):
                        for s in range(BU):
                            b = i * BU + s
                            t = (s + 1) % BU
                            if not (last and s == BU - 1):
                                turn(b + 1, t, (i + 1 + (s == BU - 1)) * 16, not (first and s < 1))
                            first_layer(b, s, (i + 1) * 16, not (first and s < 2))
                            if not (first and s == 0):
                                second_layer(b - 1, (s - 1) % BU, (i + (s > 0)) * 16, not (first and s < 3))

                    turn(0, 0, 16, False)
                    body(0, True)
                    with pe.Fori(1, NI - 1) as i:
                        body(i, False)
                    body(NI - 1, False, True)
                    second_layer(NB - 1, BU - 1, NI * 16, True)

                @block.scalar
                def _(act):
                    def index(b, s, first):
                        if not first:
                            act.wait_ge(turned, b + 1 - BU)
                        nc.scalar.activation(idx[:, s:s + 1], token[:, ds(b, 1)], ACT.Copy).then_inc(idx_ready, 1)

                    def xT_copy(b, s, first):
                        act.wait_ge(turned, b + 1)
                        if not first:
                            act.wait_ge(mm1, b + 1 - BU)
                        nc.scalar.activation(xT[:, s, :, :].rearrange("p k n -> p (k n)"), ps_x[:, s % 2, 0:D], ACT.Copy).then_inc(xT_ready, 1)

                    def hidden(b, s, first):
                        e = expert_of(act, b)
                        act.wait_ge(mm1, b + 1)
                        if not first:
                            act.wait_ge(mm2, b + 1 - BU)
                        for j in range(FJ):
                            last = nc.scalar.activation(hidT[:, s, j, :], ps_h[:, s % 2, j * P:(j + 1) * P], func,
                                                        bias=b1_cols[:, ds(e * FJ + j, 1)])
                        last.then_inc(hid_ready, 1)

                    def body(i, first, last=False):
                        for s in range(BU):
                            b = i * BU + s
                            if not (last and s == BU - 1):
                                xT_copy(b + 1, (s + 1) % BU, first and s < BU - 1)
                            if not last:
                                index(b + BU, s, False)
                            hidden(b, s, first)

                    for s in range(BU):
                        index(s, s, True)
                    xT_copy(0, 0, True)
                    body(0, True)
                    with act.Fori(1, NI - 1) as i:
                        body(i, False)
                    body(NI - 1, False, True)

                @block.vector
                def _(dve):
                    def body(i, first):
                        for s in range(BU):
                            b = i * BU + s
                            e = expert_of(dve, b)
                            dve.wait_ge(mm2, b + 1)
                            if not first:
                                dve.wait_ge(stored[s], i * 16)
                            nc.vector.tensor_tensor(ys[:, s, :], ps_y[:, s % 2, 0:D], tile_of(b2_rows, e), ALU.add).then_inc(y_ready, 1)

                    dve.wait_ge(b2_in, 16)
                    in_loops(dve, body)

        class Mix:

            def __init__(self, tag, c, NB):
                self.Y = sb(tag + "Y", [P, TU, 2, D], F32, c)
                self.own = sb(tag + "own", [P, TU, D], F32, c)
                self.idx = sb(tag + "gidx", [P, TU, 2], I32, c)
                self.gathered = [held_sem(f"{tag}gathered{u}") for u in range(TU)]
                self.own_in = [sem(f"{tag}own_in{u}") for u in range(TU)]
                self.cleared, self.idx_ready, self.once, self.twice = (
                    sem(tag + n) for n in ("cleared", "idx_ready", "mixed_once", "mixed_twice"))
                self.NB = NB

            def clear(self, pool):
                nc.gpsimd.memset(self.Y[:], 0.0).then_inc(self.cleared, 1)
                pool.wait_ge(self.cleared, 1)

            def indices(self, act, t, s):
                wait_tile(act, self.twice, t, TU)
                nc.scalar.activation(self.idx[:, s, :], tile_of(slot, t), ACT.Copy).then_inc(self.idx_ready, 1)

            def gather(self, pool, t, s):
                hold_tile(pool, "pool", self.idx_ready, t)
                for k in range(2):
                    pool.indirect_dma_start(out=self.Y[:, s, k, :], out_offset=None, in_=ys_dram,
                                            in_offset=bass.IndirectOffsetOnAxis(ap=self.idx[:, s, k:k + 1], axis=0),
                                            bounds_check=self.NB * P - 1, oob_is_err=False).then_inc(self.gathered[s], 16)

            def load_own(self, sp, t, s):
                wait_tile(sp, self.once, t, TU)
                sp.dma_start(self.own[:, s, :], rows_of(n_dram, t)).then_inc(self.own_in[s], 16)

            def first_of(self, dve, t, s, r, out):
                dve.wait_ge(self.gathered[s], (r + 1) * 32)
                dve.wait_ge(self.own_in[s], (r + 1) * 16)
                nc.vector.scalar_tensor_tensor(out, self.Y[:, s, 0, :], top_w[:, ds(t, 1), 0], self.own[:, s, :],
                                               ALU.mult, ALU.add).then_inc(self.once, 1)

            def second_of(self, dve, t, s, out):
                wait_tile(dve, self.once, t)
                nc.vector.scalar_tensor_tensor(out, self.Y[:, s, 1, :], top_w[:, ds(t, 1), 1], out, ALU.mult, ALU.add).then_inc(self.twice, 1)

        def sparse_products():
            STRUCK = -3.4028235e38
            with ExitStack() as c:
                H = sb("m0H", [P, TU, D], F32, c)
                XB = sb("m0XB", [P, TU, D], F32, c)
                N3 = sb("m0N3", [P, TU, D], F32, c)
                nT = sb("m0nT", [P, TU, K2, P], F32, c)
                HD = sb("m0HD", [P, TU, 2 * D], F32, c)
                WK = sb("m0WK", [P, TU, D], F32, c)
                v8 = sb("m0v8", [P, TU, 8], F32, c)
                mr = sb("m0mr", [P, TU], F32, c)
                ps_n = pb("m0ps_n", [P, 512], c)
                ps_d = pb("m0ps_d", [P, 512], c)
                y_norm, x_norm = Norm("my", c, eps5[:]), Norm("mx", c, eps5[:])
                mixer = Mix("m0", c, NB0)
                S = {n: sem("M0" + n) for n in ("xb_ready", "centred", "x_ready", "mean_ready", "n_ready", "turned", "nT_ready", "dense",
                                                "dense_in", "x_added", "max8", "replaced", "sparse")}
                hs_stores = Stores("M0")
                block = c.enter_context(nc.Block())

                @block.gpsimd
                def _(pool):
                    mixer.clear(pool)

                    def step(at):
                        if x := at(0):
                            mixer.gather(pool, *x)
                        if x := at(4):
                            t, s = x
                            hold_tile(pool, "pool", S["dense_in"], t)
                            nc.gpsimd.tensor_tensor(tile_of(X, t), tile_of(X, t), HD[:, s, 0:D], ALU.add).then_inc(S["x_added"], 1)
                        if x := at(0):
                            t, s = x
                            wait_tile(pool, S["x_ready"], t, TU)
                            nc.gpsimd.tensor_tensor(XB[:, s, :], tile_of(X, t), FFN_B, ALU.add).then_inc(S["xb_ready"], 1)

                    tile_steps(pool, step, 4)

                @block.sync
                def _(sp):
                    def step(at):
                        if x := at(0):
                            mixer.load_own(sp, *x)
                        if x := at(5):
                            t, s = x
                            wait_tile(sp, S["sparse"], t)
                            hs_stores.store(sp, rows_of(hs_dram, t), WK[:, s, :], s)

                    hs_stores.begin(sp)
                    tile_steps(sp, step, 5)
                    hs_stores.wait_all(sp)

                @block.scalar
                def _(act):
                    def step(at):
                        if x := at(0):
                            mixer.indices(act, *x)
                        if x := at(2):
                            x_norm.deviation(act, *x)
                        if x := at(3):
                            t, s = x
                            wait_tile(act, S["turned"], t)
                            nc.scalar.activation(nT[:, s, :, :].rearrange("p k n -> p (k n)"), ps_n[:, 0:D], ACT.Copy).then_inc(S["nT_ready"], 1)
                        if x := at(2):
                            t, s = x
                            wait_tile(act, S["mean_ready"], t)
                            nc.scalar.activation(N3[:, s, :], tile_of(X, t), ACT.Identity, bias=mr[:, s:s + 1],
                                                 scale=x_norm.inverse(s)).then_inc(S["n_ready"], 1)
                        if x := at(1):
                            y_norm.deviation(act, *x)
                        if x := at(3):
                            t, s = x
                            wait_tile(act, S["dense"], t)
                            wait_tile(act, S["sparse"], t, TU - 3)
                            nc.scalar.activation(HD[:, s, :], ps_d[:], ACT.Copy).then_inc(S["dense_in"], 1)

                    tile_steps(act, step, 5)

                @block.tensor
                def _(pe):
                    def step(at):
                        if x := at(3):
                            t, s = x
                            wait_tile(pe, S["n_ready"], t)
                            wait_tile(pe, S["nT_ready"], t, 1)
                            turn2(ps_n, N3[:, s, :], S["turned"])
                            wait_tile(pe, S["nT_ready"], t)
                            wait_tile(pe, S["dense_in"], t, 1)
                            for k in range(K2):
                                last = nc.tensor.matmul(ps_d[:], nT[:, s, k, :], w_dense[:, k, :], start=(k == 0), stop=(k == K2 - 1))
                            last.then_inc(S["dense"], 1)

                    tile_steps(pe, step, 5)

                @block.vector
                def _(dve):
                    def largest(x, r):
                        if x:
                            t, s, slot_round = x
                            if r == 0:
                                hold_tile(dve, "dve", S["dense_in"], t)
                                hs_stores.hold_free("dve", dve, s, slot_round)
                            else:
                                hold(dve, "dve", S["replaced"], t * 4 + r)
                            nc.vector.max(v8[:, s, :], HD[:, s, D:2 * D] if r == 0 else WK[:, s, :]).then_inc(S["max8"], 1)

                    def strike(x, r):
                        if x:
                            t, s, _ = x
                            hold(dve, "dve", S["max8"], t * 4 + r + 1)
                            nc.vector.match_replace(WK[:, s, :], v8[:, s, :], HD[:, s, D:2 * D] if r == 0 else WK[:, s, :],
                                                    STRUCK).then_inc(S["replaced"], 1)

                    def step(at):
                        x1, x2, x4 = at(1, True), at(2), at(4, True)
                        if x1:
                            t, s, r = x1
                            mixer.first_of(dve, t, s, r, H[:, s, :])
                        largest(x4, 0)
                        if x1:
                            mixer.second_of(dve, t, s, H[:, s, :])
                        strike(x4, 0)
                        if x2:
                            x_norm.invert(dve, *x2)
                        if x1:
                            y_norm.take_stats(dve, t, s, H[:, s, :], mixer.twice)
                        largest(x4, 1)
                        if x2:
                            t2, s2 = x2
                            nc.vector.tensor_scalar(mr[:, s2:s2 + 1], x_norm.mean(s2), x_norm.inverse(s2), -1.0,
                                                    ALU.mult, ALU.mult).then_inc(S["mean_ready"], 1)
                        if x1:
                            y_norm.join_stats(dve, t, s)
                        strike(x4, 1)
                        if x1:
                            wait_tile(dve, y_norm.joined, t)
                            nc.vector.scalar_tensor_tensor(H[:, s, :], H[:, s, :], y_norm.mean(s), FFN_S, ALU.subtract, ALU.mult).then_inc(S["centred"], 1)
                        largest(x4, 2)
                        if x1:
                            y_norm.invert(dve, t, s)
                        strike(x4, 2)
                        if x1:
                            wait_tile(dve, S["centred"], t)
                            wait_tile(dve, S["xb_ready"], t)
                            nc.vector.scalar_tensor_tensor(tile_of(X, t), H[:, s, :], y_norm.inverse(s), XB[:, s, :],
                                                           ALU.mult, ALU.add).then_inc(S["x_ready"], 1)
                        largest(x4, 3)
                        if x1:
                            x_norm.take_stats(dve, t, s, tile_of(X, t), S["x_ready"])
                        strike(x4, 3)
                        if x1:
                            x_norm.join_stats(dve, t, s)
                        if x4:
                            t4, s4, _ = x4
                            dve.wait_ge(S["replaced"], t4 * 4 + 4)
                            nc.vector.scalar_tensor_tensor(WK[:, s4, :], WK[:, s4, :], STRUCK, HD[:, s4, D:2 * D],
                                                           ALU.is_equal, ALU.mult).then_inc(S["sparse"], 1)

                    tile_steps(dve, step, 4)

        def neighbour_means():
            with ExitStack() as c:
                lhs = sb("a1lhs", [P, TU, K2, P], F32, c)
                N4 = sb("a1N4", [P, TU, D], F32, c)
                nT = sb("a1nT", [P, TU, K2, P], F32, c)
                ps_s = pb("a1ps_s", [P, TU, 512], c)
                ps_n = pb("a1ps_n", [P, 512], c)
                ps_g = pb("a1ps_g", [P, 512], c)
                norm = Norm("a1", c, eps5[:])
                S = {n: sem("A1" + n) for n in ("lhs_ready", "turned", "x_ready", "n_ready", "n_turned", "nT_ready",
                                                "logits", "logits_in")}
                n_stores = Stores("A1")
                block = c.enter_context(nc.Block())

                @block.scalar
                def _(act):
                    def step(at):
                        if x := at(0):
                            t, s = x
                            wait_tile(act, S["turned"], t, TU)
                            nc.scalar.activation(lhs[:, s, :, :], sumT[:, 0:K2, ds(t * P, P)], ACT.Copy).then_inc(S["lhs_ready"], 1)
                        if x := at(3):
                            norm.deviation(act, *x)
                        if x := at(4):
                            t, s = x
                            wait_tile(act, S["n_turned"], t)
                            nc.scalar.activation(nT[:, s, :, :].rearrange("p k n -> p (k n)"), ps_n[:, 0:D], ACT.Copy).then_inc(S["nT_ready"], 1)

                    tile_steps(act, step, 5)

                @block.tensor
                def _(pe):
                    def step(at):
                        if x := at(4):
                            t, s = x
                            wait_tile(pe, S["n_ready"], t)
                            wait_tile(pe, S["nT_ready"], t, 1)
                            turn2(ps_n, N4[:, s, :], S["n_turned"])
                        if x := at(1):
                            t, s = x
                            wait_tile(pe, S["lhs_ready"], t)
                            wait_tile(pe, S["x_ready"], t, TU - 1)
                            turn2(ps_s[:, s, :], lhs[:, s, :, :].rearrange("p k n -> p (k n)"), S["turned"])
                        if x := at(5):
                            t, s = x
                            wait_tile(pe, S["nT_ready"], t)
                            wait_tile(pe, S["logits_in"], t, 1)
                            for k in range(K2):
                                last = nc.tensor.matmul(ps_g[:, 0:E1], nT[:, s, k, :], gate_w1[:, k, :], start=(k == 0), stop=(k == K2 - 1))
                            last.then_inc(S["logits"], 1)

                    tile_steps(pe, step, 5)

                @block.vector
                def _(dve):
                    def step(at):
                        x2, x3, x5 = at(2), at(3, True), at(5)
                        if x2:
                            t, s = x2
                            wait_tile(dve, S["turned"], t)
                            nc.vector.scalar_tensor_tensor(tile_of(X, t), ps_s[:, s, 0:D], deg_inv[:, ds(t, 1)], tile_of(X, t),
                                                           ALU.mult, ALU.add).then_inc(S["x_ready"], 1)
                        if x3:
                            t3, s3, r = x3
                            norm.invert(dve, t3, s3)
                        if x2:
                            norm.take_stats(dve, t, s, tile_of(X, t), S["x_ready"])
                        if x3:
                            n_stores.wait_free(dve, s3, r)
                            nc.vector.tensor_scalar(N4[:, s3, :], tile_of(X, t3), norm.mean(s3), norm.inverse(s3),
                                                    ALU.subtract, ALU.mult).then_inc(S["n_ready"], 1)
                        if x2:
                            norm.join_stats(dve, t, s)
                        if x5:
                            t, s = x5
                            wait_tile(dve, S["logits"], t)
                            nc.vector.tensor_copy(tile_of(logit1, t), ps_g[:, 0:E1]).then_inc(S["logits_in"], 1)

                    tile_steps(dve, step, 5)

                @block.sync
                def _(sp):
                    def step(at):
                        if x := at(3):
                            t, s = x
                            wait_tile(sp, S["n_ready"], t)
                            n_stores.store(sp, rows_of(n_dram, t), N4[:, s, :], s)

                    n_stores.begin(sp)
                    tile_steps(sp, step, 5)
                    n_stores.wait_all(sp)

        def last_sums():
            with ExitStack() as c:
                H = sb("o1H", [P, TU, D], F32, c)
                mixer = Mix("o1", c, NB1)
                s_res, s_out = sem("result_ready"), [sem(f"out_stored{u}") for u in range(TU)]
                block = c.enter_context(nc.Block())

                @block.gpsimd
                def _(pool):
                    mixer.clear(pool)

                    def step(at):
                        if x := at(0):
                            mixer.gather(pool, *x)

                    tile_steps(pool, step, 0)

                @block.scalar
                def _(act):
                    def step(at):
                        if x := at(0):
                            mixer.indices(act, *x)

                    tile_steps(act, step, 0)

                @block.vector
                def _(dve):
                    def step(at):
                        if x := at(0, True):
                            t, s, r = x
                            if not (isinstance(r, int) and r == 0):
                                dve.wait_ge(s_out[s], r * 16)
                            mixer.first_of(dve, t, s, r, H[:, s, :])
                            mixer.second_of(dve, t, s, H[:, s, :])
                            wait_tile(dve, mixer.twice, t)
                            nc.vector.tensor_tensor(H[:, s, :], H[:, s, :], tile_of(X, t), ALU.add).then_inc(s_res, 1)

                    tile_steps(dve, step, 0)

                @block.sync
                def _(sp):
                    def store(t, s):
                        wait_tile(sp, s_res, t)
                        if isinstance(t, int) and t == T - 1:
                            sp.dma_start(out[t * P:N, :], H[0:LAST, s, :]).then_inc(s_out[s], 16)
                        else:
                            sp.dma_start(rows_of(out, t), H[:, s, :]).then_inc(s_out[s], 16)

                    for u in range(TU):
                        mixer.load_own(sp, u, u)
                    with sp.Fori(1, IT) as i:
                        for u in range(TU):
                            store(i * TU + u - TU, u)
                            mixer.load_own(sp, i * TU + u, u)
                    for u in range(TU):
                        store(T - TU + u, u)
                    for u in range(TU):
                        sp.wait_ge(s_out[u], T // TU * 16)

        def show_x():
            with ExitStack() as c:
                s_o = sem("dbgx")
                block = c.enter_context(nc.Block())

                @block.sync
                def _(sp):
                    sp.dma_start(out[0:(T - 1) * P, :].rearrange("(t p) d -> p t d", p=P), X[:, 0:T - 1, :]).then_inc(s_o, 16)
                    sp.dma_start(out[(T - 1) * P:N, :], X[0:LAST, T - 1, :]).then_inc(s_o, 16)
                    sp.wait_ge(s_o, 32)

        node_mlp()
        end_step()
        if debug == "x1":
            return show_x()
        route("r0", E0, NB0, logit0, False)
        end_step()
        experts("e0", E0, F0, NB0, a["L0_ffn_w1"], b1_cols0, a["L0_ffn_w2"], a["L0_ffn_b2"], ACT.Relu)
        end_step()
        sparse_products()
        end_step()
        if debug == "x2":
            return show_x()
        segment_sums("L1_", hs_dram, False)
        end_step()
        neighbour_means()
        end_step()
        if debug == "x3":
            return show_x()
        route("r1", E1, NB1, logit1, True)
        end_step()
        experts("e1", E1, F1, NB1, a["L1_ffn_w1"], b1_cols1, a["L1_ffn_w2"], a["L1_ffn_b2"], ACT.Gelu)
        end_step()
        last_sums()


def kernel(**inputs):
    import numpy as _np
    import concourse.bacc as _bacc
    from concourse import mybir as _mybir
    from concourse.bass_utils import run_bass_kernel_spmd as _run

    nc = _bacc.Bacc("TRN2", target_bir_lowering=False, num_devices=1)
    arrays, args = {}, {}
    for name in inputs:
        v = _np.ascontiguousarray(inputs[name])
        arrays[f"in_{name}"] = v
        args[name] = nc.dram_tensor(f"in_{name}", v.shape, _mybir.dt.from_np(v.dtype), kind="ExternalInput").ap()
    shape = DBG_SHAPE or inputs["x"].shape
    out = nc.dram_tensor("out", shape, _mybir.dt.from_np(_np.dtype("float32")), kind="ExternalOutput").ap()
    build(nc, args, out, DEBUG)
    r = _run(nc, [arrays], core_ids=[0])
    return r.results[0]["out"]


DEBUG, DBG_SHAPE = None, None
```

```python
from contextlib import ExitStack

import numpy as np
import concourse.bass as bass
from concourse import mybir

P = 128
F32 = mybir.dt.float32
I32 = mybir.dt.int32
U32 = mybir.dt.uint32
ALU = mybir.AluOpType
ACT = mybir.ActivationFunctionType
AX_X = mybir.AxisListType.X
ds = bass.ds

TU = 5
GC = 4
GU = 7
GS = 4
BU = 4
FAR = 1.0e6


def build(nc, a, out):
    N, D = a["x"].shape
    E_N, DE = a["edge_attr_64"].shape
    T = -(-N // P)
    NPAD = T * P
    LAST = N - (T - 1) * P
    IT = T // TU
    assert IT * TU == T and D == 256
    GE = GC * P
    NG = -(-E_N // GE)
    GI = NG // GU
    assert GI * GU == NG and NG <= P
    E_LAST = E_N - (NG - 1) * GE
    P_LAST = E_LAST // GC
    assert P_LAST * GC == E_LAST
    WIN = NPAD + P
    K2 = D // P

    GPS = -(-NG // T)
    SHORT = T * GPS - NG
    LEAD = 2
    assert GPS == GS and SHORT < GPS and IT > 2

    E0, _, F0 = a["L0_ffn_w1"].shape
    E1, _, F1 = a["L1_ffn_w1"].shape

    def n_blocks(experts):
        most = 2 * N // P + experts
        return -(-most // BU) * BU

    NB0, NB1 = n_blocks(E0), n_blocks(E1)
    XS_ROWS = max(NB0, NB1) * P

    n_dram = nc.dram_tensor("n_rows", [NPAD, D], F32, kind="Internal").ap()
    token_dram = nc.dram_tensor("token_rows", [NPAD, D], F32, kind="Internal").ap()
    hs_dram = nc.dram_tensor("sparse_rows", [NPAD, D], F32, kind="Internal").ap()
    ys_dram = nc.dram_tensor("expert_out", [XS_ROWS, D], F32, kind="Internal").ap()

    with ExitStack() as ctx:
        def sb(name, shape, dt=F32, c=ctx):
            return c.enter_context(nc.sbuf_tensor(name, shape, dt))

        def pb(name, shape, c=ctx):
            return c.enter_context(nc.psum_tensor(name, shape, F32))

        step_sems = []

        def sem(name):
            step_sems.append(nc.alloc_semaphore(name=name))
            return step_sems[-1]

        def held_sem(name):
            return ctx.enter_context(nc.semaphore(name))

        def end_step():
            nc.clear_and_free_semaphores(step_sems)
            step_sems.clear()
            nc.all_engine_barrier()

        carried = {e: held_sem(e + "_carried") for e in ("dve", "pool", "pe")}

        def hold(eng, name, semaphore, value):
            eng.wait_ge(semaphore, value)
            eng.sem_inc(carried[name], 1)

        X = sb("X", [P, T, D])
        NR = sb("NR", [P, T, D])
        sumT = sb("sumT", [P, 3, WIN])
        ident = sb("ident", [P, P])
        ones = sb("ones", [P, P])
        before = sb("before", [P, P])
        iota_w = sb("iota_w", [P, P])
        win_off = sb("win_off", [P, T])
        row_far = sb("row_far", [P, T])
        src_tab = sb("src_tab", [P, NG, GC], I32)
        rel_tab = sb("rel_tab", [P, NG + 1, GC])
        base_row = sb("base_row", [1, NG], I32)
        iterations_left = sb("iterations_left", [1, IT], I32)
        wide_flag = sb("wide_flag", [1, 1], I32)
        mixed_flag = sb("mixed_flag", [1, 1], I32)
        order_flag = sb("order_flag", [1, 1], I32)
        deg_inv = sb("deg_inv", [P, T])
        row_1 = sb("row_1", [P, T])
        logit0 = sb("logit0", [P, T, E0])
        logit1 = sb("logit1", [P, T, E1])
        token = sb("token", [P, max(NB0, NB1)], I32)
        eps5 = sb("eps5", [P, 1])
        eps6 = sb("eps6", [P, 1])
        top_w = sb("top_w", [P, T, 2])
        slot = sb("slot", [P, T, 2], I32)
        block_expert = sb("block_expert", [1, max(NB0, NB1)], I32)

        w_nodes = sb("w_nodes", [P, K2, D])
        w_edges = sb("w_edges", [DE, D])
        w_mlp = sb("w_mlp", [P, 3, K2, D])
        b_mlp = sb("b_mlp", [P, 3, K2])
        ln_rows = sb("ln_rows", [P, 4, D])
        gate_w0 = sb("gate_w0", [P, K2, E0])
        gate_b0 = sb("gate_b0", [P, E0])
        gate_w1 = sb("gate_w1", [P, K2, E1])
        router_rows = sb("router_rows", [E1, D])
        w_dense = sb("w_dense", [P, K2, 2 * D])
        FJ0, FJ1 = F0 // P, F1 // P
        b1_cols0 = sb("b1_cols0", [P, E0 * FJ0])
        b1_cols1 = sb("b1_cols1", [P, E1 * FJ1])
        aggr_cols = sb("aggr_cols", [P, 2, K2])
        s_w = held_sem("weights_loaded")
        N_LOADS = 21
        LN_NAMES = ["L0_gnn_ln_out_scale", "L0_gnn_ln_out_bias",
                    "L0_ffn_gamma", "L0_ffn_beta"]
        OUT_S, OUT_B, FFN_S, FFN_B = (ln_rows[:, k, :] for k in range(4))

        with ExitStack() as c1:
            srci = sb("srci", [NG, GE], I32, c1)
            dsti = sb("dsti", [NG, GE], I32, c1)
            srcf = sb("srcf", [NG, GE], F32, c1)
            dstf = sb("dstf", [NG, GE], F32, c1)
            dlow = sb("dlow", [NG, GE], F32, c1)
            ends = sb("ends", [NG, 2], F32, c1)
            endr = sb("endr", [1, 2, NG], F32, c1)
            rowid = sb("rowid", [P, T], I32, c1)
            iota_i = sb("iota_i", [P, P], I32, c1)
            offi = sb("offi", [P, T], I32, c1)
            duei = sb("duei", [1, T * GPS], I32, c1)
            late = sb("late", [1, NG], F32, c1)
            st = sb("st", [P, T, 6], F32, c1)
            mv = sb("mv", [P, T, 2], F32, c1)
            rs = sb("rs", [P, T], F32, c1)
            b1r0 = sb("b1r0", [E0 * FJ0, P], F32, c1)
            b1r1 = sb("b1r1", [E1 * FJ1, P], F32, c1)
            bmr = sb("bmr", [5 * K2, P], F32, c1)
            ps_w = pb("ps_w", [P, 512], c1)
            ps_t = pb("ps_t", [P, GC, P], c1)
            ps_u = pb("ps_u", [P, GC, P], c1)
            ps_e = pb("ps_e", [P, 512], c1)
            ps_b = pb("ps_b", [P, 512], c1)

            x_in = [sem(f"x_loaded{p}") for p in range(IT)]
            s_edges, s_n = sem("edges_loaded"), sem("norm_stored")
            s_st, s_jo, s_nm = sem("stats_taken"), sem("stats_joined"), sem("normalized")
            s_pad, s_cst, s_pc = sem("pads_set"), sem("consts_set"), sem("pool_chain")
            s_tr, s_end, s_rowp, s_row, s_bb, s_dv = (sem("edges_transposed"), sem("ends_found"),
                                                           sem("ends_transposed"), sem("base_row_ready"), sem("base_broadcast"), sem("dve_chain"))
            s_wt, s_fl = sem("weights_turned"), sem("flags")
            s_sq, s_rs = sem("deviation"), sem("deviation_inverse")
            block = c1.enter_context(nc.Block())

            @block.sync
            def _(sp):
                def load_x(p, tiles):
                    t = p * TU
                    sp.dma_start(X[:, t:t + tiles, :], a["x"][t * P:(t + tiles) * P, :].rearrange("(t p) d -> p t d", p=P)).then_inc(x_in[p], 16)

                sp.wait_ge(s_pad, 1)
                for tab, name in ((srci, "src"), (dsti, "dst")):
                    sp.dma_start(tab[0:NG - 1, :], a[name][0:(NG - 1) * GE].rearrange("(g e) -> g e", e=GE)).then_inc(s_edges, 16)
                    sp.dma_start(tab[NG - 1:NG, 0:E_LAST], a[name][(NG - 1) * GE:E_N].rearrange("(a e) -> a e", a=1)).then_inc(s_edges, 16)
                for p in range(IT - 1):
                    load_x(p, TU)
                load_x(IT - 1, TU - 1)
                sp.dma_start(X[0:LAST, T - 1, :], a["x"][(T - 1) * P:N, :]).then_inc(x_in[IT - 1], 16)
                for p in range(IT):
                    sp.wait_ge(s_nm, p + 1)
                    t = p * TU
                    sp.dma_start(n_dram[t * P:(t + TU) * P, :].rearrange("(t p) d -> p t d", p=P), NR[:, t:t + TU, :]).then_inc(s_n, 16)
                sp.wait_ge(s_n, 16 * IT)

            @block.gpsimd
            def _(pool):
                nc.gpsimd.memset(X[:, T - 1, :], 0.0)
                nc.gpsimd.memset(srci[:], 0)
                nc.gpsimd.memset(dsti[:], -1).then_inc(s_pad, 1)
                nc.gpsimd.memset(eps5[:], 1e-5)
                nc.gpsimd.memset(eps6[:], 1e-6)
                nc.gpsimd.memset(ident[:], 0.0)
                nc.gpsimd.memset(ones[:], 1.0)
                nc.gpsimd.memset(before[:], 1.0)
                nc.gpsimd.iota(iota_i[:], [[1, P]], base=0, channel_multiplier=0)
                nc.gpsimd.iota(offi[:], [[P, T]], base=0, channel_multiplier=0)
                nc.gpsimd.iota(iterations_left[:], [[-1, IT]], base=IT - 1, channel_multiplier=0)
                nc.gpsimd.iota(rowid[:], [[P, T]], base=0, channel_multiplier=1)
                nc.gpsimd.iota(duei[:], [[P, T], [0, GPS]], base=P * (LEAD - 1), channel_multiplier=0)
                nc.gpsimd.memset(rel_tab[:], -1.0).then_inc(s_pc, 1)
                pool.wait_ge(s_pc, 1)
                nc.gpsimd.affine_select(out=ident[:], in_=ident[:], compare_op=ALU.not_equal, fill=1.0,
                                        base=0, pattern=[[-1, P]], channel_multiplier=1)
                nc.gpsimd.affine_select(out=before[:], in_=before[:], compare_op=ALU.is_gt, fill=0.0,
                                        base=0, pattern=[[1, P]], channel_multiplier=-1)
                nc.gpsimd.tensor_copy(iota_w[:], iota_i[:])
                nc.gpsimd.tensor_copy(win_off[:], offi[:])
                nc.gpsimd.tensor_scalar(row_1[:], rowid[:], 1.0, None, ALU.add)
                nc.gpsimd.tensor_scalar(row_far[:], rowid[:], float(N), FAR, ALU.is_ge, ALU.mult).then_inc(s_cst, 1)
                nc.gpsimd.memset(sumT[:], 0.0)

            @block.scalar
            def _(act):
                loads = [(w_nodes[:], a["L0_gnn_W_message"][0:D, :].rearrange("(k p) n -> p k n", p=P)),
                         (w_edges[:], a["L0_gnn_W_message"][D:D + DE, :]),
                         (gate_w0[:], a["L0_ffn_gate_w"].rearrange("(k p) n -> p k n", p=P)),
                         (gate_b0[:], a["L0_ffn_gate_b"].rearrange("(a n) -> a n", a=1).to_broadcast([P, E0])),
                         (router_rows[:], a["L1_ffn_router_w"]),
                         (w_dense[:, :, 0:D], a["L1_gnn_W_self"].rearrange("(k p) n -> p k n", p=P)),
                         (w_dense[:, :, D:2 * D], a["L1_gnn_W_neigh"].rearrange("(k p) n -> p k n", p=P)),
                         (b1r0[:], a["L0_ffn_b1"].rearrange("e (j p) -> (e j) p", p=P)),
                         (b1r1[:], a["L1_ffn_b1"].rearrange("e (j p) -> (e j) p", p=P)),
                         (bmr[3 * K2:4 * K2, :], a["L0_gnn_ln_aggr_scale"].rearrange("(k p) -> k p", p=P)),
                         (bmr[4 * K2:5 * K2, :], a["L0_gnn_ln_aggr_bias"].rearrange("(k p) -> k p", p=P))]
                for l in range(3):
                    loads.append((w_mlp[:, l, :, :], a[f"L0_gnn_mlp_W{l}"].rearrange("(k p) n -> p k n", p=P)))
                    loads.append((bmr[K2 * l:K2 * l + K2, :], a[f"L0_gnn_mlp_b{l}"].rearrange("(k p) -> k p", p=P)))
                for k, name in enumerate(LN_NAMES):
                    loads.append((ln_rows[:, k, :], a[name].rearrange("(a n) -> a n", a=1).to_broadcast([P, D])))
                for to, src in loads:
                    act.dma_start(to, src).then_inc(s_w, 16)
                assert len(loads) == N_LOADS
                act.wait_ge(s_pc, 1)
                for p in range(IT):
                    act.wait_ge(s_jo, p + 1)
                    nc.scalar.activation(rs[:, p * TU:(p + 1) * TU], mv[:, p * TU:(p + 1) * TU, 1], ACT.Sqrt, bias=eps5[:]).then_inc(s_sq, 1)

            @block.tensor
            def _(pe):
                pe.wait_ge(s_cst, 1)
                pe.wait_ge(s_dv, 1)
                for c in range(GC):
                    nc.tensor.transpose(ps_t[:, c, 0:NG], srcf[:, c::GC], ident[0:NG, 0:NG])
                for c in range(GC):
                    last = nc.tensor.transpose(ps_u[:, c, 0:NG], dstf[:, c::GC], ident[0:NG, 0:NG])
                last.then_inc(s_tr, 1)
                pe.wait_ge(s_end, 1)
                for c in range(2):
                    last = nc.tensor.matmul(ps_e[0:1, c * P:c * P + NG], ends[:, c:c + 1], ident[0:NG, 0:NG], start=True, stop=True)
                last.then_inc(s_rowp, 1)
                pe.wait_ge(s_row, 1)
                nc.tensor.matmul(ps_b[:, 0:NG], ones[0:1, :], endr[0:1, 0, :], start=True, stop=True).then_inc(s_bb, 1)
                pe.wait_ge(s_w, 16 * N_LOADS)
                at = 0
                for rows in (b1r0[:], b1r1[:], bmr[:], router_rows[:, 0:P], router_rows[:, P:D]):
                    n = rows.shape[0]
                    last = nc.tensor.transpose(ps_w[:, at:at + n], rows, ident[0:n, 0:n])
                    at += n
                last.then_inc(s_wt, 1)

            @block.vector
            def _(dve):
                dve.wait_ge(s_edges, 64)
                nc.vector.tensor_copy(srcf[:], srci[:])
                nc.vector.tensor_copy(dstf[:], dsti[:]).then_inc(s_dv, 1)
                dve.wait_ge(s_dv, 1)
                nc.vector.tensor_scalar(dlow[:], dstf[:], 0.0, FAR, ALU.is_lt, ALU.mult).then_inc(s_dv, 1)
                dve.wait_ge(s_dv, 2)
                nc.vector.tensor_tensor(dlow[:], dlow[:], dstf[:], ALU.add).then_inc(s_dv, 1)
                dve.wait_ge(s_dv, 3)
                nc.vector.tensor_reduce(ends[:, 0:1], dlow[:], AX_X, ALU.min)
                nc.vector.tensor_reduce(ends[:, 1:2], dstf[:], AX_X, ALU.max).then_inc(s_dv, 1)
                dve.wait_ge(s_dv, 4)
                nc.vector.tensor_scalar(ends[:, 0:1], ends[:, 0:1], float(NPAD), None, ALU.min).then_inc(s_dv, 1)
                dve.wait_ge(s_dv, 5)
                nc.vector.tensor_tensor(ends[:, 1:2], ends[:, 1:2], ends[:, 0:1], ALU.subtract).then_inc(s_end, 1)
                for p in range(IT + 1):
                    if p < IT:
                        dve.wait_ge(x_in[p], 16 if p < IT - 1 else 32)
                        for t in range(p * TU, p * TU + TU):
                            last = nc.vector.bn_stats(st[:, t, :], X[:, t, :])
                        last.then_inc(s_st, 1)
                        dve.wait_ge(s_st, p + 1)
                        for t in range(p * TU, p * TU + TU):
                            last = nc.vector.bn_aggr(mv[:, t, :], st[:, t, :])
                        last.then_inc(s_jo, 1)
                    if p > 0:
                        dve.wait_ge(s_sq, p)
                        nc.vector.reciprocal(rs[:, (p - 1) * TU:p * TU], rs[:, (p - 1) * TU:p * TU]).then_inc(s_rs, 1)
                        dve.wait_ge(s_rs, p)
                        for t in range((p - 1) * TU, p * TU):
                            last = nc.vector.tensor_scalar(NR[:, t, :], X[:, t, :], mv[:, t, 0:1], rs[:, t:t + 1], ALU.subtract, ALU.mult)
                        last.then_inc(s_nm, 1)
                dve.wait_ge(s_tr, 1)
                nc.vector.tensor_copy(src_tab[:].rearrange("p g c -> p c g"), ps_t[:, :, 0:NG])
                dve.wait_ge(s_rowp, 1)
                nc.vector.tensor_copy(endr[:], ps_e[0:1, 0:2 * P].rearrange("p (c g) -> p c g", c=2)[:, :, 0:NG]).then_inc(s_row, 1)
                dve.wait_ge(s_row, 1)
                nc.vector.tensor_copy(base_row[:], endr[0:1, 0, :])
                dve.wait_ge(s_pc, 1)
                nc.vector.tensor_copy(late[:], duei[0:1, 0:NG])
                nc.vector.tensor_reduce(endr[0:1, 1, 0:1], endr[0:1, 1, :], AX_X, ALU.max).then_inc(s_dv, 1)
                dve.wait_ge(s_dv, 6)
                nc.vector.tensor_scalar(wide_flag[:], endr[0:1, 1, 0:1], float(P), None, ALU.is_ge)
                nc.vector.tensor_scalar(endr[0:1, 1, 1:2], endr[0:1, 1, 0:1], float(P), None, ALU.is_ge)
                nc.vector.tensor_tensor(late[:], endr[0:1, 0, :], late[:], ALU.subtract).then_inc(s_fl, 1)
                dve.wait_ge(s_fl, 1)
                nc.vector.tensor_reduce(endr[0:1, 1, 2:3], late[:], AX_X, ALU.max).then_inc(s_fl, 1)
                dve.wait_ge(s_fl, 2)
                nc.vector.tensor_scalar(endr[0:1, 1, 2:3], endr[0:1, 1, 2:3], 0.0, endr[0:1, 1, 1:2], ALU.is_gt, ALU.max).then_inc(s_fl, 1)
                dve.wait_ge(s_fl, 3)
                nc.vector.tensor_copy(mixed_flag[:], endr[0:1, 1, 2:3])
                nc.vector.tensor_scalar(order_flag[:], endr[0:1, 1, 2:3], 0.5, None, ALU.is_lt)
                dve.wait_ge(s_bb, 1)
                nc.vector.tensor_copy(rel_tab[:, 0:NG, :].rearrange("p g c -> p c g"), ps_u[:, :, 0:NG]).then_inc(s_dv, 1)
                dve.wait_ge(s_dv, 7)
                nc.vector.tensor_tensor(rel_tab[:, 0:NG, :], rel_tab[:, 0:NG, :],
                                        ps_b[:, 0:NG].unsqueeze(2).to_broadcast([P, NG, GC]), ALU.subtract).then_inc(s_dv, 1)
                dve.wait_ge(s_wt, 1)
                at = 0
                for to in (b1_cols0[:], b1_cols1[:], b_mlp[:].rearrange("p l k -> p (l k)"), aggr_cols[:].rearrange("p l k -> p (l k)"), gate_w1[:, 0, :], gate_w1[:, 1, :]):
                    n = to.shape[1]
                    nc.vector.tensor_copy(to, ps_w[:, at:at + n])
                    at += n

        def when(eng, flag):
            return eng.If(eng.value_load(flag[0:1, 0:1], min_val=0, max_val=1) > 0)

        def segment_sums(tag, rows_dram, with_edges):
            halves = 3 if with_edges else 2
            with ExitStack() as c:
                G = sb(tag + "G", [P, GU, GC, D], F32, c)
                EA = sb(tag + "EA", [P, GU, GC, P], F32, c) if with_edges else None
                OH = sb(tag + "OH", [P, GU, GC, P], F32, c)
                idx = sb(tag + "idx", [P, GU, GC], I32, c)
                rel_s = sb(tag + "rel_s", [P, GC], F32, c)
                wbase = sb(tag + "wbase", [1, 1], I32, c)
                ps = pb(tag + "ps", [P, GU, 512], c)
                gathered = [held_sem(f"{tag}gathered{s}") for s in range(GU)]
                edges_in = [sem(f"{tag}edges_in{s}") for s in range(GU)]
                idx_ready, hot_ready, summed, added = (sem(tag + "idx_ready"), sem(tag + "hot_ready"),
                                                       sem(tag + "summed"), sem(tag + "added"))
                ones_set = sem(tag + "ones_set")
                w_idx, w_gath, w_edge, w_hot, w_sum, w_turn, w_rel = (sem(tag + "wide_idx"), held_sem(tag + "wide_gathered"), sem(tag + "wide_edges"),
                                                                     sem(tag + "wide_hot"), sem(tag + "wide_summed"), sem(tag + "wide_turn"), sem(tag + "wide_rel"))
                w_free = sem(tag + "wide_free")
                block = c.enter_context(nc.Block())

                def edge_rows(g):
                    return a["edge_attr_64"][ds(g * GE, GE), :].rearrange("(p c) f -> p c f", c=GC)

                edge_rows_last = a["edge_attr_64"][(NG - 1) * GE:E_N, :].rearrange("(p c) f -> p c f", c=GC)

                def in_loops(eng, body):
                    body(0, True)
                    with eng.Fori(1, GI) as i:
                        body(i, False)

                def wide_groups(eng, group, window=None):
                    with eng.If(eng.value_load(wide_flag[0:1, 0:1], min_val=0, max_val=1) > 0):
                        with eng.Fori(0, NG) as g:
                            group(g)
                            if window:
                                with eng.Fori(1, T) as w:
                                    window(g, w, g * (T - 1) + w)

                if with_edges:
                    @block.sync
                    def _(sp):
                        with when(sp, mixed_flag):
                            def body(i, first, last=False):
                                for s in range(GU):
                                    if not first:
                                        sp.wait_ge(summed, i * GU + s + 1 - GU)
                                    if last and s == GU - 1:
                                        sp.dma_start(EA[0:P_LAST, s, :, 0:DE], edge_rows_last).then_inc(edges_in[s], 16)
                                    else:
                                        sp.dma_start(EA[:, s, :, 0:DE], edge_rows(i * GU + s)).then_inc(edges_in[s], 16)

                            body(0, True)
                            with sp.Fori(1, GI - 1) as i:
                                body(i, False)
                            body(GI - 1, False, True)

                        with sp.If(sp.value_load(wide_flag[0:1, 0:1], min_val=0, max_val=1) > 0):
                            sp.wait_ge(summed, NG)
                            sp.dma_start(EA[:, 0, :, 0:DE], edge_rows(0)).then_inc(w_edge, 16)
                            with sp.Fori(1, NG - 1) as g:
                                sp.wait_ge(w_sum, g * (T - 1))
                                sp.dma_start(EA[:, 0, :, 0:DE], edge_rows(g)).then_inc(w_edge, 16)
                            sp.wait_ge(w_sum, (NG - 1) * (T - 1))
                            sp.dma_start(EA[0:P_LAST, 0, :, 0:DE], edge_rows_last).then_inc(w_edge, 16)

                @block.gpsimd
                def _(pool):
                    with when(pool, mixed_flag):
                        def body(i, first):
                            for s in range(GU):
                                hold(pool, "pool", idx_ready, i * GU + s + 1)
                                for k in range(GC):
                                    pool.indirect_dma_start(out=G[:, s, k, :], out_offset=None, in_=rows_dram,
                                                            in_offset=bass.IndirectOffsetOnAxis(ap=idx[:, s, k:k + 1], axis=0)
                                                            ).then_inc(gathered[s], 16)

                        in_loops(pool, body)

                        def wide(g):
                            hold(pool, "pool", w_idx, g + 1)
                            for k in range(GC):
                                pool.indirect_dma_start(out=G[:, 0, k, :], out_offset=None, in_=rows_dram,
                                                        in_offset=bass.IndirectOffsetOnAxis(ap=idx[:, 0, k:k + 1], axis=0)
                                                        ).then_inc(w_gath, 16)

                    wide_groups(pool, wide)

                @block.scalar
                def _(act):
                    with when(act, mixed_flag):
                        def body(i, first):
                            for s in range(GU):
                                if not first:
                                    act.wait_ge(summed, i * GU + s + 1 - GU)
                                nc.scalar.activation(idx[:, s, :], src_tab[:, ds(i * GU + s, 1), :].rearrange("p a c -> p (a c)"),
                                                     ACT.Copy).then_inc(idx_ready, 1)

                        in_loops(act, body)

                        def wide(g):
                            act.wait_ge(w_free, g + 1)
                            nc.scalar.activation(idx[:, 0, :], src_tab[:, ds(g, 1), :].rearrange("p a c -> p (a c)"),
                                                 ACT.Copy).then_inc(w_idx, 1)

                    wide_groups(act, wide)

                def products(pe, s):
                    for h in range(halves):
                        for k in range(GC):
                            rows = EA[:, s, k, :] if h == 2 else G[:, s, k, h * P:(h + 1) * P]
                            last = nc.tensor.matmul(ps[:, s, h * P:(h + 1) * P], rows, OH[:, s, k, :],
                                                    start=(k == 0), stop=(k == GC - 1))
                    return last

                @block.tensor
                def _(pe):
                    with when(pe, mixed_flag):
                        if with_edges:
                            pe.wait_ge(ones_set, 1)

                        def body(i, first):
                            for s in range(GU):
                                pe.wait_ge(hot_ready, i * GU + s + 1)
                                if with_edges:
                                    pe.wait_ge(edges_in[s], (i + 1) * 16)
                                pe.wait_ge(gathered[s], (i + 1) * 16 * GC)
                                if not first:
                                    pe.wait_ge(added, i * GU + s + 1 - GU)
                                products(pe, s).then_inc(summed, 1)

                        in_loops(pe, body)

                        def wide(g):
                            if with_edges:
                                pe.wait_ge(w_edge, (g + 1) * 16)
                            hold(pe, "pe", w_gath, (g + 1) * 16 * GC)

                        def window(g, w, n):
                            pe.wait_ge(w_hot, n)
                            products(pe, 0).then_inc(w_sum, 1)

                    wide_groups(pe, wide, window)

                @block.vector
                def _(dve):
                    with when(dve, mixed_flag):
                        iota_b = iota_w[:].unsqueeze(1).to_broadcast([P, GC, P])

                        def hot(g, s):
                            return nc.vector.tensor_tensor(
                                OH[:, s, :, :], iota_b,
                                rel_tab[:, ds(g, 1), :].rearrange("p a c -> p (a c)").unsqueeze(2).to_broadcast([P, GC, P]), ALU.is_equal)

                        def add(base, s):
                            window = sumT[:, 0:halves, ds(base, P)]
                            return nc.vector.tensor_tensor(window, window,
                                                           ps[:, s, 0:halves * P].rearrange("p (h w) -> p h w", h=halves), ALU.add)

                        def body(i, first):
                            for s in range(GU):
                                if not (first and s < GU - 1):
                                    dve.wait_ge(summed, i * GU + s + 2 - GU)
                                hot(i * GU + s + 1, (s + 1) % GU).then_inc(hot_ready, 1)
                                base = dve.value_load(base_row[0:1, ds(i * GU + s, 1)], min_val=0, max_val=NPAD)
                                dve.wait_ge(summed, i * GU + s + 1)
                                if not (first and s == 0):
                                    dve.wait_ge(added, i * GU + s)
                                add(base, s).then_inc(added, 1)

                        hot(0, 0).then_inc(hot_ready, 1)
                        if with_edges:
                            nc.vector.memset(EA[:, :, :, DE:P], 1.0).then_inc(ones_set, 1)
                        in_loops(dve, body)

                        def wide(g):
                            dve.sem_inc(w_free, 1)

                        def window(g, w, n):
                            dve.wait_ge(w_turn, n)
                            rel_g = rel_tab[:, ds(g, 1), :].rearrange("p a c -> p (a c)")
                            nc.vector.tensor_scalar(rel_s[:], rel_g, win_off[:, ds(w, 1)], None, ALU.subtract)
                            nc.vector.tensor_scalar(wbase[:], base_row[0:1, ds(g, 1)], win_off[0:1, ds(w, 1)], float(NPAD),
                                                    ALU.add, ALU.min).then_inc(w_rel, 1)
                            dve.wait_ge(w_rel, n)
                            nc.vector.tensor_tensor(OH[:, 0, :, :], iota_b, rel_s[:].unsqueeze(2).to_broadcast([P, GC, P]),
                                                    ALU.is_equal).then_inc(w_hot, 1)
                            base = dve.value_load(wbase[0:1, 0:1], min_val=0, max_val=NPAD)
                            dve.wait_ge(w_sum, n)
                            add(base, 0).then_inc(w_turn, 1)

                        dve.wait_ge(added, NG)
                        dve.wait_ge(hot_ready, NG + 1)
                        dve.sem_inc(w_turn, 1)
                    wide_groups(dve, wide, window)

        def tile_of(t3, t):
            return t3[:, ds(t, 1), :].rearrange("p a d -> p (a d)")

        def rows_of(dram, t):
            return dram[ds(t * P, P), :]

        def turn2(ps_cols, rows, ready):
            for k in range(K2):
                last = nc.tensor.transpose(ps_cols[:, k * P:(k + 1) * P], rows[:, k * P:(k + 1) * P], ident[:])
            last.then_inc(ready, 1)

        def tile_steps(eng, step, most, peeled=1):
            def turn(i, u):
                def at(lag, with_round=False):
                    t = i * TU + u - lag
                    if isinstance(t, int) and not 0 <= t < T:
                        return None
                    return (t, (u - lag) % TU, i + (u - lag) // TU) if with_round else (t, (u - lag) % TU)
                step(at)

            for i in range(peeled):
                for u in range(TU):
                    turn(i, u)
            with eng.Fori(peeled, IT) as i:
                for u in range(TU):
                    turn(i, u)
            for u in range(most):
                turn(IT, u)

        def tile_steps_back(eng, step, most):
            def turn(i, u, down=None):
                def at(lag, with_round=False):
                    t = turn_of(i, down, u - lag)
                    if isinstance(t.n, int) and not 0 <= t.n < T:
                        return None
                    return (t, (u - lag) % TU, i + (u - lag) // TU) if with_round else (t, (u - lag) % TU)
                step(at)

            for i in range(2):
                for u in range(TU):
                    turn(i, u)
            with eng.Fori(2, IT) as i:
                down = eng.value_load(iterations_left[0:1, ds(i, 1)], min_val=0, max_val=IT - 3)
                for u in range(TU):
                    turn(i, u, down)
            for u in range(most):
                turn(IT, u)

        def wait_tile(eng, semaphore, t, ago=0, per=1):
            n = ((t.n if isinstance(t, Turn) else t) + 1 - ago) * per
            if not (isinstance(n, int) and n <= 0):
                eng.wait_ge(semaphore, n)

        def hold_tile(eng, name, semaphore, t, ago=0, per=1):
            n = ((t.n if isinstance(t, Turn) else t) + 1 - ago) * per
            if not (isinstance(n, int) and n <= 0):
                hold(eng, name, semaphore, n)

        class Stores:

            def __init__(self, tag):
                self.free = [sem(f"{tag}slot_stored{u}") for u in range(TU)]

            def begin(self, sp):
                for u in range(TU):
                    sp.sem_inc(self.free[u], 16)

            def wait_free(self, eng, s, r):
                eng.wait_ge(self.free[s], (r + 1) * 16)

            def hold_free(self, name, eng, s, r):
                hold(eng, name, self.free[s], (r + 1) * 16)

            def store(self, sp, out, rows, s):
                sp.dma_start(out, rows).then_inc(self.free[s], 16)

            def wait_all(self, sp):
                for u in range(TU):
                    sp.wait_ge(self.free[u], (T // TU + 1) * 16)

        class Norm:

            def __init__(self, tag, c, eps):
                self.st, self.mv = sb(tag + "st", [P, TU, 6], F32, c), sb(tag + "mv", [P, TU, 2], F32, c)
                self.rs = sb(tag + "rs", [P, TU], F32, c)
                self.stats, self.joined, self.dev, self.inv = (
                    sem(tag + "stats_taken"), sem(tag + "stats_joined"), sem(tag + "deviation"), sem(tag + "deviation_inverse"))
                self.eps = eps

            def take(self, dve, t, s, rows, written):
                self.take_stats(dve, t, s, rows, written)
                self.join_stats(dve, t, s)

            def take_stats(self, dve, t, s, rows, written):
                hold_tile(dve, "dve", written, t)
                nc.vector.bn_stats(self.st[:, s, :], rows).then_inc(self.stats, 1)

            def join_stats(self, dve, t, s):
                hold_tile(dve, "dve", self.stats, t)
                nc.vector.bn_aggr(self.mv[:, s, :], self.st[:, s, :]).then_inc(self.joined, 1)

            def deviation(self, act, t, s):
                wait_tile(act, self.joined, t)
                nc.scalar.activation(self.rs[:, s:s + 1], self.mv[:, s, 1:2], ACT.Sqrt, bias=self.eps).then_inc(self.dev, 1)

            def invert(self, dve, t, s):
                wait_tile(dve, self.dev, t)
                nc.vector.reciprocal(self.rs[:, s:s + 1], self.rs[:, s:s + 1]).then_inc(self.inv, 1)
                wait_tile(dve, self.inv, t)

            def mean(self, s):
                return self.mv[:, s, 0:1]

            def inverse(self, s):
                return self.rs[:, s:s + 1]

        class Turn:

            def __init__(self, n, node):
                self.n, self.node = n, node

        def node_tile(t):
            return t.node

        def turn_of(i, down, e):
            n = i * TU + e
            return Turn(n, T - 1 - n) if isinstance(n, int) else Turn(n, down * TU + (TU - 1 - e))

        class Sums:

            def __init__(self, tag, c, rows_dram, with_edges):
                self.rows_dram, self.with_edges, self.halves = rows_dram, with_edges, 3 if with_edges else 2
                self.G = sb(tag + "G", [P, GS, GC, D], F32, c)
                self.EA = sb(tag + "EA", [P, GS, GC, P], F32, c) if with_edges else None
                self.OH = sb(tag + "OH", [P, GS, GC, P], F32, c)
                self.idx = sb(tag + "idx", [P, GS, GC], I32, c)
                self.ps = [pb(f"{tag}ps_sums{b}", [P, 512], c) for b in range(2)]
                self.gathered = [held_sem(f"{tag}gathered{s}") for s in range(GS)]
                self.edges_in = [sem(f"{tag}edges_in{s}") for s in range(GS)]
                self.idx_ready, self.hot_ready, self.summed, self.added, self.ones_set = (
                    sem(tag + n) for n in ("idx_ready", "hot_ready", "summed", "added", "ones_set"))

            def wait_group(self, eng, semaphore, o, ago=0):
                n = o + 1 - ago
                if not (isinstance(n, int) and n <= 0):
                    eng.wait_ge(semaphore, n)

            def load_edges(self, sp, o, g, s, r):
                self.wait_group(sp, self.summed, o, GS)
                if isinstance(g, int) and g == NG - 1:
                    to, rows = self.EA[0:P_LAST, s, :, 0:DE], a["edge_attr_64"][g * GE:E_N, :]
                else:
                    to, rows = self.EA[:, s, :, 0:DE], a["edge_attr_64"][ds(g * GE, GE), :]
                sp.dma_start(to, rows.rearrange("(p c) f -> p c f", c=GC)).then_inc(self.edges_in[s], 16)

            def indices(self, act, o, g, s, r):
                self.wait_group(act, self.summed, o, GS)
                nc.scalar.activation(self.idx[:, s, :], src_tab[:, ds(g, 1), :].rearrange("p a c -> p (a c)"), ACT.Copy).then_inc(self.idx_ready, 1)

            def gather(self, pool, o, g, s, r):
                hold(pool, "pool", self.idx_ready, o + 1)
                for k in range(GC):
                    pool.indirect_dma_start(out=self.G[:, s, k, :], out_offset=None, in_=self.rows_dram,
                                            in_offset=bass.IndirectOffsetOnAxis(ap=self.idx[:, s, k:k + 1], axis=0)
                                            ).then_inc(self.gathered[s], 16)

            def products(self, pe, o, g, s, r):
                pe.wait_ge(self.hot_ready, o + 1)
                if self.with_edges:
                    pe.wait_ge(self.edges_in[s], (r + 1) * 16)
                pe.wait_ge(self.gathered[s], (r + 1) * 16 * GC)
                self.wait_group(pe, self.added, o, 2)
                for h in range(self.halves):
                    for k in range(GC):
                        rows = self.EA[:, s, k, :] if h == 2 else self.G[:, s, k, h * P:(h + 1) * P]
                        last = nc.tensor.matmul(self.ps[s % 2][:, h * P:(h + 1) * P], rows, self.OH[:, s, k, :],
                                                start=(k == 0), stop=(k == GC - 1))
                last.then_inc(self.summed, 1)

            def hot(self, g, s):
                nc.vector.tensor_tensor(
                    self.OH[:, s, :, :], iota_w[:].unsqueeze(1).to_broadcast([P, GC, P]),
                    rel_tab[:, ds(g, 1), :].rearrange("p a c -> p (a c)").unsqueeze(2).to_broadcast([P, GC, P]),
                    ALU.is_equal).then_inc(self.hot_ready, 1)

            def add(self, dve, o, g, s, r):
                if not (isinstance(o, int) and o + 1 == NG):
                    self.wait_group(dve, self.summed, o + 1, GS)
                    self.hot(g - 1, (s + 1) % GS)
                base = dve.value_load(base_row[0:1, ds(g, 1)], min_val=0, max_val=NPAD)
                dve.wait_ge(self.summed, o + 1)
                self.wait_group(dve, self.added, o, 1)
                window = sumT[:, 0:self.halves, ds(base, P)]
                nc.vector.tensor_tensor(window, window, self.ps[s % 2][:, 0:self.halves * P].rearrange("p (h w) -> p h w", h=self.halves),
                                        ALU.add).then_inc(self.added, 1)

        def sums_and_nodes(tag, rows_dram, with_edges, Stage):
            with ExitStack() as c:
                sums, stage = Sums(tag, c, rows_dram, with_edges), Stage(tag, c)
                block = c.enter_context(nc.Block())

                def steps(eng, step, most):
                    def turn(i, u, down=None):
                        def at(lag, with_round=False):
                            e = u - LEAD - lag
                            t = turn_of(i, down, e)
                            if isinstance(t.n, int) and not 0 <= t.n < T:
                                return None
                            return (t, e % TU, i + e // TU) if with_round else (t, e % TU)

                        def group(work, q, lag):
                            o = (i * TU + u - lag) * GPS - SHORT + q
                            e = (u - lag) * GPS - SHORT + q
                            if isinstance(o, int):
                                g = NG - 1 - o
                            else:
                                g = down * (TU * GPS) + (NG - 1 - (IT - 1) * TU * GPS - e)
                            if not isinstance(o, int) or 0 <= o < NG:
                                work(eng, o, g, e % GS, i * (TU * GPS // GS) + e // GS)

                        def sums_in():
                            n = (i * TU + u) * GPS - SHORT
                            eng.wait_ge(sums.added, min(n, NG) if isinstance(n, int) else n)

                        step(at, group, sums_in)

                    for i in range(2):
                        for u in range(TU):
                            turn(i, u)
                    with eng.Fori(2, IT) as i:
                        down = eng.value_load(iterations_left[0:1, ds(i, 1)], min_val=0, max_val=IT - 3)
                        for u in range(TU):
                            turn(i, u, down)
                    for u in range(most):
                        turn(IT, u)

                @block.sync
                def _(sp):
                    with when(sp, order_flag):
                        def step(at, group, sums_in):
                            if with_edges:
                                for q in range(GPS):
                                    group(sums.load_edges, q, 1)
                            stage.store_rows(sp, at)

                        stage.n_stores.begin(sp)
                        if with_edges:
                            sp.wait_ge(sums.ones_set, 1)
                        steps(sp, step, LEAD + 5)
                        stage.n_stores.wait_all(sp)

                @block.gpsimd
                def _(pool):
                    with when(pool, order_flag):
                        def step(at, group, sums_in):
                            for q in range(GPS):
                                group(sums.gather, q, 0)

                        steps(pool, step, 0)

                @block.scalar
                def _(act):
                    with when(act, order_flag):
                        steps(act, lambda at, group, sums_in: stage.act(act, at, lambda q: group(sums.indices, q, 0), sums_in), LEAD + 5)

                @block.tensor
                def _(pe):
                    with when(pe, order_flag):
                        if with_edges:
                            pe.wait_ge(sums.ones_set, 1)
                        steps(pe, lambda at, group, sums_in: stage.pe(pe, at, lambda q: group(sums.products, q, 1)), LEAD + 5)

                @block.vector
                def _(dve):
                    with when(dve, order_flag):
                        sums.hot(NG - 1, 0)
                        if with_edges:
                            nc.vector.memset(sums.EA[:, 0, :, 0:DE], 0.0)
                            nc.vector.memset(sums.EA[:, :, :, DE:P], 1.0).then_inc(sums.ones_set, 1)
                        steps(dve, lambda at, group, sums_in: stage.dve(dve, at, lambda q: group(sums.add, q, 1)), LEAD + 5)
                        stage.finish(dve)

        def nodes_alone(tag, Stage):
            def nothing(*_):
                pass

            with ExitStack() as c:
                stage = Stage(tag, c)
                block = c.enter_context(nc.Block())

                @block.sync
                def _(sp):
                    with when(sp, mixed_flag):
                        stage.n_stores.begin(sp)
                        tile_steps_back(sp, lambda at: stage.store_rows(sp, at), 5)
                        stage.n_stores.wait_all(sp)

                @block.scalar
                def _(act):
                    with when(act, mixed_flag):
                        tile_steps_back(act, lambda at: stage.act(act, at, nothing, nothing), 5)

                @block.tensor
                def _(pe):
                    with when(pe, mixed_flag):
                        tile_steps_back(pe, lambda at: stage.pe(pe, at, nothing), 5)

                @block.vector
                def _(dve):
                    with when(dve, mixed_flag):
                        tile_steps_back(dve, lambda at: stage.dve(dve, at, nothing), 5)
                        stage.finish(dve)

        class NodeMlp:
            def __init__(self, tag, c):
                self.lhs = sb(tag + "lhs", [P, TU, 3, P], F32, c)
                self.H = sb(tag + "H", [P, TU, D], F32, c)
                self.hT = sb(tag + "hT", [P, TU, K2, P], F32, c)
                self.yT = sb(tag + "yT", [P, K2, P], F32, c)
                self.Z = sb(tag + "Z", [P, D], F32, c)
                self.N2 = sb(tag + "N2", [P, TU, D], F32, c)
                self.nT = sb(tag + "nT", [P, K2, P], F32, c)
                self.ps_agg, self.ps_tn, self.ps_0, self.ps_1, self.ps_2, self.ps_bg = (
                    pb(f"{tag}ps_{n}", [P, 512], c) for n in ("agg", "turned", "0", "1", "2", "back"))
                self.h_norm, self.z_norm, self.x_norm = (
                    Norm(tag + "nh", c, eps6[:]), Norm(tag + "nz", c, eps6[:]), Norm(tag + "nx", c, eps5[:]))
                self.S = {n: sem(tag + n) for n in (
                    "lhs_ready", "agg_done", "hpre", "h_ready", "turned", "hT_ready", "first", "relu0", "added0", "second", "relu1",
                    "added1", "third", "added2", "back", "z_ready", "centred", "scaled", "x_ready", "n2_ready", "n_turned",
                    "nT_ready", "logits", "logits_in")}
                self.n_stores = Stores(tag)

            def act(self, act, at, group, sums_in):
                S, yT = self.S, self.yT

                def relu(l, ps_l, t, done):
                    if l == 0:
                        wait_tile(act, S["added1"], t, 1)
                    else:
                        wait_tile(act, S["added0"], t)
                    for m in range(K2):
                        last = nc.scalar.activation(yT[:, m, :], ps_l[:, m * P:(m + 1) * P], ACT.Relu, bias=b_mlp[:, l, m:m + 1])
                    last.then_inc(done, 1)

                if x := at(5):
                    self.x_norm.deviation(act, *x)
                if x := at(1):
                    self.h_norm.deviation(act, *x)
                if x := at(2):
                    t, s = x
                    wait_tile(act, S["turned"], t)
                    for k in range(K2):
                        last = nc.scalar.activation(self.hT[:, s, k, :], self.ps_tn[:, k * P:(k + 1) * P], ACT.Identity,
                                                    bias=aggr_cols[:, 1, k:k + 1], scale=aggr_cols[:, 0, k:k + 1])
                    last.then_inc(S["hT_ready"], 1)
                group(0)
                if x := at(2):
                    wait_tile(act, S["first"], x[0])
                    relu(0, self.ps_0, x[0], S["relu0"])
                group(1)
                if x := at(4):
                    self.z_norm.deviation(act, *x)
                if x := at(5):
                    t, s = x
                    wait_tile(act, S["n_turned"], t)
                    nc.scalar.activation(self.nT[:].rearrange("p k n -> p (k n)"), self.ps_tn[:, 0:D], ACT.Copy).then_inc(S["nT_ready"], 1)
                group(2)
                if x := at(2):
                    wait_tile(act, S["second"], x[0])
                    relu(1, self.ps_1, x[0], S["relu1"])
                group(3)
                if x := at(0):
                    t, s = x
                    sums_in()
                    wait_tile(act, S["agg_done"], t, TU)
                    nc.scalar.activation(self.lhs[:, s, :, :], sumT[:, :, ds(node_tile(t) * P, P)], ACT.Copy).then_inc(S["lhs_ready"], 1)

            def pe(self, pe, at, group):
                S, hT = self.S, self.hT

                def layer(l, ps_l, s, done):
                    for m in range(K2):
                        for k in range(K2):
                            last = nc.tensor.matmul(ps_l[:, m * P:(m + 1) * P], w_mlp[:, l, k, m * P:(m + 1) * P],
                                                    hT[:, s, k, :], start=(k == 0), stop=(k == K2 - 1))
                    last.then_inc(done, 1)

                if x := at(2):
                    t, s = x
                    wait_tile(pe, S["h_ready"], t)
                    wait_tile(pe, S["hT_ready"], t, 1)
                    turn2(self.ps_tn, self.H[:, s, :], S["turned"])
                group(0)
                if x := at(4):
                    t, s = x
                    wait_tile(pe, S["added2"], t)
                    wait_tile(pe, S["z_ready"], t, 1)
                    wait_tile(pe, S["logits_in"], t, 2)
                    for k in range(K2):
                        last = nc.tensor.transpose(self.ps_bg[:, k * P:(k + 1) * P], hT[:, s, k, :], ident[:])
                    last.then_inc(S["back"], 1)
                if x := at(2):
                    t, s = x
                    wait_tile(pe, S["hT_ready"], t)
                    wait_tile(pe, S["relu0"], t, 1)
                    layer(0, self.ps_0, s, S["first"])
                group(1)
                if x := at(3):
                    t, s = x
                    wait_tile(pe, S["added1"], t)
                    wait_tile(pe, S["added2"], t, 1)
                    layer(2, self.ps_2, s, S["third"])
                if x := at(5):
                    t, s = x
                    wait_tile(pe, S["n2_ready"], t)
                    wait_tile(pe, S["nT_ready"], t, 1)
                    turn2(self.ps_tn, self.N2[:, s, :], S["n_turned"])
                group(2)
                if x := at(2):
                    t, s = x
                    wait_tile(pe, S["added0"], t)
                    wait_tile(pe, S["relu1"], t, 1)
                    layer(1, self.ps_1, s, S["second"])
                if x := at(5):
                    t, s = x
                    wait_tile(pe, S["nT_ready"], t)
                    wait_tile(pe, S["logits_in"], t, 1)
                    wait_tile(pe, S["z_ready"], at(4)[0] if at(4) else t)
                    for k in range(K2):
                        last = nc.tensor.matmul(self.ps_bg[:, 0:E0], self.nT[:, k, :], gate_w0[:, k, :], start=(k == 0), stop=(k == K2 - 1))
                    last.then_inc(S["logits"], 1)
                group(3)
                if x := at(0):
                    t, s = x
                    lhs, ps_agg = self.lhs, self.ps_agg
                    wait_tile(pe, S["lhs_ready"], t)
                    wait_tile(pe, S["hpre"], t, 1)
                    for k in range(K2):
                        nc.tensor.matmul(ps_agg[:, 0:D], lhs[:, s, k, :], w_nodes[:, k, :], start=(k == 0), stop=False)
                    nc.tensor.matmul(ps_agg[:, 0:D], lhs[0:DE, s, 2, :], w_edges[:], start=False, stop=True)
                    nc.tensor.matmul(ps_agg[:, D:D + 1], lhs[:, s, 2, :], ident[:, DE:DE + 1], start=True, stop=True).then_inc(S["agg_done"], 1)

            def dve(self, dve, at, group):
                S, H, Z, hT = self.S, self.H, self.Z, self.hT
                h_norm, z_norm, x_norm = self.h_norm, self.z_norm, self.x_norm
                x0, x1, x2, x3, x4, x5 = at(0), at(1), at(2), at(3), at(4), at(5, True)

                def add_skip(t, s, ready, done):
                    wait_tile(dve, ready, t)
                    nc.vector.tensor_tensor(hT[:, s, :, :], hT[:, s, :, :], self.yT[:], ALU.add).then_inc(done, 1)

                if x5:
                    t5, s5, r = x5
                    x_norm.invert(dve, t5, s5)
                if x1:
                    h_norm.invert(dve, *x1)
                if x5:
                    self.n_stores.wait_free(dve, s5, r)
                    nc.vector.tensor_scalar(self.N2[:, s5, :], tile_of(X, node_tile(t5)), x_norm.mean(s5), x_norm.inverse(s5),
                                            ALU.subtract, ALU.mult).then_inc(S["n2_ready"], 1)
                if x1:
                    t, s = x1
                    nc.vector.tensor_scalar(H[:, s, :], H[:, s, :], h_norm.mean(s), h_norm.inverse(s),
                                            ALU.subtract, ALU.mult).then_inc(S["h_ready"], 1)
                group(0)
                if x4:
                    t, s = x4
                    wait_tile(dve, S["back"], t)
                    nc.vector.tensor_tensor(Z[:], self.ps_bg[:, 0:D], tile_of(NR, node_tile(t)), ALU.add).then_inc(S["z_ready"], 1)
                if x2:
                    add_skip(*x2, S["relu0"], S["added0"])
                if x4:
                    z_norm.take_stats(dve, t, s, Z[:], S["z_ready"])
                group(1)
                if x4:
                    z_norm.join_stats(dve, t, s)
                if x3:
                    t3, s3 = x3
                    wait_tile(dve, S["third"], t3)
                    for m in range(K2):
                        last = nc.vector.scalar_tensor_tensor(hT[:, s3, m, :], self.ps_2[:, m * P:(m + 1) * P], b_mlp[:, 2, m:m + 1],
                                                              hT[:, s3, m, :], ALU.add, ALU.add)
                    last.then_inc(S["added2"], 1)
                if x4:
                    wait_tile(dve, z_norm.joined, t)
                    nc.vector.scalar_tensor_tensor(Z[:], Z[:], z_norm.mean(s), OUT_S, ALU.subtract, ALU.mult).then_inc(S["centred"], 1)
                group(2)
                if x4:
                    z_norm.invert(dve, t, s)
                    wait_tile(dve, S["centred"], t)
                    nc.vector.scalar_tensor_tensor(Z[:], Z[:], z_norm.inverse(s), OUT_B, ALU.mult, ALU.add).then_inc(S["scaled"], 1)
                if x5:
                    wait_tile(dve, S["logits"], t5)
                    nc.vector.tensor_tensor(tile_of(logit0, node_tile(t5)), self.ps_bg[:, 0:E0], gate_b0[:], ALU.add).then_inc(S["logits_in"], 1)
                if x4:
                    wait_tile(dve, S["scaled"], t)
                    nc.vector.tensor_tensor(tile_of(X, node_tile(t)), tile_of(X, node_tile(t)), Z[:], ALU.add).then_inc(S["x_ready"], 1)
                if x2:
                    add_skip(*x2, S["relu1"], S["added1"])
                group(3)
                if x4:
                    x_norm.take_stats(dve, t, s, tile_of(X, node_tile(t)), S["x_ready"])
                if x0:
                    t0, s0 = x0
                    wait_tile(dve, S["agg_done"], t0)
                    nc.vector.scalar_tensor_tensor(H[:, s0, :], self.ps_agg[:, 0:D], 0.0, tile_of(NR, node_tile(t0)), ALU.max, ALU.add)
                    nc.vector.tensor_scalar(deg_inv[:, ds(node_tile(t0), 1)], self.ps_agg[:, D:D + 1], 1.0, None, ALU.max).then_inc(S["hpre"], 1)
                    h_norm.take_stats(dve, t0, s0, H[:, s0, :], S["hpre"])
                if x4:
                    x_norm.join_stats(dve, t, s)
                if x0:
                    h_norm.join_stats(dve, t0, s0)

            def store_rows(self, sp, at):
                if x := at(5):
                    t, s = x
                    wait_tile(sp, self.S["n2_ready"], t)
                    self.n_stores.store(sp, rows_of(token_dram, node_tile(t)), self.N2[:, s, :], s)

            def finish(self, dve):
                dve.wait_ge(self.S["hpre"], T)
                nc.vector.reciprocal(deg_inv[:], deg_inv[:])

        def route(tag, E, NB, logits, of_probs):
            with ExitStack() as c:
                hot = sb(tag + "hot", [P, 2, T, E], F32, c)
                both = sb(tag + "both", [P, T, E], F32, c)
                tot = sb(tag + "tot", [P, E, T], F32, c)
                inc = sb(tag + "inc", [P, E, T], F32, c)
                fresh = sb(tag + "fresh", [P, E, T], F32, c)
                cnt_i = sb(tag + "cnt_i", [P, E], I32, c)
                cnt = sb(tag + "cnt", [P, E], F32, c)
                end = sb(tag + "end", [P, E], F32, c)
                iota_e = sb(tag + "iota_e", [P, E], F32, c)
                at_e = sb(tag + "at", [P, T, E], F32, c)
                tmp = sb(tag + "tmp", [P, T, E], F32, c)
                v8 = sb(tag + "v8", [P, T, 8], F32, c)
                i8 = sb(tag + "i8", [P, T, 8], U32, c)
                top_idx = sb(tag + "top_idx", [P, T, 2], F32, c)
                rowf = sb(tag + "rowf", [P, T, 2], F32, c)
                part_i = sb(tag + "part_i", [P, 2, T, 2], I32, c)
                part = sb(tag + "part", [P, 2, T, 2], F32, c)
                in_block = sb(tag + "in_block", [P, TU, 2, NB], F32, c)
                in_place = sb(tag + "in_place", [P, 2, TU, 2, P], F32, c)
                named = sb(tag + "named", [P, 2, TU, 2, NB], F32, c)
                tok_f = sb(tag + "tok_f", [NB, P], F32, c)
                iota_bk = sb(tag + "iota_bk", [P, NB], F32, c)
                blk_ge = sb(tag + "blk_ge", [1, NB, E], F32, c)
                blk_f = sb(tag + "blk_f", [1, NB], F32, c)
                ii = sb(tag + "ii", [P, NB], I32, c)
                e1 = sb(tag + "e1", [P, T], F32, c)
                e2 = sb(tag + "e2", [P, T], F32, c)
                ps_b = pb(tag + "ps_before", [P, 512], c)
                ps_a = pb(tag + "ps_all", [P, 512], c)
                ps_n = pb(tag + "ps_token", [P, 512], c)
                ps_c = pb(tag + "ps_turned", [P, 512], c)
                s_c, s_h, s_p, s_d, s_less, s_exp = (sem(tag + "consts"), sem(tag + "hot_ready"), sem(tag + "counted"),
                                                     sem(tag + "dve_chain"), sem(tag + "differences"), sem(tag + "exp"))
                s_pc, s_named, s_mm, s_tok, s_turned = (sem(tag + n) for n in ("pool_chain", "named", "placed", "tokens", "turned"))
                block = c.enter_context(nc.Block())
                TE = T * E

                @block.gpsimd
                def _(pool):
                    nc.gpsimd.iota(ii[:], [[1, NB]], base=0, channel_multiplier=0)
                    nc.gpsimd.memset(fresh[:], 1.0).then_inc(s_pc, 1)
                    pool.wait_ge(s_pc, 1)
                    nc.gpsimd.tensor_copy(iota_e[:], ii[:, 0:E])
                    nc.gpsimd.tensor_copy(iota_bk[:], ii[:])
                    nc.gpsimd.memset(fresh[:, :, 0], 0.0).then_inc(s_c, 1)

                @block.tensor
                def _(pe):
                    pe.wait_ge(s_h, 1)
                    nc.tensor.matmul(ps_b[:, 0:TE], before[:], both[:].rearrange("p t e -> p (t e)"), start=True, stop=True)
                    nc.tensor.matmul(ps_a[:, 0:TE], ones[:], both[:].rearrange("p t e -> p (t e)"), start=True, stop=True).then_inc(s_p, 1)
                    for i in range(IT):
                        pe.wait_ge(s_named, i + 1)
                        for u in range(TU):
                            for k in range(2):
                                last = nc.tensor.matmul(ps_n[0:NB, 0:P], named[:, i % 2, u, k, :], in_place[:, i % 2, u, k, :],
                                                        start=(i == u == k == 0), stop=(i == IT - 1 and u == TU - 1 and k == 1))
                        last.then_inc(s_mm, 1)
                    pe.wait_ge(s_tok, 1)
                    nc.tensor.transpose(ps_c[:, 0:NB], tok_f[:], ident[0:NB, 0:NB]).then_inc(s_turned, 1)

                @block.scalar
                def _(act):
                    act.wait_ge(s_less, 1)
                    if of_probs:
                        nc.scalar.activation(logits[:], logits[:], ACT.Exp).then_inc(s_exp, 1)
                    else:
                        nc.scalar.activation(e1[:], e1[:], ACT.Exp).then_inc(s_exp, 1)

                @block.vector
                def _(dve):
                    n = [0]

                    def link(ins):
                        n[0] += 1
                        ins.then_inc(s_d, 1)
                        dve.wait_ge(s_d, n[0])

                    if of_probs:
                        link(nc.vector.tensor_reduce(e1[:], logits[:], AX_X, ALU.max))
                        nc.vector.tensor_tensor(logits[:], logits[:], e1[:].unsqueeze(2).to_broadcast([P, T, E]), ALU.subtract).then_inc(s_less, 1)
                        dve.wait_ge(s_exp, 1)
                        link(nc.vector.tensor_reduce(e1[:], logits[:], AX_X, ALU.add))
                        link(nc.vector.reciprocal(e2[:], e1[:]))
                        link(nc.vector.tensor_tensor(logits[:], logits[:], e2[:].unsqueeze(2).to_broadcast([P, T, E]), ALU.mult))
                    for t in range(T):
                        last = nc.vector.max(v8[:, t, :], logits[:, t, :])
                    link(last)
                    for t in range(T):
                        last = nc.vector.max_index(i8[:, t, :], v8[:, t, :], logits[:, t, :])
                    link(last)
                    if of_probs:
                        link(nc.vector.tensor_tensor(e1[:], v8[:, :, 1], v8[:, :, 0], ALU.add))
                        link(nc.vector.tensor_scalar(e1[:], e1[:], 1e-12, None, ALU.max))
                        link(nc.vector.reciprocal(e2[:], e1[:]))
                        nc.vector.tensor_tensor(top_w[:], v8[:, :, 0:2], e2[:].unsqueeze(2).to_broadcast([P, T, 2]), ALU.mult)
                    else:
                        nc.vector.tensor_tensor(e1[:], v8[:, :, 1], v8[:, :, 0], ALU.subtract).then_inc(s_less, 1)
                    link(nc.vector.tensor_tensor(top_idx[:], i8[:, :, 0:2], row_far[:].unsqueeze(2).to_broadcast([P, T, 2]), ALU.add))
                    dve.wait_ge(s_c, 1)
                    for k in range(2):
                        last = nc.vector.tensor_tensor(hot[:, k, :, :], iota_e[:].unsqueeze(1).to_broadcast([P, T, E]),
                                                       top_idx[:, :, k:k + 1].to_broadcast([P, T, E]), ALU.is_equal)
                    link(last)
                    nc.vector.tensor_tensor(both[:], hot[:, 0, :, :], hot[:, 1, :, :], ALU.add).then_inc(s_h, 1)
                    if not of_probs:
                        dve.wait_ge(s_exp, 1)
                        link(nc.vector.tensor_scalar(e2[:], e1[:], 1.0, None, ALU.add))
                        link(nc.vector.reciprocal(top_w[:, :, 0], e2[:]))
                        nc.vector.tensor_tensor(top_w[:, :, 1], top_w[:, :, 0], e1[:], ALU.mult)
                    dve.wait_ge(s_p, 1)
                    link(nc.vector.tensor_copy(tot[:], ps_a[:, 0:TE].rearrange("p (t e) -> p e t", e=E)))
                    link(nc.vector.tensor_tensor_scan(inc[:].rearrange("p e t -> p (e t)"), fresh[:].rearrange("p e t -> p (e t)"),
                                                      tot[:].rearrange("p e t -> p (e t)"), 0.0, ALU.mult, ALU.add))
                    link(nc.vector.tensor_scalar(cnt_i[:], inc[:, :, T - 1], float(P - 1), None, ALU.add))
                    link(nc.vector.tensor_scalar(cnt_i[:], cnt_i[:], 7, 7, ALU.arith_shift_right, ALU.logical_shift_left))
                    link(nc.vector.tensor_copy(cnt[:], cnt_i[:]))
                    link(nc.vector.tensor_tensor_scan(end[:], ones[:, 0:E], cnt[:], 0.0, ALU.mult, ALU.add))
                    link(nc.vector.tensor_tensor(cnt[:], end[:], cnt[:], ALU.subtract))
                    link(nc.vector.tensor_tensor(inc[:], inc[:], tot[:], ALU.subtract))
                    link(nc.vector.tensor_tensor(inc[:], inc[:], cnt[:].unsqueeze(2).to_broadcast([P, E, T]), ALU.add))
                    link(nc.vector.tensor_tensor(at_e[:], ps_b[:, 0:TE].rearrange("p (t e) -> p t e", e=E),
                                                 inc[:].rearrange("p e t -> p t e"), ALU.add))
                    for k in range(2):
                        link(nc.vector.tensor_tensor(tmp[:], hot[:, k, :, :], at_e[:], ALU.mult))
                        link(nc.vector.tensor_reduce(rowf[:, :, k], tmp[:], AX_X, ALU.add))
                    link(nc.vector.tensor_tensor(slot[:], rowf[:], row_far[:].unsqueeze(2).to_broadcast([P, T, 2]), ALU.add))
                    nc.vector.tensor_scalar(part_i[:, 0, :, :], slot[:], 7, None, ALU.arith_shift_right)
                    link(nc.vector.tensor_scalar(part_i[:, 1, :, :], slot[:], P - 1, None, ALU.bitwise_and))
                    link(nc.vector.tensor_copy(part[:], part_i[:]))
                    for i in range(IT):
                        ts_ = slice(i * TU, (i + 1) * TU)
                        if i >= 2:
                            dve.wait_ge(s_mm, i - 1)
                        nc.vector.tensor_tensor(in_place[:, i % 2], iota_w[:].unsqueeze(1).unsqueeze(1).to_broadcast([P, TU, 2, P]),
                                                part[:, 1, ts_, :].unsqueeze(3).to_broadcast([P, TU, 2, P]), ALU.is_equal)
                        link(nc.vector.tensor_tensor(in_block[:], iota_bk[:].unsqueeze(1).unsqueeze(1).to_broadcast([P, TU, 2, NB]),
                                                     part[:, 0, ts_, :].unsqueeze(3).to_broadcast([P, TU, 2, NB]), ALU.is_equal))
                        nc.vector.tensor_tensor(named[:, i % 2], in_block[:],
                                                row_1[:, ts_].unsqueeze(2).unsqueeze(3).to_broadcast([P, TU, 2, NB]), ALU.mult).then_inc(s_named, 1)
                        dve.wait_ge(s_named, i + 1)
                    link(nc.vector.tensor_scalar(blk_f[:], iota_bk[0:1, :], float(P), None, ALU.mult))
                    link(nc.vector.tensor_tensor(blk_ge[:], blk_f[:].unsqueeze(2).to_broadcast([1, NB, E]),
                                                 end[0:1, :].unsqueeze(1).to_broadcast([1, NB, E]), ALU.is_ge))
                    link(nc.vector.tensor_reduce(blk_f[:], blk_ge[:], AX_X, ALU.add))
                    nc.vector.tensor_scalar(block_expert[:, 0:NB], blk_f[:], float(E - 1), None, ALU.min)
                    dve.wait_ge(s_mm, IT)
                    nc.vector.tensor_copy(tok_f[:], ps_n[0:NB, 0:P]).then_inc(s_tok, 1)
                    dve.wait_ge(s_turned, 1)
                    nc.vector.tensor_scalar(token[:, 0:NB], ps_c[:, 0:NB], 1.0, 0.0, ALU.subtract, ALU.max)

        def experts(tag, E, F, NB, w1, b1_cols, w2, b2, func):
            FJ = F // P
            with ExitStack() as c:
                xs = sb(tag + "xs", [P, BU, D], F32, c)
                xT = sb(tag + "xT", [P, BU, K2, P], F32, c)
                W1 = sb(tag + "W1", [P, BU, K2, F], F32, c)
                W2 = sb(tag + "W2", [P, BU, FJ, D], F32, c)
                hidT = sb(tag + "hidT", [P, BU, FJ, P], F32, c)
                ys = sb(tag + "ys", [P, BU, D], F32, c)
                idx = sb(tag + "idx", [P, BU], I32, c)
                b2_rows = sb(tag + "b2_rows", [P, E, D], F32, c)
                ps_x = pb(tag + "ps_x", [P, 2, 512], c)
                ps_h = pb(tag + "ps_h", [P, 2, 512], c)
                ps_y = pb(tag + "ps_y", [P, 2, 512], c)
                rows_in = [held_sem(f"{tag}rows_in{s}") for s in range(BU)]
                w1_in = [sem(f"{tag}w1_in{s}") for s in range(BU)]
                w2_in = [sem(f"{tag}w2_in{s}") for s in range(BU)]
                stored = [sem(f"{tag}stored{s}") for s in range(BU)]
                b2_in, idx_ready, turned, xT_ready, mm1, hid_ready, mm2, y_ready = (sem(tag + n) for n in (
                    "b2_in", "idx_ready", "turned", "xT_ready", "first_done", "hidden_ready", "second_done", "y_ready"))
                block = c.enter_context(nc.Block())
                NI = NB // BU
                assert NI * BU == NB

                def in_loops(eng, body):
                    body(0, True)
                    with eng.Fori(1, NI) as i:
                        body(i, False)

                def expert_of(eng, b):
                    return eng.value_load(block_expert[0:1, ds(b, 1)], min_val=0, max_val=E - 1)

                @block.sync
                def _(sp):
                    def store(b, s):
                        sp.wait_ge(y_ready, b + 1)
                        sp.dma_start(rows_of(ys_dram, b), ys[:, s, :]).then_inc(stored[s], 16)

                    def body(i, first):
                        for s in range(BU):
                            b = i * BU + s
                            e = expert_of(sp, b)
                            if not first:
                                sp.wait_ge(mm1, b + 1 - BU)
                            sp.dma_start(W1[:, s, :, :], w1[ds(e, 1), :, :].rearrange("a (k p) f -> p (a k) f", p=P)).then_inc(w1_in[s], 16)
                            if not first:
                                sp.wait_ge(mm2, b + 1 - BU)
                            sp.dma_start(W2[:, s, :, :], w2[ds(e, 1), :, :].rearrange("a (j p) d -> p (a j) d", p=P)).then_inc(w2_in[s], 16)
                            if first and s == 0:
                                sp.dma_start(b2_rows[:], b2.rearrange("(a e) d -> a e d", a=1).to_broadcast([P, E, D])).then_inc(b2_in, 16)
                            if not first:
                                store(b - BU, s)

                    in_loops(sp, body)
                    for s in range(BU):
                        store(NB - BU + s, s)
                    for s in range(BU):
                        sp.wait_ge(stored[s], NI * 16)

                @block.gpsimd
                def _(pool):
                    def body(i, first):
                        for s in range(BU):
                            hold(pool, "pool", idx_ready, i * BU + s + 1)
                            pool.indirect_dma_start(out=xs[:, s, :], out_offset=None, in_=token_dram,
                                                    in_offset=bass.IndirectOffsetOnAxis(ap=idx[:, s:s + 1], axis=0)).then_inc(rows_in[s], 16)
                        if first:
                            nc.gpsimd.memset(sumT[:], 0.0)

                    in_loops(pool, body)

                @block.tensor
                def _(pe):
                    def turn(b, s, pre, reuse):
                        pe.wait_ge(rows_in[s], pre)
                        if reuse:
                            pe.wait_ge(xT_ready, b - 1)
                        turn2(ps_x[:, s % 2, 0:D], xs[:, s, :], turned)

                    def first_layer(b, s, pre, reuse):
                        pe.wait_ge(w1_in[s], pre)
                        pe.wait_ge(xT_ready, b + 1)
                        if reuse:
                            pe.wait_ge(hid_ready, b - 1)
                        for j in range(FJ):
                            for k in range(K2):
                                last = nc.tensor.matmul(ps_h[:, s % 2, j * P:(j + 1) * P], W1[:, s, k, j * P:(j + 1) * P],
                                                        xT[:, s, k, :], start=(k == 0), stop=(k == K2 - 1))
                        last.then_inc(mm1, 1)

                    def second_layer(b, s, pre, reuse):
                        pe.wait_ge(w2_in[s], pre)
                        pe.wait_ge(hid_ready, b + 1)
                        if reuse:
                            pe.wait_ge(y_ready, b - 1)
                        for j in range(FJ):
                            last = nc.tensor.matmul(ps_y[:, s % 2, 0:D], hidT[:, s, j, :], W2[:, s, j, :], start=(j == 0), stop=(j == FJ - 1))
                        last.then_inc(mm2, 1)

                    def body(i, first, last=False):
                        for s in range(BU):
                            b = i * BU + s
                            t = (s + 1) % BU
                            if not (last and s == BU - 1):
                                turn(b + 1, t, (i + 1 + (s == BU - 1)) * 16, not (first and s < 1))
                            first_layer(b, s, (i + 1) * 16, not (first and s < 2))
                            if not (first and s == 0):
                                second_layer(b - 1, (s - 1) % BU, (i + (s > 0)) * 16, not (first and s < 3))

                    turn(0, 0, 16, False)
                    body(0, True)
                    with pe.Fori(1, NI - 1) as i:
                        body(i, False)
                    body(NI - 1, False, True)
                    second_layer(NB - 1, BU - 1, NI * 16, True)

                @block.scalar
                def _(act):
                    def index(b, s, first):
                        if not first:
                            act.wait_ge(turned, b + 1 - BU)
                        nc.scalar.activation(idx[:, s:s + 1], token[:, ds(b, 1)], ACT.Copy).then_inc(idx_ready, 1)

                    def xT_copy(b, s, first):
                        act.wait_ge(turned, b + 1)
                        if not first:
                            act.wait_ge(mm1, b + 1 - BU)
                        nc.scalar.activation(xT[:, s, :, :].rearrange("p k n -> p (k n)"), ps_x[:, s % 2, 0:D], ACT.Copy).then_inc(xT_ready, 1)

                    def hidden(b, s, first):
                        e = expert_of(act, b)
                        act.wait_ge(mm1, b + 1)
                        if not first:
                            act.wait_ge(mm2, b + 1 - BU)
                        for j in range(FJ):
                            last = nc.scalar.activation(hidT[:, s, j, :], ps_h[:, s % 2, j * P:(j + 1) * P], func,
                                                        bias=b1_cols[:, ds(e * FJ + j, 1)])
                        last.then_inc(hid_ready, 1)

                    def body(i, first, last=False):
                        for s in range(BU):
                            b = i * BU + s
                            if not (last and s == BU - 1):
                                xT_copy(b + 1, (s + 1) % BU, first and s < BU - 1)
                            if not last:
                                index(b + BU, s, False)
                            hidden(b, s, first)

                    for s in range(BU):
                        index(s, s, True)
                    xT_copy(0, 0, True)
                    body(0, True)
                    with act.Fori(1, NI - 1) as i:
                        body(i, False)
                    body(NI - 1, False, True)

                @block.vector
                def _(dve):
                    def body(i, first):
                        for s in range(BU):
                            b = i * BU + s
                            e = expert_of(dve, b)
                            dve.wait_ge(mm2, b + 1)
                            if not first:
                                dve.wait_ge(stored[s], i * 16)
                            nc.vector.tensor_tensor(ys[:, s, :], ps_y[:, s % 2, 0:D], tile_of(b2_rows, e), ALU.add).then_inc(y_ready, 1)

                    dve.wait_ge(b2_in, 16)
                    in_loops(dve, body)

        class Mix:

            def __init__(self, tag, c, NB):
                self.Y = sb(tag + "Y", [P, TU, 2, D], F32, c)
                self.own = sb(tag + "own", [P, TU, D], F32, c)
                self.idx = sb(tag + "gidx", [P, TU, 2], I32, c)
                self.gathered = [held_sem(f"{tag}gathered{u}") for u in range(TU)]
                self.own_in = [sem(f"{tag}own_in{u}") for u in range(TU)]
                self.w = sb(tag + "w", [P, TU, 2], F32, c)
                self.cleared, self.idx_ready, self.w_ready, self.scaled, self.once, self.twice = (
                    sem(tag + n) for n in ("cleared", "idx_ready", "w_ready", "scaled", "mixed_once", "mixed_twice"))
                self.NB = NB

            def clear(self, pool):
                nc.gpsimd.memset(self.Y[:], 0.0).then_inc(self.cleared, 1)
                pool.wait_ge(self.cleared, 1)

            def indices(self, act, t, s):
                wait_tile(act, self.twice, t, TU)
                nc.scalar.activation(self.idx[:, s, :], tile_of(slot, t), ACT.Copy).then_inc(self.idx_ready, 1)
                nc.scalar.activation(self.w[:, s, :], tile_of(top_w, t), ACT.Copy).then_inc(self.w_ready, 1)

            def gather(self, pool, t, s):
                hold_tile(pool, "pool", self.idx_ready, t)
                for k in range(2):
                    pool.indirect_dma_start(out=self.Y[:, s, k, :], out_offset=None, in_=ys_dram,
                                            in_offset=bass.IndirectOffsetOnAxis(ap=self.idx[:, s, k:k + 1], axis=0),
                                            bounds_check=self.NB * P - 1, oob_is_err=False).then_inc(self.gathered[s], 16)

            def load_own(self, sp, t, s):
                wait_tile(sp, self.once, t, TU)
                sp.dma_start(self.own[:, s, :], rows_of(token_dram, t)).then_inc(self.own_in[s], 16)

            def scale(self, act, t, s, r):
                act.wait_ge(self.gathered[s], (r + 1) * 32)
                wait_tile(act, self.w_ready, t)
                for k in range(2):
                    last = nc.scalar.activation(self.Y[:, s, k, :], self.Y[:, s, k, :], ACT.Copy, scale=self.w[:, s, k:k + 1])
                last.then_inc(self.scaled, 1)

            def add(self, eng, on, t, s, r, out):
                wait_tile(eng, self.scaled, t)
                eng.wait_ge(self.own_in[s], (r + 1) * 16)
                on.tensor_tensor(out, self.Y[:, s, 0, :], self.own[:, s, :], ALU.add).then_inc(self.once, 1)
                wait_tile(eng, self.once, t)
                on.tensor_tensor(out, self.Y[:, s, 1, :], out, ALU.add).then_inc(self.twice, 1)

        def sparse_products():
            STRUCK = -3.4028235e38
            with ExitStack() as c:
                H = sb("m0H", [P, TU, D], F32, c)
                XB = sb("m0XB", [P, TU, D], F32, c)
                N3 = sb("m0N3", [P, TU, D], F32, c)
                nT = sb("m0nT", [P, TU, K2, P], F32, c)
                HD = sb("m0HD", [P, TU, 2 * D], F32, c)
                WK = sb("m0WK", [P, TU, D], F32, c)
                v8 = sb("m0v8", [P, TU, 8], F32, c)
                mr = sb("m0mr", [P, TU], F32, c)
                ps_n = pb("m0ps_n", [P, 512], c)
                ps_d = pb("m0ps_d", [P, 512], c)
                y_norm, x_norm = Norm("my", c, eps5[:]), Norm("mx", c, eps5[:])
                mixer = Mix("m0", c, NB0)
                S = {n: sem("M0" + n) for n in ("xb_ready", "centred", "x_ready", "mean_ready", "n_ready", "turned", "nT_ready", "dense",
                                                "dense_in", "x_added", "max8", "replaced", "sparse")}
                hs_stores = Stores("M0")
                block = c.enter_context(nc.Block())

                @block.gpsimd
                def _(pool):
                    mixer.clear(pool)

                    def step(at):
                        if x := at(0):
                            mixer.gather(pool, *x)
                        if x := at(1, True):
                            t, s, r = x
                            wait_tile(pool, S["x_ready"], t, TU)
                            mixer.add(pool, nc.gpsimd, t, s, r, H[:, s, :])
                        if x := at(5):
                            t, s = x
                            hold_tile(pool, "pool", S["dense_in"], t)
                            nc.gpsimd.tensor_tensor(tile_of(X, t), tile_of(X, t), HD[:, s, 0:D], ALU.add).then_inc(S["x_added"], 1)
                        if x := at(0):
                            t, s = x
                            wait_tile(pool, S["x_ready"], t, TU)
                            nc.gpsimd.tensor_tensor(XB[:, s, :], tile_of(X, t), FFN_B, ALU.add).then_inc(S["xb_ready"], 1)

                    tile_steps(pool, step, 5, peeled=2)

                @block.sync
                def _(sp):
                    def step(at):
                        if x := at(0):
                            mixer.load_own(sp, *x)
                        if x := at(5):
                            t, s = x
                            wait_tile(sp, S["sparse"], t)
                            hs_stores.store(sp, rows_of(hs_dram, t), WK[:, s, :], s)

                    hs_stores.begin(sp)
                    tile_steps(sp, step, 5, peeled=2)
                    hs_stores.wait_all(sp)

                @block.scalar
                def _(act):
                    def step(at):
                        if x := at(0):
                            mixer.indices(act, *x)
                        if x := at(1, True):
                            mixer.scale(act, *x)
                        if x := at(3):
                            x_norm.deviation(act, *x)
                        if x := at(4):
                            t, s = x
                            wait_tile(act, S["turned"], t)
                            nc.scalar.activation(nT[:, s, :, :].rearrange("p k n -> p (k n)"), ps_n[:, 0:D], ACT.Copy).then_inc(S["nT_ready"], 1)
                        if x := at(3):
                            t, s = x
                            wait_tile(act, S["mean_ready"], t)
                            nc.scalar.activation(N3[:, s, :], tile_of(X, t), ACT.Identity, bias=mr[:, s:s + 1],
                                                 scale=x_norm.inverse(s)).then_inc(S["n_ready"], 1)
                        if x := at(2):
                            y_norm.deviation(act, *x)
                        if x := at(4):
                            t, s = x
                            wait_tile(act, S["dense"], t)
                            wait_tile(act, S["sparse"], t, TU)
                            nc.scalar.activation(HD[:, s, :], ps_d[:], ACT.Copy).then_inc(S["dense_in"], 1)

                    tile_steps(act, step, 5, peeled=2)

                @block.tensor
                def _(pe):
                    def step(at):
                        if x := at(4):
                            t, s = x
                            wait_tile(pe, S["n_ready"], t)
                            wait_tile(pe, S["nT_ready"], t, 1)
                            turn2(ps_n, N3[:, s, :], S["turned"])
                            wait_tile(pe, S["nT_ready"], t)
                            wait_tile(pe, S["dense_in"], t, 1)
                            for k in range(K2):
                                last = nc.tensor.matmul(ps_d[:], nT[:, s, k, :], w_dense[:, k, :], start=(k == 0), stop=(k == K2 - 1))
                            last.then_inc(S["dense"], 1)

                    tile_steps(pe, step, 5, peeled=2)

                @block.vector
                def _(dve):
                    def largest(x, r):
                        if x:
                            t, s, slot_round = x
                            if r == 0:
                                hold_tile(dve, "dve", S["dense_in"], t)
                                hs_stores.hold_free("dve", dve, s, slot_round)
                            else:
                                hold(dve, "dve", S["replaced"], t * 4 + r)
                            nc.vector.max(v8[:, s, :], HD[:, s, D:2 * D] if r == 0 else WK[:, s, :]).then_inc(S["max8"], 1)

                    def strike(x, r):
                        if x:
                            t, s, _ = x
                            hold(dve, "dve", S["max8"], t * 4 + r + 1)
                            nc.vector.match_replace(WK[:, s, :], v8[:, s, :], HD[:, s, D:2 * D] if r == 0 else WK[:, s, :],
                                                    STRUCK).then_inc(S["replaced"], 1)

                    def step(at):
                        x2, x3, x5 = at(2), at(3), at(5, True)
                        largest(x5, 0)
                        if x3:
                            x_norm.invert(dve, *x3)
                        if x2:
                            t, s = x2
                            y_norm.take_stats(dve, t, s, H[:, s, :], mixer.twice)
                        strike(x5, 0)
                        if x3:
                            t3, s3 = x3
                            nc.vector.tensor_scalar(mr[:, s3:s3 + 1], x_norm.mean(s3), x_norm.inverse(s3), -1.0,
                                                    ALU.mult, ALU.mult).then_inc(S["mean_ready"], 1)
                        if x2:
                            y_norm.join_stats(dve, t, s)
                        largest(x5, 1)
                        if x2:
                            wait_tile(dve, y_norm.joined, t)
                            nc.vector.scalar_tensor_tensor(H[:, s, :], H[:, s, :], y_norm.mean(s), FFN_S, ALU.subtract, ALU.mult).then_inc(S["centred"], 1)
                        strike(x5, 1)
                        if x2:
                            y_norm.invert(dve, t, s)
                        largest(x5, 2)
                        if x2:
                            wait_tile(dve, S["centred"], t)
                            wait_tile(dve, S["xb_ready"], t)
                            nc.vector.scalar_tensor_tensor(tile_of(X, t), H[:, s, :], y_norm.inverse(s), XB[:, s, :],
                                                           ALU.mult, ALU.add).then_inc(S["x_ready"], 1)
                        strike(x5, 2)
                        if x2:
                            x_norm.take_stats(dve, t, s, tile_of(X, t), S["x_ready"])
                        largest(x5, 3)
                        if x2:
                            x_norm.join_stats(dve, t, s)
                        strike(x5, 3)
                        if x5:
                            t5, s5, _ = x5
                            dve.wait_ge(S["replaced"], t5 * 4 + 4)
                            nc.vector.scalar_tensor_tensor(WK[:, s5, :], WK[:, s5, :], STRUCK, HD[:, s5, D:2 * D],
                                                           ALU.is_equal, ALU.mult).then_inc(S["sparse"], 1)

                    tile_steps(dve, step, 5, peeled=2)

        class NeighbourMeans:
            def __init__(self, tag, c):
                self.lhs = sb(tag + "lhs", [P, TU, K2, P], F32, c)
                self.N4 = sb(tag + "N4", [P, TU, D], F32, c)
                self.nT = sb(tag + "nT", [P, K2, P], F32, c)
                self.ps_s, self.ps_n, self.ps_g = (pb(tag + n, [P, 512], c) for n in ("ps_s", "ps_n", "ps_g"))
                self.norm = Norm(tag + "n", c, eps5[:])
                self.S = {n: sem(tag + n) for n in ("lhs_ready", "turned", "x_ready", "n_ready", "n_turned", "nT_ready",
                                                    "logits", "logits_in")}
                self.n_stores = Stores(tag)

            def act(self, act, at, group, sums_in):
                S = self.S
                if x := at(3):
                    self.norm.deviation(act, *x)
                group(0)
                if x := at(4):
                    t, s = x
                    wait_tile(act, S["n_turned"], t)
                    nc.scalar.activation(self.nT[:].rearrange("p k n -> p (k n)"), self.ps_n[:, 0:D], ACT.Copy).then_inc(S["nT_ready"], 1)
                for q in range(1, GPS):
                    group(q)
                if x := at(0):
                    t, s = x
                    sums_in()
                    wait_tile(act, S["turned"], t, TU)
                    nc.scalar.activation(self.lhs[:, s, :, :], sumT[:, 0:K2, ds(node_tile(t) * P, P)], ACT.Copy).then_inc(S["lhs_ready"], 1)

            def pe(self, pe, at, group):
                S = self.S
                if x := at(1):
                    t, s = x
                    wait_tile(pe, S["lhs_ready"], t)
                    wait_tile(pe, S["x_ready"], t, 1)
                    turn2(self.ps_s, self.lhs[:, s, :, :].rearrange("p k n -> p (k n)"), S["turned"])
                group(0)
                if x := at(4):
                    t, s = x
                    wait_tile(pe, S["n_ready"], t)
                    wait_tile(pe, S["nT_ready"], t, 1)
                    turn2(self.ps_n, self.N4[:, s, :], S["n_turned"])
                group(1)
                if x := at(4):
                    t, s = x
                    wait_tile(pe, S["nT_ready"], t)
                    wait_tile(pe, S["logits_in"], t, 1)
                    for k in range(K2):
                        last = nc.tensor.matmul(self.ps_g[:, 0:E1], self.nT[:, k, :], gate_w1[:, k, :], start=(k == 0), stop=(k == K2 - 1))
                    last.then_inc(S["logits"], 1)
                for q in range(2, GPS):
                    group(q)

            def dve(self, dve, at, group):
                S, norm = self.S, self.norm
                x1, x3, x4 = at(1), at(3, True), at(4)
                if x1:
                    t, s = x1
                    wait_tile(dve, S["turned"], t)
                    nc.vector.scalar_tensor_tensor(tile_of(X, node_tile(t)), self.ps_s[:, 0:D], deg_inv[:, ds(node_tile(t), 1)], tile_of(X, node_tile(t)),
                                                   ALU.mult, ALU.add).then_inc(S["x_ready"], 1)
                if x3:
                    t3, s3, r = x3
                    norm.invert(dve, t3, s3)
                group(0)
                if x3:
                    self.n_stores.wait_free(dve, s3, r)
                    nc.vector.tensor_scalar(self.N4[:, s3, :], tile_of(X, node_tile(t3)), norm.mean(s3), norm.inverse(s3),
                                            ALU.subtract, ALU.mult).then_inc(S["n_ready"], 1)
                if x1:
                    norm.take_stats(dve, t, s, tile_of(X, node_tile(t)), S["x_ready"])
                group(1)
                if x1:
                    norm.join_stats(dve, t, s)
                group(2)
                if x4:
                    t, s = x4
                    wait_tile(dve, S["logits"], t)
                    nc.vector.tensor_copy(tile_of(logit1, node_tile(t)), self.ps_g[:, 0:E1]).then_inc(S["logits_in"], 1)
                group(3)

            def store_rows(self, sp, at):
                if x := at(3):
                    t, s = x
                    wait_tile(sp, self.S["n_ready"], t)
                    self.n_stores.store(sp, rows_of(token_dram, node_tile(t)), self.N4[:, s, :], s)

            def finish(self, dve):
                pass

        def last_sums():
            with ExitStack() as c:
                H = sb("o1H", [P, TU, D], F32, c)
                mixer = Mix("o1", c, NB1)
                s_res, s_out = sem("result_ready"), [sem(f"out_stored{u}") for u in range(TU)]
                block = c.enter_context(nc.Block())

                @block.gpsimd
                def _(pool):
                    mixer.clear(pool)

                    def step(at):
                        if x := at(0):
                            mixer.gather(pool, *x)

                    tile_steps(pool, step, 0)

                @block.scalar
                def _(act):
                    def step(at):
                        if x := at(0):
                            mixer.indices(act, *x)
                        if x := at(2, True):
                            mixer.scale(act, *x)

                    tile_steps(act, step, 2)

                @block.vector
                def _(dve):
                    def step(at):
                        if x := at(0, True):
                            t, s, r = x
                            if not (isinstance(r, int) and r == 0):
                                dve.wait_ge(s_out[s], r * 16)
                            mixer.add(dve, nc.vector, t, s, r, H[:, s, :])
                            wait_tile(dve, mixer.twice, t)
                            nc.vector.tensor_tensor(H[:, s, :], H[:, s, :], tile_of(X, t), ALU.add).then_inc(s_res, 1)

                    tile_steps(dve, step, 0)

                @block.sync
                def _(sp):
                    def store(t, s):
                        wait_tile(sp, s_res, t)
                        if isinstance(t, int) and t == T - 1:
                            sp.dma_start(out[t * P:N, :], H[0:LAST, s, :]).then_inc(s_out[s], 16)
                        else:
                            sp.dma_start(rows_of(out, t), H[:, s, :]).then_inc(s_out[s], 16)

                    for u in range(TU):
                        mixer.load_own(sp, u, u)
                    with sp.Fori(1, IT) as i:
                        for u in range(TU):
                            store(i * TU + u - TU, u)
                            mixer.load_own(sp, i * TU + u, u)
                    for u in range(TU):
                        store(T - TU + u, u)
                    for u in range(TU):
                        sp.wait_ge(s_out[u], T // TU * 16)

        end_step()
        sums_and_nodes("O0", n_dram, True, NodeMlp)
        end_step()
        segment_sums("L0_", n_dram, True)
        end_step()
        nodes_alone("A0", NodeMlp)
        end_step()
        route("r0", E0, NB0, logit0, False)
        end_step()
        experts("e0", E0, F0, NB0, a["L0_ffn_w1"], b1_cols0, a["L0_ffn_w2"], a["L0_ffn_b2"], ACT.Relu)
        end_step()
        sparse_products()
        end_step()
        sums_and_nodes("O1", hs_dram, False, NeighbourMeans)
        end_step()
        segment_sums("L1_", hs_dram, False)
        end_step()
        nodes_alone("A1", NeighbourMeans)
        end_step()
        route("r1", E1, NB1, logit1, True)
        end_step()
        experts("e1", E1, F1, NB1, a["L1_ffn_w1"], b1_cols1, a["L1_ffn_w2"], a["L1_ffn_b2"], ACT.Gelu)
        end_step()
        last_sums()


def kernel(**inputs):
    import numpy as _np
    import concourse.bacc as _bacc
    from concourse import mybir as _mybir
    from concourse.bass_utils import run_bass_kernel_spmd as _run

    nc = _bacc.Bacc("TRN2", target_bir_lowering=False, num_devices=1)
    arrays, args = {}, {}
    for name in inputs:
        v = _np.ascontiguousarray(inputs[name])
        arrays[f"in_{name}"] = v
        args[name] = nc.dram_tensor(f"in_{name}", v.shape, _mybir.dt.from_np(v.dtype), kind="ExternalInput").ap()
    shape = inputs["x"].shape
    out = nc.dram_tensor("out", shape, _mybir.dt.from_np(_np.dtype("float32")), kind="ExternalOutput").ap()
    build(nc, args, out)
    r = _run(nc, [arrays], core_ids=[0])
    return r.results[0]["out"]
```
